# Optimizing a Trainium2 kernel written in Bass

```python
import numpy as np
import jax
import jax.numpy as jnp

def _softmax(x, axis=-1):
    return jax.nn.softmax(x, axis=axis)

def _gelu(x):
    return jax.nn.gelu(x, approximate=True)

def _silu(x):
    return jax.nn.silu(x)

def _sigmoid(x):
    return jax.nn.sigmoid(x)

def _layernorm(x, axis=-1, eps=1e-05):
    m = jnp.mean(x, axis=axis, keepdims=True)
    v = jnp.var(x, axis=axis, keepdims=True)
    return (x - m) / jnp.sqrt(v + eps)

def _scatter_add(tgt, idx, src, axis=0):
    return tgt.at[idx].add(src)

def _segment_sum(src, seg, n):
    return jax.ops.segment_sum(src, seg, n)
kernel_name = 'mk_flamingo_gated_d1_seqx_r4_fc640f'

def setup_inputs(seed: int=0):
    np.random.seed(seed)
    _w = jnp.asarray

    def _rec_inputs():
        import jax
        import jax.numpy as jnp
        _rk = jax.random.key(seed)
        x = -0.0002928 + 1 * jax.random.normal(jax.random.fold_in(_rk, 1), (16, 128, 256), jnp.float32)
        _lenS = 128 - jax.random.randint(jax.random.fold_in(_rk, 7), (16,), 0, max(1, 128 // 4) + 1, jnp.int32)
        _lenS2 = 128 - jax.random.randint(jax.random.fold_in(_rk, 8), (16,), 0, max(1, 128 // 4) + 1, jnp.int32)
        _ctx_1024P = jax.random.normal(jax.random.fold_in(_rk, 11), (16, 16, 256), jnp.float32)
        _ctx_1024c = jax.random.dirichlet(jax.random.fold_in(_rk, 511), 0.3 * jnp.ones((16,), jnp.float32), (16, 128))
        _ctx_1024t = jnp.einsum('bsk,bkd->bsd', _ctx_1024c, _ctx_1024P)
        _ctx_1024t = _ctx_1024t * jax.lax.rsqrt(jnp.mean(jnp.square(_ctx_1024t)) + 1e-12) * 0.953939
        ctx_1024 = 4.13588e-05 + 0.999923 * (_ctx_1024t + 0.3 * jax.random.normal(jax.random.fold_in(_rk, 611), (16, 128, 256), jnp.float32))
        _validS = jnp.arange(128)[None, :] < _lenS[:, None]
        _validS2 = jnp.arange(128)[None, :] < _lenS2[:, None]
        _causal = jnp.tril(jnp.ones((128, 128), dtype=bool))
        mask_BxSxS2_bf0 = jnp.logical_not(jnp.ones((16, 128, 128), dtype=bool))
        _g = jax.random.normal(jax.random.fold_in(_rk, 9001), (2, 1), jnp.float32)
        _g = jnp.sign(_g) * jnp.maximum(jnp.abs(_g), 1.0) + (_g == 0) * 1.0
        g_xattn = _g[0]
        g_ffn = _g[1]
        return (x, ctx_1024, mask_BxSxS2_bf0, g_xattn, g_ffn)
    x, ctx_1024, mask_BxSxS2_bf0, g_xattn, g_ffn = _rec_inputs()

    def _L0_xattn_setup():
        import jax, jax.numpy as jnp
        import numpy as np
        HIDDEN = 256
        HEADS = 16
        D_K = HIDDEN // HEADS
        B, LQ, LKV = (4, 256, 512)
        NEG_INF = -1e+18
        key = jax.random.key(seed)
        ks = jax.random.split(key, 12)
        s = 1.0 / np.sqrt(HIDDEN)
        return {'tgt': jax.random.normal(ks[0], (B, LQ, HIDDEN), jnp.float32), 'memory': jax.random.normal(ks[1], (B, LKV, HIDDEN), jnp.float32), 'mask': jnp.zeros((B, LQ, LKV), dtype=bool), 'Wq': jax.random.normal(ks[2], (HIDDEN, HIDDEN), jnp.float32) * s, 'bq': jnp.zeros((HIDDEN,), jnp.float32), 'Wk': jax.random.normal(ks[3], (HIDDEN, HIDDEN), jnp.float32) * s, 'bk': jnp.zeros((HIDDEN,), jnp.float32), 'Wv': jax.random.normal(ks[4], (HIDDEN, HIDDEN), jnp.float32) * s, 'bv': jnp.zeros((HIDDEN,), jnp.float32), 'Wo': jax.random.normal(ks[5], (HIDDEN, HIDDEN), jnp.float32) * s, 'bo': jnp.zeros((HIDDEN,), jnp.float32)}
    _L0_xattn_all = _L0_xattn_setup()
    _L0_xattn_in = {k: v for k, v in _L0_xattn_all.items() if k in ('Wq', 'bq', 'Wk', 'bk', 'Wv', 'bv', 'Wo', 'bo')}
    del _L0_xattn_all

    def _L0_ffn_setup():
        import jax, jax.numpy as jnp
        import numpy as np
        DIM = 256
        DEPTH = 6
        HEADS = 16
        DIM_HEAD = 64
        WINDOW = 64
        INNER = HEADS * DIM_HEAD
        DIM_INNER = int(DIM * 4 * 2 / 3)
        QK_SCALE = 8.0

        def shift_tokens(t):
            a, s = jnp.split(t, 2, -1)
            s = jnp.pad(s, ((0, 0), (1, 0), (0, 0)))[:, :-1]
            return jnp.concatenate([a, s], -1)

        def l2norm(t):
            return t / jnp.maximum(jnp.linalg.norm(t, axis=-1, keepdims=True), 1e-12)

        def rotate_half(x):
            x1, x2 = jnp.split(x, 2, -1)
            return jnp.concatenate([-x2, x1], -1)

        def rotary_tables(n):
            half = jnp.arange(0, DIM_HEAD, 2, dtype=jnp.float32)
            inv_freq = 1.0 / 10000.0 ** (half / DIM_HEAD)
            t = jnp.arange(n, dtype=jnp.float32)
            freqs = t[:, None] * inv_freq[None, :]
            freqs = jnp.concatenate([freqs, freqs], -1)
            base_scale = (half + 0.4 * DIM_HEAD) / (1.4 * DIM_HEAD)
            power = (t - n // 2) / (WINDOW // 2)
            scale = base_scale[None, :] ** power[:, None]
            scale = jnp.concatenate([scale, scale], -1)
            return (freqs, scale)

        def local_attention(q, k, v):
            b, h, n, d = q.shape
            w = WINDOW
            nw = n // w
            bq = q.reshape(b, h, nw, w, d)
            bk = k.reshape(b, h, nw, w, d)
            bv = v.reshape(b, h, nw, w, d)

            def look(t):
                p = jnp.pad(t, ((0, 0), (0, 0), (1, 0), (0, 0), (0, 0)))
                return jnp.concatenate([p[:, :, :nw], p[:, :, 1:]], axis=3)
            bk2, bv2 = (look(bk), look(bv))
            seq = jnp.arange(n).reshape(nw, w)
            seq_p = jnp.pad(seq, ((1, 0), (0, 0)), constant_values=-1)
            jt = jnp.concatenate([seq_p[:nw], seq_p[1:]], axis=1)
            it = seq[:, :, None]
            jb = jt[:, None, :]
            mask = (it < jb) | (it > jb + w) | (jb == -1)
            sim = jnp.einsum('bhwie,bhwje->bhwij', bq, bk2) * QK_SCALE
            sim = jnp.where(mask, -jnp.finfo(sim.dtype).max, sim)
            attn = jax.nn.softmax(sim, -1)
            out = jnp.einsum('bhwij,bhwje->bhwie', attn, bv2)
            return out.reshape(b, h, n, d)

        def attn_layer(x, Wqkv, qs, ksc, Wo):
            b, n, _ = x.shape
            qkv = x @ Wqkv
            q, k, v = jnp.split(qkv, 3, -1)
            sh = lambda t: t.reshape(b, n, HEADS, DIM_HEAD).transpose(0, 2, 1, 3)
            q, k, v = (sh(q), sh(k), sh(v))
            q = l2norm(q) * qs
            k = l2norm(k) * ksc
            freqs, scale = rotary_tables(n)
            cos, sin = (jnp.cos(freqs), jnp.sin(freqs))
            q = q * cos * scale + rotate_half(q) * sin * scale
            inv = 1.0 / scale
            k = k * cos * inv + rotate_half(k) * sin * inv
            out = local_attention(q, k, v)
            out = out.transpose(0, 2, 1, 3).reshape(b, n, INNER)
            return out @ Wo

        def ffn_layer(x, g, bln, W1, b1, W2, b2):
            mu = x.mean(-1, keepdims=True)
            var = ((x - mu) ** 2).mean(-1, keepdims=True)
            xn = (x - mu) / jnp.sqrt(var + 1e-05) * g + bln
            hg = xn @ W1 + b1
            a, gate = jnp.split(hg, 2, -1)
            return a * jax.nn.gelu(gate, approximate=False) @ W2 + b2
        key = jax.random.key(seed)
        ks = jax.random.split(key, 8)
        B, N = (2, 512)
        init = lambda k, shape: jax.random.normal(k, shape, jnp.float32) * 0.02
        return {'x': jax.random.normal(ks[0], (B, N, DIM), jnp.float32), 'Wqkv': init(ks[1], (DEPTH, DIM, 3 * INNER)), 'q_scale': jnp.ones((DEPTH, DIM_HEAD), jnp.float32), 'k_scale': jnp.ones((DEPTH, DIM_HEAD), jnp.float32), 'Wo': init(ks[2], (DEPTH, INNER, DIM)), 'ln_g': jnp.ones((DEPTH, DIM), jnp.float32), 'ln_b': jnp.zeros((DEPTH, DIM), jnp.float32), 'W1': init(ks[3], (DEPTH, DIM, 2 * DIM_INNER)), 'b1': jnp.zeros((DEPTH, 2 * DIM_INNER), jnp.float32), 'W2': init(ks[4], (DEPTH, DIM_INNER, DIM)), 'b2': jnp.zeros((DEPTH, DIM), jnp.float32)}
    _L0_ffn_all = _L0_ffn_setup()
    _L0_ffn_in = {k: v for k, v in _L0_ffn_all.items() if k in ('Wqkv', 'q_scale', 'k_scale', 'Wo', 'ln_g', 'ln_b', 'W1', 'b1', 'W2', 'b2')}
    del _L0_ffn_all
    return {'x': x, 'ctx_1024': ctx_1024, 'mask_BxSxS2_bf0': mask_BxSxS2_bf0, 'g_xattn': g_xattn, 'g_ffn': g_ffn, 'L0_xattn_Wq': _L0_xattn_in['Wq'], 'L0_xattn_bq': _L0_xattn_in['bq'], 'L0_xattn_Wk': _L0_xattn_in['Wk'], 'L0_xattn_bk': _L0_xattn_in['bk'], 'L0_xattn_Wv': _L0_xattn_in['Wv'], 'L0_xattn_bv': _L0_xattn_in['bv'], 'L0_xattn_Wo': _L0_xattn_in['Wo'], 'L0_xattn_bo': _L0_xattn_in['bo'], 'L0_ffn_Wqkv': _L0_ffn_in['Wqkv'], 'L0_ffn_q_scale': _L0_ffn_in['q_scale'], 'L0_ffn_k_scale': _L0_ffn_in['k_scale'], 'L0_ffn_Wo': _L0_ffn_in['Wo'], 'L0_ffn_ln_g': _L0_ffn_in['ln_g'], 'L0_ffn_ln_b': _L0_ffn_in['ln_b'], 'L0_ffn_W1': _L0_ffn_in['W1'], 'L0_ffn_b1': _L0_ffn_in['b1'], 'L0_ffn_W2': _L0_ffn_in['W2'], 'L0_ffn_b2': _L0_ffn_in['b2']}

def reference(x, ctx_1024, mask_BxSxS2_bf0, g_xattn, g_ffn, L0_xattn_Wq, L0_xattn_bq, L0_xattn_Wk, L0_xattn_bk, L0_xattn_Wv, L0_xattn_bv, L0_xattn_Wo, L0_xattn_bo, L0_ffn_Wqkv, L0_ffn_q_scale, L0_ffn_k_scale, L0_ffn_Wo, L0_ffn_ln_g, L0_ffn_ln_b, L0_ffn_W1, L0_ffn_b1, L0_ffn_W2, L0_ffn_b2):
    import jax
    import jax.numpy as jnp

    def _L0_xattn_ref(tgt, memory, mask, Wq, bq, Wk, bk, Wv, bv, Wo, bo):
        import jax, jax.numpy as jnp
        import numpy as np
        HIDDEN = 256
        HEADS = 16
        D_K = HIDDEN // HEADS
        B, LQ, LKV = (4, 256, 512)
        NEG_INF = -1e+18
        b = tgt.shape[0]

        def heads(x):
            return x.reshape(b, -1, HEADS, D_K).transpose(0, 2, 1, 3)
        q = heads(tgt @ Wq + bq) / jnp.sqrt(jnp.asarray(D_K, tgt.dtype))
        k = heads(memory @ Wk + bk)
        v = heads(memory @ Wv + bv)
        scores = jnp.einsum('bhqd,bhkd->bhqk', q, k)
        scores = jnp.where(mask[:, None, :, :], NEG_INF, scores)
        attn = jax.nn.softmax(scores, axis=-1)
        ctx = jnp.einsum('bhqk,bhkd->bhqd', attn, v)
        ctx = ctx.transpose(0, 2, 1, 3).reshape(b, -1, HIDDEN)
        return ctx @ Wo + bo

    def _L0_ffn_ref(x, Wqkv, q_scale, k_scale, Wo, ln_g, ln_b, W1, b1, W2, b2):
        import jax, jax.numpy as jnp
        import numpy as np
        DIM = 256
        DEPTH = 6
        HEADS = 16
        DIM_HEAD = 64
        WINDOW = 64
        INNER = HEADS * DIM_HEAD
        DIM_INNER = int(DIM * 4 * 2 / 3)
        QK_SCALE = 8.0

        def shift_tokens(t):
            a, s = jnp.split(t, 2, -1)
            s = jnp.pad(s, ((0, 0), (1, 0), (0, 0)))[:, :-1]
            return jnp.concatenate([a, s], -1)

        def l2norm(t):
            return t / jnp.maximum(jnp.linalg.norm(t, axis=-1, keepdims=True), 1e-12)

        def rotate_half(x):
            x1, x2 = jnp.split(x, 2, -1)
            return jnp.concatenate([-x2, x1], -1)

        def rotary_tables(n):
            half = jnp.arange(0, DIM_HEAD, 2, dtype=jnp.float32)
            inv_freq = 1.0 / 10000.0 ** (half / DIM_HEAD)
            t = jnp.arange(n, dtype=jnp.float32)
            freqs = t[:, None] * inv_freq[None, :]
            freqs = jnp.concatenate([freqs, freqs], -1)
            base_scale = (half + 0.4 * DIM_HEAD) / (1.4 * DIM_HEAD)
            power = (t - n // 2) / (WINDOW // 2)
            scale = base_scale[None, :] ** power[:, None]
            scale = jnp.concatenate([scale, scale], -1)
            return (freqs, scale)

        def local_attention(q, k, v):
            b, h, n, d = q.shape
            w = WINDOW
            nw = n // w
            bq = q.reshape(b, h, nw, w, d)
            bk = k.reshape(b, h, nw, w, d)
            bv = v.reshape(b, h, nw, w, d)

            def look(t):
                p = jnp.pad(t, ((0, 0), (0, 0), (1, 0), (0, 0), (0, 0)))
                return jnp.concatenate([p[:, :, :nw], p[:, :, 1:]], axis=3)
            bk2, bv2 = (look(bk), look(bv))
            seq = jnp.arange(n).reshape(nw, w)
            seq_p = jnp.pad(seq, ((1, 0), (0, 0)), constant_values=-1)
            jt = jnp.concatenate([seq_p[:nw], seq_p[1:]], axis=1)
            it = seq[:, :, None]
            jb = jt[:, None, :]
            mask = (it < jb) | (it > jb + w) | (jb == -1)
            sim = jnp.einsum('bhwie,bhwje->bhwij', bq, bk2) * QK_SCALE
            sim = jnp.where(mask, -jnp.finfo(sim.dtype).max, sim)
            attn = jax.nn.softmax(sim, -1)
            out = jnp.einsum('bhwij,bhwje->bhwie', attn, bv2)
            return out.reshape(b, h, n, d)

        def attn_layer(x, Wqkv, qs, ksc, Wo):
            b, n, _ = x.shape
            qkv = x @ Wqkv
            q, k, v = jnp.split(qkv, 3, -1)
            sh = lambda t: t.reshape(b, n, HEADS, DIM_HEAD).transpose(0, 2, 1, 3)
            q, k, v = (sh(q), sh(k), sh(v))
            q = l2norm(q) * qs
            k = l2norm(k) * ksc
            freqs, scale = rotary_tables(n)
            cos, sin = (jnp.cos(freqs), jnp.sin(freqs))
            q = q * cos * scale + rotate_half(q) * sin * scale
            inv = 1.0 / scale
            k = k * cos * inv + rotate_half(k) * sin * inv
            out = local_attention(q, k, v)
            out = out.transpose(0, 2, 1, 3).reshape(b, n, INNER)
            return out @ Wo

        def ffn_layer(x, g, bln, W1, b1, W2, b2):
            mu = x.mean(-1, keepdims=True)
            var = ((x - mu) ** 2).mean(-1, keepdims=True)
            xn = (x - mu) / jnp.sqrt(var + 1e-05) * g + bln
            hg = xn @ W1 + b1
            a, gate = jnp.split(hg, 2, -1)
            return a * jax.nn.gelu(gate, approximate=False) @ W2 + b2
        for i in range(DEPTH):
            x = attn_layer(shift_tokens(x), Wqkv[i], q_scale[i], k_scale[i], Wo[i]) + x
            x = ffn_layer(shift_tokens(x), ln_g[i], ln_b[i], W1[i], b1[i], W2[i], b2[i]) + x
        return x
    x = x + jnp.tanh(g_xattn[0]) * _L0_xattn_ref(_layernorm(x, axis=-1), ctx_1024, mask_BxSxS2_bf0, L0_xattn_Wq, L0_xattn_bq, L0_xattn_Wk, L0_xattn_bk, L0_xattn_Wv, L0_xattn_bv, L0_xattn_Wo, L0_xattn_bo)
    x = x + jnp.tanh(g_ffn[0]) * _L0_ffn_ref(_layernorm(x, axis=-1), L0_ffn_Wqkv, L0_ffn_q_scale, L0_ffn_k_scale, L0_ffn_Wo, L0_ffn_ln_g, L0_ffn_ln_b, L0_ffn_W1, L0_ffn_b1, L0_ffn_W2, L0_ffn_b2)
    return x

_drawn_inputs = setup_inputs


def setup_inputs(seed=0):
    import zlib

    import numpy as np

    out = dict(_drawn_inputs(seed))
    spreads = {'L0_xattn_bq': (0.0, 0.372),
     'L0_xattn_bk': (0.0, 0.8),
     'L0_xattn_bv': (0.0, 0.1),
     'L0_xattn_bo': (0.0, 0.1),
     'L0_ffn_q_scale': (1.0, 0.2),
     'L0_ffn_k_scale': (1.0, 0.2),
     'L0_ffn_ln_g': (1.0, 0.2),
     'L0_ffn_ln_b': (0.0, 0.269),
     'L0_ffn_b1': (0.0, 0.1),
     'L0_ffn_b2': (0.0, 0.1)}
    factors = {}
    for name, (base, spread) in spreads.items():
        noise = np.random.default_rng([zlib.crc32(name.encode()), seed]).standard_normal(out[name].shape)
        drawn = base * np.exp(spread * noise) if base else spread * noise
        out[name] = jnp.asarray(drawn.astype(out[name].dtype))
    for name, factor in factors.items():
        out[name] = (out[name] * factor).astype(out[name].dtype)
    return out
```

```python
from contextlib import ExitStack

import numpy as np

import concourse.bass as bass
from concourse import mybir

P = 128
ALU = mybir.AluOpType
ACT = mybir.ActivationFunctionType
F32 = mybir.dt.float32
F32R = mybir.dt.float32r
BF16 = mybir.dt.bfloat16
U8 = mybir.dt.uint8
AX_X = mybir.AxisListType.X

BATCH, SEQ, DIM = 16, 128, 256
KC = DIM // P
XH, XD = 16, 16
XPAD = 32
DEPTH, HEADS, DH = 6, 16, 64
WINDOW = 64
INNER = HEADS * DH
OC = INNER // P
FF = DIM * 4 * 2 // 3
FULL = FF // P
REST = FF - FULL * P
GATE0 = 64
HALF = DH // 2
CH = 512
HPC = CH // DH
GROUP = 4
TOK = 4 * SEQ
VA = DH + 1
XVA = XD + 1
NEG_MASK = -1e30
NEG_INF = -1e18

XW_LOADS = 16
XLINKS = 15
VECTORS = 9

BATCH_STEPS = [("S", 0), ("S", 1), ("A", 0), ("T", 0), ("A", 1), ("V", 0), ("B", 0), ("T", 1), ("S", 2),
               ("B", 1), ("V", 1), ("S", 3), ("A", 2), ("O", 0), ("T", 2), ("A", 3), ("V", 2), ("T", 3),
               ("B", 2), ("A", 4), ("V", 3), ("A", 5), ("B", 3), ("O", 1)]
FIRST_STEPS = [("A", 0), ("A", 1), ("B", 0), ("A", 2), ("B", 1), ("A", 3), ("A", 4), ("B", 2), ("A", 5), ("B", 3)]
QK_CHUNKS = [0, 1, 3, 4]
V_CHUNKS = [2, 5]
FFN_STEPS = [("U", 0), ("U", 1), ("D", 0), ("U", 2), ("M", 0), ("D", 1), ("U", 3), ("R", 0), ("D", 2),
             ("U", 4), ("N", 0), ("D", 3), ("U", 5), ("D", 4), ("D", 5), ("N", 1)]


def build(nc, x, ctx_1024, mask, g_xattn, g_ffn, Wq, bq, Wk, bk, Wv, bv, Wo, bo,
          Wqkv, q_scale, k_scale, Wout, ln_g, ln_b, W1, b1, W2, b2, rope, band, eye, out):
    with ExitStack() as stack:
        def sb(name, shape, dt=F32):
            return stack.enter_context(nc.sbuf_tensor(name, shape, dt))

        def sem(name):
            return stack.enter_context(nc.semaphore(name))

        bank = [stack.enter_context(nc.psum_tensor(f"bank{i}", [P, CH], F32)) for i in range(8)]

        X0 = sb("X0", [P, BATCH, SEQ])
        X1 = sb("X1", [P, BATCH, SEQ + 1])
        wqkv = sb("wqkv", [P, 2, KC, 3 * INNER], F32R)
        wout = sb("wout", [P, 2, OC, DIM], F32R)
        w1 = sb("w1", [P, 2, KC, 2 * FULL + 1, P], F32R)
        w2 = sb("w2", [P, 2, FULL + 1, DIM], F32R)
        parts = sb("parts", [P, 2 * OC * 2 * SEQ], F32R)
        xs = sb("xs", [P, 2, KC, SEQ], F32R)
        oT = parts[:, :].rearrange("p (s c t) -> p s c t", s=2, c=OC)
        xn_parts = parts[:, 0:2 * KC * TOK].rearrange("p (s c t) -> p s c t", s=2, c=KC)
        h_parts = parts[:, 2 * KC * TOK:].rearrange("p (b s t) -> p b s t", b=2, s=2)
        ident = sb("ident", [P, P])
        ident_bf = sb("ident_bf", [P, P], BF16)
        band_f = sb("band_f", [P, P])
        band_bf = sb("band_bf", [P, P], BF16)
        rope_t = sb("rope_t", [P, 4, DH])
        qk_scale = sb("qk_scale", [P, 2, DH])
        rope_q = sb("rope_q", [P, 2, 2, DH])
        inv_dim = sb("inv_dim", [P, P])
        ones = sb("ones", [P, XH])
        ln_gb = sb("ln_gb", [P, 2, KC])
        b1_t = sb("b1_t", [P, 2 * FULL + 1])
        b2_t = sb("b2_t", [P, KC])
        gates = sb("gates", [P, 4])
        half = sb("half", [P, 16])
        work = sb("work", [P, 12032])

        offset = [0]

        def part(n):
            a = offset[0]
            offset[0] += n
            assert offset[0] <= work.shape[1], offset[0]
            return work[:, a:a + n]

        raw = part(2 * 1024).rearrange("p (b n) -> p b n", b=2)
        after_raw = offset[0]
        m1 = part(2 * CH).rearrange("p (b n) -> p b n", b=2)
        m2 = part(2 * CH).rearrange("p (b n) -> p b n", b=2)
        sq = part(CH)
        qkr = part(2 * CH).rearrange("p (b n) -> p b n", b=2)
        probs = part(2 * CH).rearrange("p (b n) -> p b n", b=2)
        probsT = part(2 * CH).rearrange("p (b n) -> p b n", b=2)
        qkT = part(4 * CH).rearrange("p (s n) -> p s n", s=4)
        vals = part(HEADS * VA).rearrange("p (h d) -> p h d", h=HEADS)
        outs = part(INNER).rearrange("p (h d) -> p h d", h=HEADS)
        norm2 = part(4 * HPC).rearrange("p (b n) -> p b n", b=4)
        rnorm = part(4 * HPC).rearrange("p (b n) -> p b n", b=4)
        smax = part(4 * GROUP).rearrange("p (b n) -> p b n", b=4)
        rsum = part(4 * GROUP).rearrange("p (b n) -> p b n", b=4)
        offset[0] = after_raw
        xc = part(KC * TOK).rearrange("p (c t) -> p c t", c=KC)
        xq = part(KC * TOK).rearrange("p (c t) -> p c t", c=KC)
        xg = part(KC * TOK).rearrange("p (c t) -> p c t", c=KC)
        gelu = part(2 * TOK).rearrange("p (b t) -> p b t", b=2)
        hf = part(2 * TOK).rearrange("p (b t) -> p b t", b=2)
        var4 = part(4)
        rstd4 = part(4)
        offset[0] = after_raw
        xwq = part(KC * XH * XPAD).rearrange("p (c h d) -> p c h d", c=KC, h=XH)
        xwk = part(KC * XH * XPAD).rearrange("p (c h d) -> p c h d", c=KC, h=XH)
        xwv = part(KC * DIM).rearrange("p (c n) -> p c n", c=KC)
        xwo = part(KC * DIM).rearrange("p (c n) -> p c n", c=KC)
        bqk = part(2 * 4).rearrange("p (a c) -> p a c", a=2)
        bvo = part(2 * DIM).rearrange("p (a n) -> p a n", a=2)
        xin = part(DIM)
        cin = part(DIM)
        mv = part(2)
        xnorm = part(DIM)
        xcent = part(DIM)
        tT = part(2 * KC * SEQ).rearrange("p (a c t) -> p a c t", a=2, c=KC)
        xqk = part(2 * 4 * SEQ).rearrange("p (a c t) -> p a c t", a=2, c=4)
        xv = part(XH * XVA).rearrange("p (h d) -> p h d", h=XH)
        xp = part(2 * CH).rearrange("p (b n) -> p b n", b=2)
        xpT = part(2 * CH).rearrange("p (b n) -> p b n", b=2)
        xo = part(DIM).rearrange("p (h d) -> p h d", h=XH)
        xoT = part(KC * SEQ).rearrange("p (c t) -> p c t", c=KC)
        x1 = part(DIM)
        xmax = part(16).rearrange("p (j i) -> p j i", j=4)
        xsum = part(16).rearrange("p (j i) -> p j i", j=4)
        xr = part(1)
        maskf = sb("maskf", [P, SEQ], BF16)
        mask8 = sb("mask8", [P, SEQ], U8)

        x1_dram = nc.dram_tensor("x_after_xattn", (BATCH, SEQ, DIM), F32, kind="Internal").ap()

        loaded = sem("constants_loaded")
        consts = sem("constants_ready")
        xw_loaded = sem("xattn_weights_loaded")
        x_in = sem("x_loaded")
        x1_out = sem("x1_stored")
        phase_done = sem("phase_done")
        consts_act, half_ok, v_ones = sem("constants_made"), sem("exponents_ready"), sem("ones_beside_values")
        chain, xvar_ready, xrstd, xn_made = sem("xattn_chain"), sem("xattn_variance"), sem("xattn_rstd"), sem("xattn_normalised")
        ctx_mm, xnT_mm, xT_copied = sem("ctx_transposed"), sem("xn_transposed"), sem("xattn_inputs_transposed")
        xk_mm, xv_mm, xq_mm, xqk_ready, xv_ready = (sem("xattn_k"), sem("xattn_v"), sem("xattn_q"), sem("xattn_qk_ready"),
                                                    sem("xattn_v_ready"))
        mask_made, xs_mm, xs_sub, xs_exp = sem("mask_made"), sem("xattn_scores"), sem("xattn_minus_max"), sem("xattn_probs")
        xt_mm, xpT_copied, xpv_mm, xo_norm = (sem("xattn_probs_transposed"), sem("xattn_probsT"), sem("xattn_pv"),
                                              sem("xattn_outs"))
        xoT_mm, xoT_copied, xwo_mm = sem("xattn_outs_transposed"), sem("xattn_outsT"), sem("xattn_wo")
        x1_made, x_mm, x_stored = sem("x1_made"), sem("x_transposed"), sem("x_stored")
        norm_sum, cleared, fin_copied = sem("norm_sums_ready"), sem("work_cleared"), sem("x_copied_back")

        raw_in = [sem("raw_weights_loaded0"), sem("raw_weights_loaded1")]
        raw_hi = sem("weights_high_part")
        raw_lo = sem("weights_low_part")
        vec_in = sem("layer_vectors_loaded")
        tables = sem("rope_tables_ready")
        xs_hi, xs_ready = sem("xs_high_part"), sem("xs_ready")
        qkv_mm = sem("qkv_chunk_done")
        squared, rotated, v_copied = sem("qk_squared"), sem("qk_rotated"), sem("v_copied")
        norms, rope_sum, rnorms, qk_ready = sem("norms_summed"), sem("rope_summed"), sem("rnorms_ready"), sem("qk_ready")
        b_mm, b_copied = sem("qk_transposed"), sem("qkT_copied")
        s_mm, s_max, s_sub, s_exp = sem("scores_done"), sem("max_ready"), sem("scores_minus_max"), sem("probs_ready")
        t_mm, t_copied = sem("probs_transposed"), sem("probsT_copied")
        v_mm, r_sum, o_norm = sem("pv_done"), sem("sum_inverted"), sem("outs_normalised")
        o_mm, o_hi, o_lo = sem("outs_transposed"), sem("outT_high_part"), sem("outT_low_part")
        w_mm, x_added = sem("wo_done"), sem("attention_added")

        mean_mm, centred, xsq, var_mm, var_ok, rstd_ok = (sem("mean_done"), sem("centred"), sem("centred_squared"),
                                                          sem("variance_done"), sem("variance_ready"), sem("rstd_ready"))
        bc_mm, xn_ok, xg_ok, xn_hi, xn_lo = (sem("rstd_spread"), sem("xn_ready"), sem("xn_affine"), sem("xn_high_part"),
                                             sem("xn_low_part"))
        u_mm, gelu_ok, h_ok, h_hi, h_lo = (sem("up_done"), sem("gelu_ready"), sem("h_ready"), sem("h_high_part"),
                                           sem("h_low_part"))
        d_mm, f_added = sem("down_done"), sem("ffn_added")
        fin_in, fin_mm, fin_ok, fin_out = sem("x1_loaded"), sem("x_back"), sem("out_ready"), sem("out_stored")

        def barrier(eng, phase):
            eng.drain().then_inc(phase_done, 1)
            eng.wait_ge(phase_done, phase * 4 + 4)

        def attn_pieces(layer):
            r = Wqkv[layer].rearrange("(c p) n -> c p n", p=P)
            o = Wout[layer].rearrange("(c p) n -> p c n", p=P)
            for c in range(KC):
                for n in range(0, 3 * INNER, 1024):
                    yield P, r[c, :, n:n + 1024], [(0, 1024, lambda s, c=c, n=n: wqkv[:, s, c, n:n + 1024])]
            for c in range(0, OC, 4):
                yield P, o[:, c:c + 4, :], [(0, 1024, lambda s, c=c: wout[:, s, c:c + 4, :].rearrange("p c n -> p (c n)"))]

        def ffn_pieces(layer):
            r = W1[layer].rearrange("(c p) n -> c p n", p=P)
            d = W2[layer]
            for c in range(KC):
                for a in range(2):
                    g0 = GATE0 if a else 0
                    yield P, r[c, :, a * FF:(a + 1) * FF], [
                        (0, FULL * P, lambda s, c=c, a=a: w1[:, s, c, a * FULL:(a + 1) * FULL, :].rearrange("p m n -> p (m n)")),
                        (FULL * P, FF, lambda s, c=c, g0=g0: w1[:, s, c, 2 * FULL, g0:g0 + REST])]
            full = d[0:FULL * P, :].rearrange("(c p) n -> p c n", p=P)
            for c, n in ((0, 4), (4, 1)):
                yield P, full[:, c:c + n, :], [(0, n * DIM, lambda s, c=c, n=n: w2[:, s, c:c + n, :].rearrange("p c n -> p (c n)"))]
            yield REST, d[FULL * P:FF, :], [(0, DIM, lambda s: w2[0:REST, s, FULL, :])]

        ATTN_N, FFN_N = KC * 3 + OC // 4, KC * 2 + 3
        PIECES = ATTN_N + FFN_N

        def load_pieces(sp, pieces, base):
            for i, (rows, src, _) in enumerate(pieces):
                sp.wait_ge(raw_lo, base + i - 1 if i else base)
                n = 1
                for w in src.shape[1:]:
                    n *= w
                dst = raw[0:rows, i % 2, 0:n]
                if len(src.shape) == 3:
                    dst = dst.rearrange("p (c n) -> p c n", c=src.shape[1])
                sp.dma_start(dst, src).then_inc(raw_in[i % 2], 16)

        def raw_count(layer, kind, i):
            per = [(ATTN_N + 1) // 2 + (FFN_N + 1) // 2, ATTN_N // 2 + FFN_N // 2][i % 2]
            before = 0 if kind == 0 else [(ATTN_N + 1) // 2, ATTN_N // 2][i % 2]
            return (layer * per + (before + i // 2 + 1)) * 16

        def high_parts(act, pieces, layer, kind):
            for i, (rows, _, dests) in enumerate(pieces):
                act.wait_ge(raw_in[i % 2], raw_count(layer, kind, i))
                for k, (a, b, dst) in enumerate(dests):
                    ins = nc.scalar.copy(dst(0), raw[0:rows, i % 2, a:b])
                ins.then_inc(raw_hi, 1)

        def low_parts(dve, pieces, layer, kind):
            base = layer * PIECES + (ATTN_N if kind else 0)
            for i, (rows, _, dests) in enumerate(pieces):
                dve.wait_ge(raw_hi, base + i + 1)
                dve.wait_ge(raw_in[i % 2], raw_count(layer, kind, i))
                for k, (a, b, dst) in enumerate(dests):
                    ins = nc.vector.tensor_tensor(dst(1), raw[0:rows, i % 2, a:b], dst(0).bitcast(F32), ALU.subtract)
                ins.then_inc(raw_lo, 1)

        def three(pe, out_ap, lhs, rhs, first, last):
            pe.matmul(out_ap, lhs(0), rhs(0), start=first, stop=False)
            pe.matmul(out_ap, lhs(0), rhs(1), start=False, stop=False)
            return pe.matmul(out_ap, lhs(1), rhs(0), start=False, stop=last)

        def heads_of(u):
            return [HPC * (u // 2) + 2 * i + u % 2 for i in range(GROUP)]

        block = stack.enter_context(nc.Block())

        @block.sync
        def _(sp):
            for dst, src in ((ident, eye), (band_f, band)):
                sp.dma_start(dst[:, :], src).then_inc(loaded, 16)
            sp.dma_start(rope_t[:, :, :], rope).then_inc(loaded, 16)
            sp.dma_start(gates[:, 0:1], g_xattn.rearrange("(o n) -> o n", o=1).to_broadcast([P, 1])).then_inc(loaded, 16)
            sp.dma_start(gates[:, 1:2], g_ffn.rearrange("(o n) -> o n", o=1).to_broadcast([P, 1])).then_inc(loaded, 16)
            sp.wait_ge(consts, 1)
            for dst, src, c in ((xwq, Wq, 0), (xwk, Wk, 0), (xwq, Wq, 1), (xwk, Wk, 1)):
                sp.dma_start(dst[:, c, :, 0:XD], src[c * P:(c + 1) * P, :].rearrange("p (h d) -> p h d", h=XH)).then_inc(xw_loaded, 16)
            sp.dma_start(xwv, Wv.rearrange("(c p) n -> p c n", p=P)).then_inc(xw_loaded, 16)
            sp.dma_start(xwo, Wo.rearrange("(c p) n -> p c n", p=P)).then_inc(xw_loaded, 16)
            for a, b in ((0, bq), (1, bk)):
                for j in range(4):
                    sp.dma_start(bqk[32 * j:32 * j + XD, a, :], b.rearrange("(c j d) -> j d c", j=4, d=XD)[j],
                                 allow_slow_non_contiguous=True).then_inc(xw_loaded, 16)
            for a, b in ((0, bv), (1, bo)):
                sp.dma_start(bvo[:, a, :], b.rearrange("(o n) -> o n", o=1).to_broadcast([P, DIM])).then_inc(xw_loaded, 16)
            with sp.Fori(0, BATCH) as b:
                sp.wait_ge(x1_made, b)
                sp.wait_ge(mask_made, b)
                sp.wait_ge(ctx_mm, b)
                sp.dma_start(xin, x[b]).then_inc(x_in, 16)
                sp.dma_start(cin, ctx_1024[b]).then_inc(x_in, 16)
                sp.dma_start(mask8[:, :], mask[b]).then_inc(x_in, 16)
                sp.wait_ge(x1_made, b + 1)
                sp.dma_start(x1_dram[b], x1).then_inc(x1_out, 16)
            sp.wait_ge(x1_out, BATCH * 16)
            load_pieces(sp, list(attn_pieces(0)), 0)
            with sp.Fori(0, DEPTH) as layer:
                after = sp.snap((layer + 1) % DEPTH)
                ffn_base = sp.snap(layer * PIECES + ATTN_N)
                attn_base = sp.snap(layer * PIECES + PIECES)
                sp.wait_ge(phase_done, layer * 8 + 4)
                sp.dma_start(qk_scale[:, 0, :], q_scale[bass.ds(layer, 1), :].to_broadcast([P, DH])).then_inc(vec_in, 16)
                sp.dma_start(qk_scale[:, 1, :], k_scale[bass.ds(layer, 1), :].to_broadcast([P, DH])).then_inc(vec_in, 16)
                for a, b in ((0, ln_g), (1, ln_b)):
                    sp.dma_start(ln_gb[:, a, :], b[layer].rearrange("(c p) -> p c", p=P), allow_slow_non_contiguous=True).then_inc(vec_in, 16)
                sp.dma_start(b2_t[:, :], b2[layer].rearrange("(c p) -> p c", p=P), allow_slow_non_contiguous=True).then_inc(vec_in, 16)
                for a in range(2):
                    v = b1[layer][a * FF:(a + 1) * FF]
                    sp.dma_start(b1_t[:, a * FULL:(a + 1) * FULL], v[0:FULL * P].rearrange("(c p) -> p c", p=P),
                                 allow_slow_non_contiguous=True).then_inc(vec_in, 16)
                    sp.dma_start(b1_t[a * GATE0:a * GATE0 + REST, 2 * FULL:2 * FULL + 1],
                                 v[FULL * P:FF].rearrange("(p o) -> p o", o=1), allow_slow_non_contiguous=True).then_inc(vec_in, 16)
                load_pieces(sp, list(ffn_pieces(layer)), ffn_base)
                load_pieces(sp, list(attn_pieces(after)), attn_base)
            sp.wait_ge(phase_done, DEPTH * 8 + 4)
            with sp.Fori(0, BATCH) as b:
                sp.wait_ge(fin_ok, b)
                sp.dma_start(xin, x1_dram[b]).then_inc(fin_in, 16)
                sp.wait_ge(fin_ok, b + 1)
                sp.dma_start(out[b], x1).then_inc(fin_out, 16)
            sp.wait_ge(fin_out, BATCH * 16)

        @block.tensor
        def _(pe):
            pe.wait_ge(consts, 1)
            pe.wait_ge(consts_act, 1)
            pe.wait_ge(xw_loaded, XW_LOADS * 16)
            pe.wait_ge(loaded, 80)
            with pe.Fori(0, BATCH) as b:
                pe.wait_ge(x_in, b * 48 + 48)
                pe.wait_ge(xo_norm, b * 4)
                for c in range(KC):
                    ins = pe.transpose(bank[0][:, c * P:(c + 1) * P], cin[:, c * P:(c + 1) * P], ident[:, :])
                ins.then_inc(ctx_mm, 1)
                pe.wait_ge(xn_made, b * 2 + 1)
                pe.wait_ge(xoT_copied, b)
                for c in range(KC):
                    ins = pe.transpose(bank[1][:, c * P:(c + 1) * P], xnorm[:, c * P:(c + 1) * P], ident[:, :])
                ins.then_inc(xnT_mm, 1)
                pe.wait_ge(xT_copied, b * 2 + 1)
                pe.wait_ge(x1_made, b)
                for j in range(4):
                    for c in range(KC):
                        ins = pe.matmul(bank[2][:, j * P:(j + 1) * P], xwk[:, c, 4 * j:4 * j + 4, :],
                                        tT[:, 1, c, :], start=(c == 0), stop=(c == KC - 1))
                ins.then_inc(xk_mm, 1)
                pe.wait_ge(x_stored, b)
                for c in range(KC):
                    ins = pe.matmul(bank[3][:, 0:DIM], tT[:, 1, c, :], xwv[:, c, :], start=(c == 0), stop=(c == KC - 1))
                ins.then_inc(xv_mm, 1)
                pe.wait_ge(xT_copied, b * 2 + 2)
                for j in range(4):
                    for c in range(KC):
                        ins = pe.matmul(bank[4][:, j * P:(j + 1) * P], xwq[:, c, 4 * j:4 * j + 4, :],
                                        tT[:, 0, c, :], start=(c == 0), stop=(c == KC - 1))
                ins.then_inc(xq_mm, 1)

                def scores(j):
                    pe.wait_ge(xs_sub, b * 4 + max(0, j - 1))
                    pe.matmul(bank[5 + j % 2][:, :], ident_bf[:, :], maskf[:, None, :].to_broadcast([P, GROUP, SEQ]),
                              start=True, stop=True)
                    for i in range(GROUP):
                        r = slice(XPAD * j, XPAD * j + XD)
                        ins = pe.matmul(bank[5 + j % 2][:, i * P:(i + 1) * P], xqk[r, 0, i, :], xqk[r, 1, i, :],
                                        start=False, stop=True, skip_group_check=True)
                    ins.then_inc(xs_mm, 1)

                pe.wait_ge(mask_made, b + 1)
                pe.wait_ge(xqk_ready, b + 1)
                pe.wait_ge(xv_ready, b + 1)
                scores(0)
                for j in range(4):
                    if j < 3:
                        scores(j + 1)
                    pe.wait_ge(xs_exp, b * 4 + j + 1)
                    pe.wait_ge(xpT_copied, b * 4 + j)
                    for i in range(GROUP):
                        ins = pe.transpose(bank[7][:, i * P:(i + 1) * P], xp[:, j % 2, i * P:(i + 1) * P], ident[:, :])
                    ins.then_inc(xt_mm, 1)
                    pe.wait_ge(xpT_copied, b * 4 + j + 1)
                    pe.wait_ge(xo_norm, b * 4 + j)
                    for i in range(GROUP):
                        ins = pe.matmul(bank[0][:, i * XVA:(i + 1) * XVA], xpT[:, j % 2, i * P:(i + 1) * P],
                                        xv[:, 4 * i + j, :], start=True, stop=True)
                    ins.then_inc(xpv_mm, 1)
                pe.wait_ge(xo_norm, b * 4 + 4)
                for c in range(KC):
                    ins = pe.transpose(bank[1][:, c * P:(c + 1) * P], xo[:, 8 * c:8 * c + 8, :], ident[:, :])
                ins.then_inc(xoT_mm, 1)
                pe.wait_ge(xoT_copied, b + 1)
                for c in range(KC):
                    ins = pe.matmul(bank[2][:, 0:DIM], xoT[:, c, :], xwo[:, c, :], start=(c == 0), stop=(c == KC - 1))
                ins.then_inc(xwo_mm, 1)
                pe.wait_ge(xn_made, b * 2 + 2)
                for c in range(KC):
                    ins = pe.transpose(bank[3][:, c * P:(c + 1) * P], xnorm[:, c * P:(c + 1) * P], ident[:, :])
                ins.then_inc(x_mm, 1)
            barrier(pe, 0)

            def a_step(c, gb):
                if c == 0:
                    pe.wait_ge(xs_ready, gb + 1)
                if c == 0:
                    pe.wait_ge(rotated, gb * 4)
                elif c == 1:
                    pe.wait_ge(v_copied, gb * 2)
                elif c in (2, 3, 5):
                    done = {2: 1, 3: 2, 5: 3}[c]
                    pe.wait_ge(rotated, gb * 4 + done)
                else:
                    pe.wait_ge(v_copied, gb * 2 + 1)
                col = (c % 3) * INNER + (c // 3) * CH
                for k in range(KC):
                    ins = three(pe, bank[c % 2][:, :], lambda s: xs[:, s, k, :],
                                lambda s: wqkv[:, s, k, col:col + CH], k == 0, k == KC - 1)
                ins.then_inc(qkv_mm, 1)

            def b_step(n, gb):
                pe.wait_ge(qk_ready, gb * 4 + n + 1)
                pe.wait_ge(b_copied, gb * 4 + n)
                for j in range(4):
                    ins = pe.transpose(bank[4][:, j * P:(j + 1) * P], qkr[:, n % 2, j * P:(j + 1) * P], ident[:, :])
                ins.then_inc(b_mm, 1)

            def s_step(u, gb):
                pe.wait_ge(b_copied, gb * 4 + (4 if u >= 2 else 2))
                pe.wait_ge(s_sub, gb * 4 + max(0, u - 1))
                b = bank[2 + u % 2]
                pe.matmul(b[:, :], ident_bf[:, :], band_bf[:, None, :].to_broadcast([P, GROUP, SEQ]), start=True, stop=True)
                r = slice(DH * (u % 2), DH * (u % 2) + DH)
                slot = 2 * (u // 2)
                for i in range(GROUP):
                    cols = slice(i * P, (i + 1) * P)
                    ins = pe.matmul(b[:, cols], qkT[r, slot, cols], qkT[r, slot + 1, cols], start=False, stop=True,
                                    skip_group_check=True)
                ins.then_inc(s_mm, 1)

            def t_step(u, gb):
                pe.wait_ge(s_exp, gb * 4 + u + 1)
                if u == 0:
                    pe.wait_ge(o_lo, gb * 2)
                elif u == 2:
                    pe.wait_ge(o_lo, gb * 2 + 1)
                else:
                    pe.wait_ge(t_copied, gb * 4 + u)
                for i in range(GROUP):
                    ins = pe.transpose(bank[5][:, i * P:(i + 1) * P], probs[:, u % 2, i * P:(i + 1) * P], ident[:, :])
                ins.then_inc(t_mm, 1)

            def v_step(u, gb):
                pe.wait_ge(t_copied, gb * 4 + u + 1)
                pe.wait_ge(v_copied, gb * 2 + 1 + u // 2)
                pe.wait_ge(o_norm, gb * 4 + u)
                for i, h in enumerate(heads_of(u)):
                    ins = pe.matmul(bank[6][:, i * VA:(i + 1) * VA], probsT[:, u % 2, i * P:(i + 1) * P], vals[:, h, :],
                                    start=True, stop=True)
                ins.then_inc(v_mm, 1)

            def o_step(j, gb):
                pe.wait_ge(o_norm, gb * 4 + 2 * j + 2)
                pe.wait_ge(t_copied, gb * 4 + 2 * j + 2)
                for i in range(4):
                    h = HPC * j + 2 * i
                    ins = pe.transpose(bank[5][:, i * P:(i + 1) * P], outs[:, h:h + 2, :], ident[:, :])
                ins.then_inc(o_mm, 1)

            def w_step(gp):
                pe.wait_ge(o_lo, gp * 4 + 4)
                pe.wait_ge(x_added, gp)
                for m in range(KC):
                    for c in range(OC):
                        ins = three(pe, bank[7][:, m * 2 * SEQ:(m + 1) * 2 * SEQ], lambda s: wout[:, s, c, m * P:(m + 1) * P],
                                    lambda s: oT[:, s, c, :], c == 0, c == OC - 1)
                ins.then_inc(w_mm, 1)

            def attend(gb, nxt):
                for kind, n in BATCH_STEPS:
                    if kind in "AB":
                        if nxt is not None:
                            (a_step if kind == "A" else b_step)(n, nxt)
                    else:
                        {"S": s_step, "T": t_step, "V": v_step, "O": o_step}[kind](n, gb)

            def m_step(k, gt, t):
                pe.wait_ge(xn_ok, gt)
                pe.matmul(bank[6][:, :], inv_dim[:, :], X0[:, bass.ds(t * 4, 4), :], start=True, stop=False)
                pe.matmul(bank[6][:, :], inv_dim[:, :], X1[:, bass.ds(t * 4, 4), 0:SEQ], start=False, stop=True).then_inc(mean_mm, 1)

            def r_step(k, gt, t):
                pe.wait_ge(xsq, gt + 1)
                pe.wait_ge(var_ok, gt)
                for j in range(4):
                    for c in range(KC):
                        ins = pe.matmul(bank[7][:, j:j + 1], xq[:, c, j * P:(j + 1) * P], inv_dim[:, 0:1],
                                        start=(c == 0), stop=(c == KC - 1))
                ins.then_inc(var_mm, 1)

            def n_step(k, gt, t):
                if k:
                    return
                pe.wait_ge(rstd_ok, gt + 1)
                pe.wait_ge(centred, gt + 1)
                for j in range(4):
                    ins = pe.matmul(bank[6][:, j * P:(j + 1) * P], rstd4[:, j:j + 1].to_broadcast([P, P]), ident[:, :],
                                    start=True, stop=True)
                ins.then_inc(bc_mm, 1)

            def u_step(m, gt):
                if m == 0:
                    pe.wait_ge(xn_lo, gt + 1)
                pe.wait_ge(h_ok, gt * 6 + max(0, m - 1))
                for a in range(2 if m < FULL else 1):
                    rows = P if m < FULL else GATE0 + REST
                    for c in range(KC):
                        ins = three(pe, bank[2 * (m % 2) + a][0:rows, :], lambda s: w1[:, s, c, a * FULL + m if m < FULL else 2 * FULL, 0:rows],
                                    lambda s: xn_parts[:, s, c, :], c == 0, c == KC - 1)
                ins.then_inc(u_mm, 1)

            def d_step(m, gt):
                pe.wait_ge(h_lo, gt * 6 + m + 1)
                if m == 0:
                    pe.wait_ge(f_added, gt)
                rows = P if m < FULL else REST
                for o in range(KC):
                    ins = three(pe, bank[4 + o][:, :], lambda s: w2[0:rows, s, m, o * P:(o + 1) * P],
                                lambda s: h_parts[0:rows, m % 2, s, :], m == 0, m == FULL)
                ins.then_inc(d_mm, 1)

            def feed(gt, nxt, t):
                for kind, n in FFN_STEPS:
                    if kind in "UD":
                        {"U": u_step, "D": d_step}[kind](n, gt)
                    elif nxt is not None:
                        {"M": m_step, "R": r_step, "N": n_step}[kind](n, nxt, t + 1)

            with pe.Fori(0, DEPTH) as layer:
                pe.wait_ge(raw_lo, layer * PIECES + ATTN_N)
                for kind, n in FIRST_STEPS:
                    (a_step if kind == "A" else b_step)(n, layer * BATCH)
                with pe.Fori(0, BATCH // 2 - 1) as pair:
                    gb = layer * BATCH + pair * 2
                    attend(gb, gb + 1)
                    attend(gb + 1, gb + 2)
                    w_step(layer * (BATCH // 2) + pair)
                gb = layer * BATCH + BATCH - 2
                attend(gb, gb + 1)
                attend(gb + 1, None)
                w_step(layer * (BATCH // 2) + BATCH // 2 - 1)
                barrier(pe, layer * 2 + 1)
                pe.wait_ge(raw_lo, layer * PIECES + PIECES)
                for kind, n in FFN_STEPS:
                    if kind in "MRN":
                        {"M": m_step, "R": r_step, "N": n_step}[kind](n, layer * 4, 0)
                with pe.Fori(0, 3) as t:
                    feed(layer * 4 + t, layer * 4 + t + 1, t)
                feed(layer * 4 + 3, None, 3)
                barrier(pe, layer * 2 + 2)
            with pe.Fori(0, BATCH) as b:
                pe.wait_ge(fin_copied, b + 1)
                for c in range(KC):
                    ins = pe.transpose(bank[0][:, c * P:(c + 1) * P], xoT[:, c, :], ident[:, :])
                ins.then_inc(fin_mm, 1)

        @block.scalar
        def _(act):
            act.wait_ge(loaded, 80)
            nc.scalar.copy(ident_bf[:, :], ident[:, :])
            nc.scalar.activation(gates[:, 2:4], gates[:, 0:2], ACT.Tanh)
            nc.scalar.copy(band_bf[:, :], band_f[:, :]).then_inc(consts_act, 1)
            act.wait_ge(xw_loaded, XW_LOADS * 16)
            act.wait_ge(consts, 1)
            with act.Fori(0, BATCH) as b:
                act.wait_ge(ctx_mm, b + 1)
                act.wait_ge(xq_mm, b)
                nc.scalar.copy(tT[:, 1, :, :], bank[0][:, 0:DIM]).then_inc(xT_copied, 1)
                act.wait_ge(xnT_mm, b + 1)
                nc.scalar.copy(tT[:, 0, :, :], bank[1][:, 0:DIM]).then_inc(xT_copied, 1)
                for a, s, done in ((1, 2, xk_mm), (0, 4, xq_mm)):
                    act.wait_ge(done, b + 1)
                    act.wait_ge(xs_mm, b * 4)
                    for i in range(4):
                        ins = nc.scalar.activation(xqk[:, a, i, :], bank[s][:, i * P:(i + 1) * P], ACT.Identity,
                                                   bias=bqk[:, a, i:i + 1])
                ins.then_inc(xqk_ready, 1)
                for j in range(4):
                    act.wait_ge(xs_sub, b * 4 + j + 1)
                    nc.scalar.activation(xp[:, j % 2, :], xp[:, j % 2, :], ACT.Exp, scale=XD ** -0.5).then_inc(xs_exp, 1)
                    act.wait_ge(xt_mm, b * 4 + j + 1)
                    act.wait_ge(xpv_mm, b * 4 + max(0, j - 1))
                    nc.scalar.copy(xpT[:, j % 2, :], bank[7][:, :]).then_inc(xpT_copied, 1)
                act.wait_ge(xoT_mm, b + 1)
                act.wait_ge(xwo_mm, b)
                nc.scalar.copy(xoT[:, :, :], bank[1][:, 0:DIM]).then_inc(xoT_copied, 1)
            barrier(act, 0)

            def a_step(c, gb):
                act.wait_ge(qkv_mm, gb * 6 + c + 1)
                src = bank[c % 2]
                if c in V_CHUNKS:
                    j = V_CHUNKS.index(c)
                    dst = vals[:, HPC * j:HPC * (j + 1), 0:DH]
                    nc.scalar.copy(dst, src[:, :].rearrange("p (h d) -> p h d", h=HPC)).then_inc(v_copied, 1)
                else:
                    n = QK_CHUNKS.index(c)
                    act.wait_ge(norms, gb * 4 + n)
                    nc.scalar.square(sq[:, :], src[:, :]).then_inc(squared, 1)

            def b_step(n, gb):
                act.wait_ge(b_mm, gb * 4 + n + 1)
                nc.scalar.copy(qkT[:, n, :], bank[4][:, :]).then_inc(b_copied, 1)

            def s_step(u, gb):
                act.wait_ge(s_sub, gb * 4 + u + 1)
                nc.scalar.activation(probs[:, u % 2, :], probs[:, u % 2, :], ACT.Exp, scale=8.0).then_inc(s_exp, 1)

            def t_step(u, gb):
                act.wait_ge(t_mm, gb * 4 + u + 1)
                act.wait_ge(v_mm, gb * 4 + max(0, u - 1))
                nc.scalar.copy(probsT[:, u % 2, :], bank[5][:, :]).then_inc(t_copied, 1)

            def o_step(j, gb, half_):
                act.wait_ge(o_mm, gb * 2 + j + 1)
                dst = oT[:, 0, 4 * j:4 * j + 4, half_ * SEQ:(half_ + 1) * SEQ]
                nc.scalar.copy(dst, bank[5][:, :].rearrange("p (c t) -> p c t", c=4)).then_inc(o_hi, 1)

            def attend(gb, nxt, half_, gp):
                for kind, n in BATCH_STEPS:
                    if kind in "AB":
                        if nxt is not None:
                            if kind == "A" and n in V_CHUNKS:
                                act.wait_ge(v_mm, gb * 4 + 2 * V_CHUNKS.index(n) + 2)
                            if kind == "B":
                                act.wait_ge(s_mm, gb * 4 + 2 * (n // 2) + 2)
                            (a_step if kind == "A" else b_step)(n, nxt)
                    elif kind == "O":
                        if n == 0 and half_ == 0:
                            act.wait_ge(w_mm, gp)
                        o_step(n, gb, half_)
                    elif kind != "V":
                        {"S": s_step, "T": t_step}[kind](n, gb)

            def ln_steps(kind, k, gt):
                if kind == "M":
                    act.wait_ge(centred, gt + 1)
                    act.wait_ge(var_mm, gt)
                    nc.scalar.square(xq[:, :, :], xc[:, :, :]).then_inc(xsq, 1)
                elif kind == "N" and k == 1:
                    act.wait_ge(xn_ok, gt + 1)
                    act.wait_ge(xn_lo, gt)
                    for c in range(KC):
                        ins = nc.scalar.activation(xg[:, c, :], xq[:, c, :], ACT.Identity, bias=ln_gb[:, 1, c:c + 1],
                                                   scale=ln_gb[:, 0, c:c + 1])
                    ins.then_inc(xg_ok, 1)

            def u_step(m, gt):
                act.wait_ge(u_mm, gt * 6 + m + 1)
                act.wait_ge(h_ok, gt * 6 + max(0, m - 1))
                if m < FULL:
                    ins = nc.scalar.activation(gelu[:, m % 2, :], bank[2 * (m % 2) + 1][:, :], ACT.Gelu,
                                               bias=b1_t[:, FULL + m:FULL + m + 1])
                else:
                    r = slice(GATE0, GATE0 + REST)
                    ins = nc.scalar.activation(gelu[0:REST, m % 2, :], bank[2 * (m % 2)][r, :], ACT.Gelu,
                                               bias=b1_t[r, 2 * FULL:2 * FULL + 1])
                ins.then_inc(gelu_ok, 1)

            def h_high(m, gt):
                rows = P if m < FULL else REST
                act.wait_ge(h_ok, gt * 6 + m + 1)
                act.wait_ge(d_mm, gt * 6 + max(0, m - 1))
                nc.scalar.copy(h_parts[0:rows, m % 2, 0, :], hf[0:rows, m % 2, :]).then_inc(h_hi, 1)

            def feed(gt, nxt):
                for kind, n in FFN_STEPS:
                    if kind == "U":
                        u_step(n, gt)
                        h_high(n, gt)
                    elif kind != "D" and nxt is not None:
                        ln_steps(kind, n, nxt)

            high_parts(act, list(attn_pieces(0)), 0, 0)
            with act.Fori(0, DEPTH) as layer:
                for kind, n in FIRST_STEPS:
                    (a_step if kind == "A" else b_step)(n, layer * BATCH)
                high_parts(act, list(ffn_pieces(0)), layer, 1)
                with act.Fori(0, BATCH // 2 - 1) as pair:
                    gb = layer * BATCH + pair * 2
                    gp = layer * (BATCH // 2) + pair
                    attend(gb, gb + 1, 0, gp)
                    attend(gb + 1, gb + 2, 1, gp)
                gb = layer * BATCH + BATCH - 2
                gp = layer * (BATCH // 2) + BATCH // 2 - 1
                attend(gb, gb + 1, 0, gp)
                attend(gb + 1, None, 1, gp)
                barrier(act, layer * 2 + 1)
                act.wait_ge(vec_in, (layer + 1) * VECTORS * 16)
                for kind, n in FFN_STEPS:
                    if kind in "MRN":
                        ln_steps(kind, n, layer * 4)
                high_parts(act, list(attn_pieces(0)), layer + 1, 0)
                with act.Fori(0, 3) as t:
                    feed(layer * 4 + t, layer * 4 + t + 1)
                feed(layer * 4 + 3, None)
                barrier(act, layer * 2 + 2)

        @block.vector
        def _(dve):
            nc.vector.memset(work[:, :], 0.0).then_inc(cleared, 1)
            dve.wait_ge(cleared, 1)
            nc.vector.memset(inv_dim[:, :], 1.0 / DIM)
            nc.vector.memset(X1[:, :, 0:1], 0.0)
            nc.vector.memset(b1_t[:, :], 0.0)
            nc.vector.memset(w1[:, :, :, 2 * FULL, REST:GATE0].bitcast(F32), 0.0)
            nc.vector.memset(xv[:, :, XD:XVA], 1.0).then_inc(consts, 1)
            dve.wait_ge(consts_act, 1)
            dve.wait_ge(xw_loaded, XW_LOADS * 16)
            dve.wait_ge(consts, 1)
            with dve.Fori(0, BATCH) as b:
                count = [0]

                def link(ins):
                    count[0] += 1
                    ins.then_inc(chain, 1)
                    dve.wait_ge(chain, b * XLINKS + count[0])

                def layernorm(src, k):
                    link(nc.vector.tensor_reduce(mv[:, 0:1], src, AX_X, ALU.add))
                    link(nc.vector.tensor_scalar(mv[:, 0:1], mv[:, 0:1], 1.0 / DIM, None, ALU.mult))
                    link(nc.vector.tensor_scalar(xcent, src, mv[:, 0:1], None, ALU.subtract))
                    nc.vector.tensor_tensor_reduce(out=xnorm, in0=xcent, in1=xcent, scale=1.0 / DIM, scalar=1e-5,
                                                   op0=ALU.mult, op1=ALU.add, accum_out=mv[:, 1:2]).then_inc(xvar_ready, 1)
                    dve.wait_ge(xrstd, b * 2 + k + 1)
                    nc.vector.tensor_scalar(xnorm, xcent, xr[:, 0:1], None, ALU.mult).then_inc(xn_made, 1)

                dve.wait_ge(x_in, b * 48 + 48)
                dve.wait_ge(x_mm, b)
                layernorm(xin, 0)
                dve.wait_ge(xs_mm, b * 4)
                nc.vector.tensor_scalar(maskf[:, :], mask8[:, :], NEG_INF, None, ALU.mult).then_inc(mask_made, 1)
                dve.wait_ge(xv_mm, b + 1)
                dve.wait_ge(xpv_mm, b * 4)
                nc.vector.tensor_tensor(xv[:, :, 0:XD], bank[3][:, 0:DIM].rearrange("p (h d) -> p h d", h=XH),
                                        bvo[:, 0, :].rearrange("p (h d) -> p h d", h=XH), ALU.add).then_inc(xv_ready, 1)

                def subtract_max(j):
                    dve.wait_ge(xs_mm, b * 4 + j + 1)
                    s3 = bank[5 + j % 2][:, :].rearrange("p (h t) -> p h t", h=GROUP)
                    link(nc.vector.tensor_reduce(xmax[:, j], s3, AX_X, ALU.max))
                    dve.wait_ge(xt_mm, b * 4 + max(0, j - 1))
                    nc.vector.tensor_tensor(xp[:, j % 2, :].rearrange("p (h t) -> p h t", h=GROUP), s3,
                                            xmax[:, j, :, None].to_broadcast([P, GROUP, SEQ]), ALU.subtract).then_inc(xs_sub, 1)

                subtract_max(0)
                for j in range(4):
                    if j < 3:
                        subtract_max(j + 1)
                    dve.wait_ge(xpv_mm, b * 4 + j + 1)
                    o3 = bank[0][:, 0:GROUP * XVA].rearrange("p (h d) -> p h d", h=GROUP)
                    link(nc.vector.reciprocal(xsum[:, j], o3[:, :, XD]))
                    nc.vector.tensor_tensor(xo.rearrange("p (i j) d -> p i j d", j=4)[:, :, j, :], o3[:, :, 0:XD],
                                            xsum[:, j, :, None].to_broadcast([P, GROUP, XD]), ALU.mult).then_inc(xo_norm, 1)
                dve.wait_ge(xwo_mm, b + 1)
                dve.wait_ge(x1_out, b * 16)
                link(nc.vector.tensor_tensor(x1, bank[2][:, 0:DIM], bvo[:, 1, :], ALU.add))
                nc.vector.scalar_tensor_tensor(out=x1, in0=x1, scalar=gates[:, 2:3], in1=xin, op0=ALU.mult,
                                               op1=ALU.add).then_inc(x1_made, 1)
                dve.wait_ge(x1_made, b + 1)
                dve.wait_ge(xnT_mm, b + 1)
                layernorm(x1, 1)
                dve.wait_ge(x_mm, b + 1)
                nc.vector.tensor_copy(X0[:, bass.ds(b, 1), :], bank[3][:, 0:P])
                nc.vector.tensor_copy(X1[:, bass.ds(b, 1), 1:SEQ + 1], bank[3][:, P:2 * P]).then_inc(x_stored, 1)
                assert count[0] == XLINKS, count
            barrier(dve, 0)
            nc.vector.memset(vals[:, :, DH:VA], 1.0).then_inc(v_ones, 1)

            def x_step(gb, b):
                dve.wait_ge(qkv_mm, gb * 6)
                nc.vector.tensor_copy(xs[:, 0, 0, :], X0[:, bass.ds(b, 1), :])
                nc.vector.tensor_copy(xs[:, 0, 1, :], X1[:, bass.ds(b, 1), 0:SEQ]).then_inc(xs_hi, 1)
                dve.wait_ge(xs_hi, gb + 1)
                nc.vector.tensor_tensor(xs[:, 1, 0, :], X0[:, bass.ds(b, 1), :], xs[:, 0, 0, :].bitcast(F32), ALU.subtract)
                nc.vector.tensor_tensor(xs[:, 1, 1, :], X1[:, bass.ds(b, 1), 0:SEQ], xs[:, 0, 1, :].bitcast(F32),
                                        ALU.subtract).then_inc(xs_ready, 1)

            def a_step(c, gb):
                if c in V_CHUNKS:
                    return
                n = QK_CHUNKS.index(c)
                a = n % 2
                dve.wait_ge(qkv_mm, gb * 6 + c + 1)
                dve.wait_ge(squared, gb * 4 + n + 1)
                dve.wait_ge(rope_sum, gb * 4 + max(0, n - 1))
                src = bank[c % 2][:, :].rearrange("p (h d) -> p h d", h=HPC)
                d1 = m1[:, n % 2, :].rearrange("p (h d) -> p h d", h=HPC)
                d2 = m2[:, n % 2, :].rearrange("p (h d) -> p h d", h=HPC)
                cos, sin = rope_q[:, a, 0, :], rope_q[:, a, 1, :]
                nc.vector.tensor_tensor(d2[:, :, 0:HALF], src[:, :, HALF:DH], sin[:, None, 0:HALF].to_broadcast([P, HPC, HALF]), ALU.mult)
                nc.vector.tensor_tensor(d2[:, :, HALF:DH], src[:, :, 0:HALF], sin[:, None, HALF:DH].to_broadcast([P, HPC, HALF]), ALU.mult)
                nc.vector.tensor_tensor(d1, src, cos[:, None, :].to_broadcast([P, HPC, DH]), ALU.mult).then_inc(rotated, 1)
                dve.wait_ge(rnorms, gb * 4 + n)
                nc.vector.tensor_reduce(norm2[:, n, :], sq[:, :].rearrange("p (h d) -> p h d", h=HPC), AX_X, ALU.add).then_inc(norm_sum, 1)
                dve.wait_ge(norm_sum, gb * 4 + n + 1)
                nc.vector.tensor_scalar(norm2[:, n, :], norm2[:, n, :], 1e-24, None, ALU.max).then_inc(norms, 1)

            def s_step(u, gb):
                dve.wait_ge(s_mm, gb * 4 + u + 1)
                s3 = bank[2 + u % 2][:, :].rearrange("p (h t) -> p h t", h=GROUP)
                nc.vector.tensor_reduce(smax[:, u, :], s3, AX_X, ALU.max).then_inc(s_max, 1)
                dve.wait_ge(s_max, gb * 4 + u + 1)
                dve.wait_ge(t_mm, gb * 4 + max(0, u - 1))
                nc.vector.tensor_tensor(probs[:, u % 2, :].rearrange("p (h t) -> p h t", h=GROUP), s3,
                                        smax[:, u, :, None].to_broadcast([P, GROUP, SEQ]), ALU.subtract).then_inc(s_sub, 1)

            def v_step(u, gb):
                dve.wait_ge(v_mm, gb * 4 + u + 1)
                o3 = bank[6][:, 0:GROUP * VA].rearrange("p (h d) -> p h d", h=GROUP)
                nc.vector.reciprocal(rsum[:, u, :], o3[:, :, DH]).then_inc(r_sum, 1)
                dve.wait_ge(r_sum, gb * 4 + u + 1)
                dst = outs[:, HPC * (u // 2):HPC * (u // 2 + 1), :].rearrange("p (i e) d -> p i e d", e=2)[:, :, u % 2, :]
                nc.vector.tensor_tensor(dst, o3[:, :, 0:DH], rsum[:, u, :, None].to_broadcast([P, GROUP, DH]),
                                        ALU.mult).then_inc(o_norm, 1)

            def o_step(j, gb, half_):
                dve.wait_ge(o_hi, gb * 2 + j + 1)
                cols = slice(half_ * SEQ, (half_ + 1) * SEQ)
                nc.vector.tensor_tensor(oT[:, 1, 4 * j:4 * j + 4, cols], bank[5][:, :].rearrange("p (c t) -> p c t", c=4),
                                        oT[:, 0, 4 * j:4 * j + 4, cols].bitcast(F32), ALU.subtract).then_inc(o_lo, 1)

            def attend(gb, nxt, half_, b):
                if nxt is not None:
                    x_step(nxt, b + 1)
                for kind, n in BATCH_STEPS:
                    if kind == "A":
                        if nxt is not None:
                            a_step(n, nxt)
                    elif kind == "O":
                        o_step(n, gb, half_)
                    elif kind in "SV":
                        {"S": s_step, "V": v_step}[kind](n, gb)

            def add_attention(gp, b):
                dve.wait_ge(w_mm, gp + 1)
                a0, a1 = X0[:, bass.ds(b, 2), :], X1[:, bass.ds(b, 2), 1:SEQ + 1]
                y = bank[7][:, :].rearrange("p (m b t) -> p m b t", m=KC, b=2)
                nc.vector.tensor_tensor(a0, a0, y[:, 0], ALU.add)
                nc.vector.tensor_tensor(a1, a1, y[:, 1], ALU.add).then_inc(x_added, 1)

            def ln_steps(kind, k, gt, t):
                if kind == "M":
                    dve.wait_ge(mean_mm, gt + 1)
                    nc.vector.tensor_tensor(xc[:, 0, :].rearrange("p (b t) -> p b t", b=4), X0[:, bass.ds(t * 4, 4), :],
                                            bank[6][:, :].rearrange("p (b t) -> p b t", b=4), ALU.subtract)
                    nc.vector.tensor_tensor(xc[:, 1, :].rearrange("p (b t) -> p b t", b=4), X1[:, bass.ds(t * 4, 4), 0:SEQ],
                                            bank[6][:, :].rearrange("p (b t) -> p b t", b=4), ALU.subtract).then_inc(centred, 1)
                elif kind == "R":
                    dve.wait_ge(var_mm, gt + 1)
                    dve.wait_ge(rstd_ok, gt)
                    nc.vector.tensor_scalar(var4, bank[7][:, 0:4], 1e-5, None, ALU.add).then_inc(var_ok, 1)
                elif kind == "N" and k == 0:
                    dve.wait_ge(bc_mm, gt + 1)
                    dve.wait_ge(centred, gt + 1)
                    dve.wait_ge(var_mm, gt + 1)
                    nc.vector.tensor_tensor(xq, xc, bank[6][:, None, :].to_broadcast([P, KC, TOK]), ALU.mult).then_inc(xn_ok, 1)
                elif kind == "N":
                    dve.wait_ge(xg_ok, gt + 1)
                    dve.wait_ge(u_mm, gt * 6)
                    nc.vector.tensor_copy(xn_parts[:, 0], xg).then_inc(xn_hi, 1)
                    dve.wait_ge(xn_hi, gt + 1)
                    nc.vector.tensor_tensor(xn_parts[:, 1], xg, xn_parts[:, 0].bitcast(F32), ALU.subtract).then_inc(xn_lo, 1)

            def u_step(m, gt):
                rows = P if m < FULL else REST
                col = m if m < FULL else 2 * FULL
                dve.wait_ge(gelu_ok, gt * 6 + m + 1)
                dve.wait_ge(h_lo, gt * 6 + max(0, m - 1))
                nc.vector.scalar_tensor_tensor(out=hf[0:rows, m % 2, :], in0=bank[2 * (m % 2)][0:rows, :],
                                               scalar=b1_t[0:rows, col:col + 1], in1=gelu[0:rows, m % 2, :],
                                               op0=ALU.add, op1=ALU.mult).then_inc(h_ok, 1)
                dve.wait_ge(h_hi, gt * 6 + m + 1)
                nc.vector.tensor_tensor(h_parts[0:rows, m % 2, 1, :], hf[0:rows, m % 2, :],
                                        h_parts[0:rows, m % 2, 0, :].bitcast(F32), ALU.subtract).then_inc(h_lo, 1)

            def add_ffn(gt, t):
                dve.wait_ge(d_mm, gt * 6 + 6)
                a0, a1 = X0[:, bass.ds(t * 4, 4), :], X1[:, bass.ds(t * 4, 4), 1:SEQ + 1]
                for o, a in enumerate((a0, a1)):
                    ins = nc.vector.scalar_tensor_tensor(out=a, in0=bank[4 + o][:, :].rearrange("p (b t) -> p b t", b=4),
                                                         scalar=b2_t[:, o:o + 1], in1=a, op0=ALU.add, op1=ALU.add)
                ins.then_inc(f_added, 1)

            def feed(gt, nxt, t):
                for kind, n in FFN_STEPS:
                    if kind == "U":
                        u_step(n, gt)
                    elif kind == "D":
                        if n == FULL:
                            add_ffn(gt, t)
                    elif nxt is not None:
                        ln_steps(kind, n, nxt, t + 1)

            low_parts(dve, list(attn_pieces(0)), 0, 0)
            with dve.Fori(0, DEPTH) as layer:
                dve.wait_ge(vec_in, (layer + 1) * VECTORS * 16)
                for a in range(2):
                    nc.vector.tensor_tensor(rope_q[:, a, 0, :], rope_t[:, 2 * a, :], qk_scale[:, a, :], ALU.mult)
                    for lo, hi in ((0, HALF), (HALF, 0)):
                        ins = nc.vector.tensor_tensor(rope_q[:, a, 1, lo:lo + HALF], rope_t[:, 2 * a + 1, lo:lo + HALF],
                                                      qk_scale[:, a, hi:hi + HALF], ALU.mult)
                ins.then_inc(tables, 1)
                dve.wait_ge(tables, layer + 1)
                x_step(layer * BATCH, 0)
                for kind, n in FIRST_STEPS:
                    if kind == "A":
                        a_step(n, layer * BATCH)
                low_parts(dve, list(ffn_pieces(0)), layer, 1)
                with dve.Fori(0, BATCH // 2 - 1) as pair:
                    gb = layer * BATCH + pair * 2
                    attend(gb, gb + 1, 0, pair * 2)
                    attend(gb + 1, gb + 2, 1, pair * 2 + 1)
                    add_attention(layer * (BATCH // 2) + pair, pair * 2)
                gb = layer * BATCH + BATCH - 2
                attend(gb, gb + 1, 0, BATCH - 2)
                attend(gb + 1, None, 1, BATCH - 1)
                add_attention(layer * (BATCH // 2) + BATCH // 2 - 1, BATCH - 2)
                barrier(dve, layer * 2 + 1)
                for kind, n in FFN_STEPS:
                    if kind in "MRN":
                        ln_steps(kind, n, layer * 4, 0)
                low_parts(dve, list(attn_pieces(0)), layer + 1, 0)
                with dve.Fori(0, 3) as t:
                    feed(layer * 4 + t, layer * 4 + t + 1, t)
                feed(layer * 4 + 3, None, 3)
                barrier(dve, layer * 2 + 2)
                nc.vector.memset(vals[:, :, DH:VA], 1.0).then_inc(v_ones, 1)
            with dve.Fori(0, BATCH) as b:
                dve.wait_ge(fin_mm, b)
                nc.vector.tensor_copy(xoT[:, 0, :], X0[:, bass.ds(b, 1), :])
                nc.vector.tensor_copy(xoT[:, 1, :], X1[:, bass.ds(b, 1), 1:SEQ + 1]).then_inc(fin_copied, 1)
                dve.wait_ge(fin_mm, b + 1)
                dve.wait_ge(fin_in, b * 16 + 16)
                dve.wait_ge(fin_out, b * 16)
                nc.vector.scalar_tensor_tensor(out=x1, in0=bank[0][:, 0:DIM], scalar=gates[:, 3:4], in1=xin, op0=ALU.mult,
                                               op1=ALU.add).then_inc(fin_ok, 1)

        @block.gpsimd
        def _(pool):
            nc.gpsimd.memset(half[:, :], -0.5).then_inc(half_ok, 1)
            pool.wait_ge(half_ok, 1)
            with pool.Fori(0, BATCH) as b:
                for k in range(2):
                    pool.wait_ge(xvar_ready, b * 2 + k + 1)
                    pool.wait_ge(xn_made, b * 2 + k)
                    nc.gpsimd.tensor_tensor(xr[:, 0:1], mv[:, 1:2], half[:, 0:1], ALU.pow).then_inc(xrstd, 1)
            barrier(pool, 0)

            def a_step(c, gb):
                if c in V_CHUNKS:
                    return
                n = QK_CHUNKS.index(c)
                pool.wait_ge(rotated, gb * 4 + n + 1)
                pool.wait_ge(b_mm, gb * 4 + max(0, n - 1))
                nc.gpsimd.tensor_tensor(qkr[:, n % 2, :], m1[:, n % 2, :], m2[:, n % 2, :], ALU.add).then_inc(rope_sum, 1)
                pool.wait_ge(norms, gb * 4 + n + 1)
                pool.wait_ge(qk_ready, gb * 4 + n)
                nc.gpsimd.tensor_tensor(rnorm[:, n, :], norm2[:, n, :], half[:, 0:HPC], ALU.pow).then_inc(rnorms, 1)
                pool.wait_ge(rnorms, gb * 4 + n + 1)
                pool.wait_ge(rope_sum, gb * 4 + n + 1)
                q3 = qkr[:, n % 2, :].rearrange("p (h d) -> p h d", h=HPC)
                nc.gpsimd.tensor_tensor(q3, q3, rnorm[:, n, :, None].to_broadcast([P, HPC, DH]), ALU.mult).then_inc(qk_ready, 1)

            with pool.Fori(0, DEPTH) as layer:
                with pool.Fori(0, BATCH) as b:
                    for c in range(6):
                        a_step(c, layer * BATCH + b)
                barrier(pool, layer * 2 + 1)
                for t in range(4):
                    gt = layer * 4 + t
                    pool.wait_ge(var_ok, gt + 1)
                    pool.wait_ge(bc_mm, gt)
                    nc.gpsimd.tensor_tensor(rstd4, var4, half[:, 0:4], ALU.pow).then_inc(rstd_ok, 1)
                barrier(pool, layer * 2 + 2)


_INS = ['x', 'ctx_1024', 'mask_BxSxS2_bf0', 'g_xattn', 'g_ffn', 'L0_xattn_Wq', 'L0_xattn_bq', 'L0_xattn_Wk',
        'L0_xattn_bk', 'L0_xattn_Wv', 'L0_xattn_bv', 'L0_xattn_Wo', 'L0_xattn_bo', 'L0_ffn_Wqkv', 'L0_ffn_q_scale',
        'L0_ffn_k_scale', 'L0_ffn_Wo', 'L0_ffn_ln_g', 'L0_ffn_ln_b', 'L0_ffn_W1', 'L0_ffn_b1', 'L0_ffn_W2', 'L0_ffn_b2']


def shape_constants():
    f = np.float32
    half = np.arange(0, DH, 2, dtype=f)
    freqs = np.arange(SEQ, dtype=f)[:, None] * (f(1.0) / f(10000.0) ** (half / f(DH)))[None, :]
    power = (np.arange(SEQ, dtype=f) - f(SEQ // 2)) / f(WINDOW // 2)
    scale = ((half + f(0.4 * DH)) / f(1.4 * DH))[None, :] ** power[:, None]
    cos, sin = np.cos(freqs), np.sin(freqs)
    signed = lambda a: np.concatenate([-a, a], -1)
    twice = lambda a: np.concatenate([a, a], -1)
    rope = np.stack([twice(cos * scale), signed(sin * scale), twice(cos / scale), signed(sin / scale)], 1).astype(f)
    i, j = np.arange(SEQ)[:, None], np.arange(SEQ)[None, :]
    band = np.where((i < j) | (i > j + WINDOW), f(NEG_MASK), f(0)).astype(f)
    return {"rope": rope, "band": band, "eye": np.eye(P, dtype=f)}


def kernel(**inputs):
    import concourse.bacc as _bacc
    from concourse.bass_utils import run_bass_kernel_spmd as _run

    nc = _bacc.Bacc("TRN2", target_bir_lowering=False, num_devices=1)
    arrays, args = {}, []
    given = [(n, inputs[n]) for n in _INS] + list(shape_constants().items())
    for name, a in given:
        a = np.ascontiguousarray(a)
        arrays[f"in_{name}_dram"] = a
        args.append(nc.dram_tensor(f"in_{name}_dram", a.shape, mybir.dt.from_np(a.dtype), kind="ExternalInput").ap())
    args.append(nc.dram_tensor("out_0_dram", (BATCH, SEQ, DIM), F32, kind="ExternalOutput").ap())
    build(nc, *args)
    r = _run(nc, [arrays], core_ids=[0])
    return r.results[0]["out_0_dram"]
```

```python
from contextlib import ExitStack

import numpy as np

import concourse.bass as bass
from concourse import mybir

P = 128
ALU = mybir.AluOpType
ACT = mybir.ActivationFunctionType
F32 = mybir.dt.float32
F32R = mybir.dt.float32r
BF16 = mybir.dt.bfloat16
U8 = mybir.dt.uint8
AX_X = mybir.AxisListType.X

BATCH, SEQ, DIM = 16, 128, 256
KC = DIM // P
XH, XD = 16, 16
XPAD = 32
DEPTH, HEADS, DH = 6, 16, 64
WINDOW = 64
INNER = HEADS * DH
OC = INNER // P
FF = DIM * 4 * 2 // 3
FULL = FF // P
REST = FF - FULL * P
GATE0 = 64
HALF = DH // 2
CH = 512
HPC = CH // DH
GROUP = 4
TOK = 4 * SEQ
VA = DH + 1
XVA = XD + 1
NEG_MASK = -1e30
NEG_INF = -1e18

XW_LOADS = 16
XPERIOD = ["S0", "S1", "L0", "E0", "T0", "V0", "L1", "E1", "T1", "S2", "V1", "N0", "I0", "S3", "T2", "V2", "P0",
           "K0", "N1", "T3", "Q0", "V3", "E2"]
VECTORS = 9

PERIOD = ["S0", "O", "S1", "Q", "B0", "T0", "K", "B1", "V0", "W0", "T1", "C", "V1", "W1", "X"]
ACT_PERIOD = ["O", "S0", "Q", "S1", "B0", "T0", "K", "T1", "B1", "C"]
UNITS = 2 * BATCH
FFN_STEPS = [("U", 0), ("U", 1), ("D", 0), ("U", 2), ("M", 0), ("D", 1), ("U", 3), ("R", 0), ("D", 2),
             ("U", 4), ("N", 0), ("D", 3), ("U", 5), ("D", 4), ("D", 5), ("N", 1)]


def build(nc, x, ctx_1024, mask, g_xattn, g_ffn, Wq, bq, Wk, bk, Wv, bv, Wo, bo,
          Wqkv, q_scale, k_scale, Wout, ln_g, ln_b, W1, b1, W2, b2, rope, band, eye, out):
    with ExitStack() as stack:
        def sb(name, shape, dt=F32):
            return stack.enter_context(nc.sbuf_tensor(name, shape, dt))

        def sem(name):
            return stack.enter_context(nc.semaphore(name))

        bank = [stack.enter_context(nc.psum_tensor(f"bank{i}", [P, CH], F32)) for i in range(8)]

        X0 = sb("X0", [P, BATCH, SEQ])
        X1 = sb("X1", [P, BATCH, SEQ + 1])
        wqkv = sb("wqkv", [P, 2, KC, 3 * INNER], F32R)
        wout = sb("wout", [P, 2, OC, DIM], F32R)
        w1 = sb("w1", [P, 2, KC, 2 * FULL + 1, P], F32R)
        w2 = sb("w2", [P, 2, FULL + 1, DIM], F32R)
        parts = sb("parts", [P, 2 * OC * 2 * SEQ], F32R)
        xs = sb("xs", [P, 2, 2, KC, SEQ], F32R)
        oT = parts[:, :].rearrange("p (s c t) -> p s c t", s=2, c=OC)
        xn_parts = parts[:, 0:2 * KC * TOK].rearrange("p (s c t) -> p s c t", s=2, c=KC)
        h_parts = parts[:, 2 * KC * TOK:].rearrange("p (b s t) -> p b s t", b=2, s=2)
        ident = sb("ident", [P, P])
        ident_bf = sb("ident_bf", [P, P], BF16)
        band_f = sb("band_f", [P, P])
        band_bf = sb("band_bf", [P, P], BF16)
        rope_t = sb("rope_t", [P, 4, DH])
        qk_scale = sb("qk_scale", [P, 2, DH])
        rope_q = sb("rope_q", [P, 2, 2, DH])
        inv_dim = sb("inv_dim", [P, P])
        ones = sb("ones", [P, XH])
        ln_gb = sb("ln_gb", [P, 2, KC])
        b1_t = sb("b1_t", [P, 2 * FULL + 1])
        b2_t = sb("b2_t", [P, KC])
        gates = sb("gates", [P, 4])
        half = sb("half", [P, 16])
        work = sb("work", [P, 15200])

        offset = [0]

        def part(n):
            a = offset[0]
            offset[0] += n
            assert offset[0] <= work.shape[1], offset[0]
            return work[:, a:a + n]

        raw = part(2 * 1024).rearrange("p (b n) -> p b n", b=2)
        after_raw = offset[0]
        m1 = part(2 * CH).rearrange("p (b n) -> p b n", b=2)
        m2 = part(2 * CH).rearrange("p (b n) -> p b n", b=2)
        sq = part(2 * CH).rearrange("p (b n) -> p b n", b=2)
        qkr = part(2 * CH).rearrange("p (b n) -> p b n", b=2)
        probs = part(2 * CH).rearrange("p (b n) -> p b n", b=2)
        probsT = part(2 * CH).rearrange("p (b n) -> p b n", b=2)
        qkT = part(2 * CH).rearrange("p (s n) -> p s n", s=2)
        vals = part(HEADS * VA).rearrange("p (h d) -> p h d", h=HEADS)
        outs = part(INNER).rearrange("p (h d) -> p h d", h=HEADS)
        norm2 = part(4 * HPC).rearrange("p (b n) -> p b n", b=4)
        rnorm = part(4 * HPC).rearrange("p (b n) -> p b n", b=4)
        smax = part(4 * GROUP).rearrange("p (b n) -> p b n", b=4)
        rsum = part(4 * GROUP).rearrange("p (b n) -> p b n", b=4)
        offset[0] = after_raw
        xc = part(KC * TOK).rearrange("p (c t) -> p c t", c=KC)
        xq = part(KC * TOK).rearrange("p (c t) -> p c t", c=KC)
        xg = part(KC * TOK).rearrange("p (c t) -> p c t", c=KC)
        gelu = part(2 * TOK).rearrange("p (b t) -> p b t", b=2)
        hf = part(2 * TOK).rearrange("p (b t) -> p b t", b=2)
        var4 = part(4)
        rstd4 = part(4)
        offset[0] = after_raw
        xwq = part(KC * XH * XPAD).rearrange("p (c h d) -> p c h d", c=KC, h=XH)
        xwk = part(KC * XH * XPAD).rearrange("p (c h d) -> p c h d", c=KC, h=XH)
        xwv = part(KC * DIM).rearrange("p (c n) -> p c n", c=KC)
        xwo = part(KC * DIM).rearrange("p (c n) -> p c n", c=KC)
        bqk = part(2 * 4).rearrange("p (a c) -> p a c", a=2)
        bvo = part(2 * DIM).rearrange("p (a n) -> p a n", a=2)
        def two(n):
            return part(2 * n).rearrange("p (b n) -> p b n", b=2)

        xin, cin, xres, x1 = two(DIM), two(DIM), two(DIM), two(DIM)
        mean1, mean2 = part(2), part(2)
        cent1, cent2 = part(DIM), part(DIM)
        xnorm1, xnorm2 = part(DIM), part(DIM)
        tT = part(2 * KC * SEQ).rearrange("p (a c t) -> p a c t", a=2, c=KC)
        xqk = part(2 * 4 * SEQ).rearrange("p (a c t) -> p a c t", a=2, c=4)
        xv = part(2 * XH * XVA).rearrange("p (b h d) -> p b h d", b=2, h=XH)
        xp, xpT = two(CH), two(CH)
        xo = part(DIM).rearrange("p (h d) -> p h d", h=XH)
        xoT = part(KC * SEQ).rearrange("p (c t) -> p c t", c=KC)
        xmax, xsum = [part(16).rearrange("p (j i) -> p j i", j=4) for _ in range(2)]
        xr1, xr2 = part(1), part(1)
        maskf = sb("maskf", [P, 2, SEQ], BF16)
        mask8 = sb("mask8", [P, 2, SEQ], U8)

        x1_dram = nc.dram_tensor("x_after_xattn", (BATCH, SEQ, DIM), F32, kind="Internal").ap()

        loaded = sem("constants_loaded")
        consts = sem("constants_ready")
        xw_loaded = sem("xattn_weights_loaded")
        x_in = [sem("even_inputs_loaded"), sem("odd_inputs_loaded")]
        x1_out = [sem("even_x1_stored"), sem("odd_x1_stored")]
        phase_done = sem("phase_done")
        consts_act, half_ok, v_ones = sem("constants_made"), sem("exponents_ready"), sem("ones_beside_values")
        link1, link2 = sem("x_norm_links"), sem("x1_norm_links")
        var1, rstd1, norm1_ok = sem("x_variance"), sem("x_rstd"), sem("x_normalised")
        var2, rstd2, norm2_ok = sem("x1_variance"), sem("x1_rstd"), sem("x1_normalised")
        xmax_ok, xsum_ok, res_in = sem("xattn_max"), sem("xattn_sum_inverted"), [sem("even_residual_loaded"), sem("odd_residual_loaded")]
        xnT_mm, xT_copied = sem("inputs_transposed"), sem("inputsT_copied")
        xk_mm, xv_mm, xq_mm, xk_ready, xqk_ready, xv_ready = (sem("xattn_k"), sem("xattn_v"), sem("xattn_q"), sem("xattn_k_ready"),
                                                              sem("xattn_q_ready"), sem("xattn_v_ready"))
        mask_made, xs_mm, xs_sub, xs_exp = sem("mask_made"), sem("xattn_scores"), sem("xattn_minus_max"), sem("xattn_probs")
        xt_mm, xpT_copied, xpv_mm, xo_norm = (sem("xattn_probs_transposed"), sem("xattn_probsT"), sem("xattn_pv"),
                                              sem("xattn_outs"))
        xoT_mm, xoT_copied, xwo_mm = sem("xattn_outs_transposed"), sem("xattn_outsT"), sem("xattn_wo")
        x1_sum, x1_made, x_mm, x_stored = sem("xattn_biased"), sem("x1_made"), sem("x_transposed"), sem("x_stored")
        norm_sum, cleared, fin_copied = sem("norm_sums_ready"), sem("work_cleared"), sem("x_copied_back")

        raw_in = [sem("raw_weights_loaded0"), sem("raw_weights_loaded1")]
        raw_hi = sem("weights_high_part")
        raw_lo = sem("weights_low_part")
        vec_in = sem("layer_vectors_loaded")
        tables = sem("rope_tables_ready")
        xs_hi, xs_ready = sem("xs_high_part"), sem("xs_ready")
        qk_mm, val_mm = sem("qk_chunk_done"), sem("v_chunk_done")
        squared, rotated, v_copied = sem("qk_squared"), sem("qk_rotated"), sem("v_copied")
        norms, rope_sum, rnorms, qk_ready = sem("norms_summed"), sem("rope_summed"), sem("rnorms_ready"), sem("qk_ready")
        b_mm, b_copied = sem("qk_transposed"), sem("qkT_copied")
        s_mm, s_max, s_sub, s_exp = sem("scores_done"), sem("max_ready"), sem("scores_minus_max"), sem("probs_ready")
        t_mm, t_copied = sem("probs_transposed"), sem("probsT_copied")
        v_mm, r_sum, o_norm = sem("pv_done"), sem("sum_inverted"), sem("outs_normalised")
        o_mm, o_hi, o_lo = sem("outs_transposed"), sem("outT_high_part"), sem("outT_low_part")
        w_mm, x_added = sem("wo_done"), sem("attention_added")

        mean_mm, centred, xsq, var_mm, var_ok, rstd_ok = (sem("mean_done"), sem("centred"), sem("centred_squared"),
                                                          sem("variance_done"), sem("variance_ready"), sem("rstd_ready"))
        bc_mm, xn_ok, xg_ok, xn_hi, xn_lo = (sem("rstd_spread"), sem("xn_ready"), sem("xn_affine"), sem("xn_high_part"),
                                             sem("xn_low_part"))
        u_mm, gelu_ok, h_ok, h_hi, h_lo = (sem("up_done"), sem("gelu_ready"), sem("h_ready"), sem("h_high_part"),
                                           sem("h_low_part"))
        d_mm, f_added = sem("down_done"), sem("ffn_added")
        fin_in, fin_mm, fin_ok, fin_out = sem("x1_loaded"), sem("x_back"), sem("out_ready"), sem("out_stored")

        def barrier(eng, phase):
            eng.drain().then_inc(phase_done, 1)
            eng.wait_ge(phase_done, phase * 4 + 4)

        def attn_pieces(layer):
            r = Wqkv[layer].rearrange("(c p) n -> c p n", p=P)
            o = Wout[layer].rearrange("(c p) n -> p c n", p=P)
            for c in range(KC):
                for n in range(0, 3 * INNER, 1024):
                    yield P, r[c, :, n:n + 1024], [(0, 1024, lambda s, c=c, n=n: wqkv[:, s, c, n:n + 1024])]
            for c in range(0, OC, 4):
                yield P, o[:, c:c + 4, :], [(0, 1024, lambda s, c=c: wout[:, s, c:c + 4, :].rearrange("p c n -> p (c n)"))]

        def ffn_pieces(layer):
            r = W1[layer].rearrange("(c p) n -> c p n", p=P)
            d = W2[layer]
            for c in range(KC):
                for a in range(2):
                    g0 = GATE0 if a else 0
                    yield P, r[c, :, a * FF:(a + 1) * FF], [
                        (0, FULL * P, lambda s, c=c, a=a: w1[:, s, c, a * FULL:(a + 1) * FULL, :].rearrange("p m n -> p (m n)")),
                        (FULL * P, FF, lambda s, c=c, g0=g0: w1[:, s, c, 2 * FULL, g0:g0 + REST])]
            full = d[0:FULL * P, :].rearrange("(c p) n -> p c n", p=P)
            for c, n in ((0, 4), (4, 1)):
                yield P, full[:, c:c + n, :], [(0, n * DIM, lambda s, c=c, n=n: w2[:, s, c:c + n, :].rearrange("p c n -> p (c n)"))]
            yield REST, d[FULL * P:FF, :], [(0, DIM, lambda s: w2[0:REST, s, FULL, :])]

        ATTN_N, FFN_N = KC * 3 + OC // 4, KC * 2 + 3
        PIECES = ATTN_N + FFN_N

        def load_pieces(sp, pieces, base):
            for i, (rows, src, _) in enumerate(pieces):
                sp.wait_ge(raw_lo, base + i - 1 if i else base)
                n = 1
                for w in src.shape[1:]:
                    n *= w
                dst = raw[0:rows, i % 2, 0:n]
                if len(src.shape) == 3:
                    dst = dst.rearrange("p (c n) -> p c n", c=src.shape[1])
                sp.dma_start(dst, src).then_inc(raw_in[i % 2], 16)

        def raw_count(layer, kind, i):
            per = [(ATTN_N + 1) // 2 + (FFN_N + 1) // 2, ATTN_N // 2 + FFN_N // 2][i % 2]
            before = 0 if kind == 0 else [(ATTN_N + 1) // 2, ATTN_N // 2][i % 2]
            return (layer * per + (before + i // 2 + 1)) * 16

        def high_parts(act, pieces, layer, kind):
            for i, (rows, _, dests) in enumerate(pieces):
                act.wait_ge(raw_in[i % 2], raw_count(layer, kind, i))
                for k, (a, b, dst) in enumerate(dests):
                    ins = nc.scalar.copy(dst(0), raw[0:rows, i % 2, a:b])
                ins.then_inc(raw_hi, 1)

        def low_parts(dve, pieces, layer, kind):
            base = layer * PIECES + (ATTN_N if kind else 0)
            for i, (rows, _, dests) in enumerate(pieces):
                dve.wait_ge(raw_hi, base + i + 1)
                dve.wait_ge(raw_in[i % 2], raw_count(layer, kind, i))
                for k, (a, b, dst) in enumerate(dests):
                    ins = nc.vector.tensor_tensor(dst(1), raw[0:rows, i % 2, a:b], dst(0).bitcast(F32), ALU.subtract)
                ins.then_inc(raw_lo, 1)

        def three(pe, out_ap, lhs, rhs, first, last):
            pe.matmul(out_ap, lhs(0), rhs(0), start=first, stop=False)
            pe.matmul(out_ap, lhs(0), rhs(1), start=False, stop=False)
            return pe.matmul(out_ap, lhs(1), rhs(0), start=False, stop=last)

        def xperiods(engine, period):
            period(-1, -1, 1)
            period(0, 0, 1)
            with engine.Fori(0, BATCH // 2 - 1) as two_:
                period(1, two_ * 2 + 1, two_ + 2)
                period(2, two_ * 2 + 2, two_ + 2)
            period(BATCH - 1, BATCH - 1, BATCH // 2 + 1)
            period(BATCH, BATCH, BATCH // 2 + 1)

        def in_xperiod(p, kinds):
            here = {**dict.fromkeys("STV", 0 <= p < BATCH), **dict.fromkeys("LIKQP", p + 1 < BATCH),
                    **dict.fromkeys("EN", p >= 1)}
            return [(step[0], int(step[1])) for step in XPERIOD if here[step[0]] and step[0] in kinds]

        def periods(engine, period):
            def run(layer):
                g0 = layer * UNITS
                for u in range(-2, 4):
                    period(u, g0 + u if u >= 0 else g0, layer, 0)
                with engine.Fori(1, BATCH // 2 - 1) as pair:
                    for u in range(4):
                        period(u + 4, g0 + pair * 4 + u, layer, pair)
                for u in range(UNITS - 4, UNITS + 1):
                    period(u, g0 + u, layer, BATCH // 2 - 1)
            return run

        def BATCH_OF(unit, pair):
            if isinstance(pair, int):
                return unit // 2
            return pair * 2 + unit // 2 - 2

        def in_period(u, order=PERIOD):
            here = {"S": 0 <= u < UNITS, "T": 0 <= u < UNITS, "V": 0 <= u < UNITS, "Q": u + 2 < UNITS,
                    "K": u + 2 < UNITS, "B": 0 <= u + 1 < UNITS, "C": 0 <= u + 1 < UNITS, "O": u >= 1,
                    "W": u >= 4 and u % 4 == 0, "X": u % 2 == 1 and u + 3 < UNITS}
            return [(step[0], int(step[1:] or 0)) for step in order if here[step[0]]]

        block = stack.enter_context(nc.Block())

        @block.sync
        def _(sp):
            for dst, src in ((ident, eye), (band_f, band)):
                sp.dma_start(dst[:, :], src).then_inc(loaded, 16)
            sp.dma_start(rope_t[:, :, :], rope).then_inc(loaded, 16)
            sp.dma_start(gates[:, 0:1], g_xattn.rearrange("(o n) -> o n", o=1).to_broadcast([P, 1])).then_inc(loaded, 16)
            sp.dma_start(gates[:, 1:2], g_ffn.rearrange("(o n) -> o n", o=1).to_broadcast([P, 1])).then_inc(loaded, 16)
            sp.wait_ge(consts, 1)
            for dst, src, c in ((xwq, Wq, 0), (xwk, Wk, 0), (xwq, Wq, 1), (xwk, Wk, 1)):
                sp.dma_start(dst[:, c, :, 0:XD], src[c * P:(c + 1) * P, :].rearrange("p (h d) -> p h d", h=XH)).then_inc(xw_loaded, 16)
            sp.dma_start(xwv, Wv.rearrange("(c p) n -> p c n", p=P)).then_inc(xw_loaded, 16)
            sp.dma_start(xwo, Wo.rearrange("(c p) n -> p c n", p=P)).then_inc(xw_loaded, 16)
            for a, b in ((0, bq), (1, bk)):
                for j in range(4):
                    sp.dma_start(bqk[32 * j:32 * j + XD, a, :], b.rearrange("(c j d) -> j d c", j=4, d=XD)[j],
                                 allow_slow_non_contiguous=True).then_inc(xw_loaded, 16)
            for a, b in ((0, bv), (1, bo)):
                sp.dma_start(bvo[:, a, :], b.rearrange("(o n) -> o n", o=1).to_broadcast([P, DIM])).then_inc(xw_loaded, 16)
            def load_inputs(b, par):
                sp.dma_start(xin[:, par, :], x[b]).then_inc(x_in[par], 16)
                sp.dma_start(cin[:, par, :], ctx_1024[b]).then_inc(x_in[par], 16)
                sp.dma_start(mask8[:, par, :], mask[b]).then_inc(x_in[par], 16)

            for b in range(2):
                load_inputs(b, b)
                sp.dma_start(xres[:, b, :], x[b]).then_inc(res_in[b], 16)
            with sp.Fori(0, BATCH // 2 - 1) as two_:
                for par in range(2):
                    b = two_ * 2 + par
                    sp.wait_ge(norm1_ok, b + 1)
                    sp.wait_ge(xnT_mm, b + 1)
                    sp.wait_ge(mask_made, b + 1)
                    load_inputs(b + 2, par)
                    sp.wait_ge(x1_made, b + 1)
                    sp.dma_start(xres[:, par, :], x[b + 2]).then_inc(res_in[par], 16)
                    sp.dma_start(x1_dram[b], x1[:, par, :]).then_inc(x1_out[par], 16)
            for par in range(2):
                sp.wait_ge(x1_made, BATCH - 1 + par)
                sp.dma_start(x1_dram[BATCH - 2 + par], x1[:, par, :]).then_inc(x1_out[par], 16)
            for par in range(2):
                sp.wait_ge(x1_out[par], BATCH * 8)
            load_pieces(sp, list(attn_pieces(0)), 0)
            with sp.Fori(0, DEPTH) as layer:
                after = sp.snap((layer + 1) % DEPTH)
                ffn_base = sp.snap(layer * PIECES + ATTN_N)
                attn_base = sp.snap(layer * PIECES + PIECES)
                sp.wait_ge(phase_done, layer * 8 + 4)
                sp.dma_start(qk_scale[:, 0, :], q_scale[bass.ds(layer, 1), :].to_broadcast([P, DH])).then_inc(vec_in, 16)
                sp.dma_start(qk_scale[:, 1, :], k_scale[bass.ds(layer, 1), :].to_broadcast([P, DH])).then_inc(vec_in, 16)
                for a, b in ((0, ln_g), (1, ln_b)):
                    sp.dma_start(ln_gb[:, a, :], b[layer].rearrange("(c p) -> p c", p=P), allow_slow_non_contiguous=True).then_inc(vec_in, 16)
                sp.dma_start(b2_t[:, :], b2[layer].rearrange("(c p) -> p c", p=P), allow_slow_non_contiguous=True).then_inc(vec_in, 16)
                for a in range(2):
                    v = b1[layer][a * FF:(a + 1) * FF]
                    sp.dma_start(b1_t[:, a * FULL:(a + 1) * FULL], v[0:FULL * P].rearrange("(c p) -> p c", p=P),
                                 allow_slow_non_contiguous=True).then_inc(vec_in, 16)
                    sp.dma_start(b1_t[a * GATE0:a * GATE0 + REST, 2 * FULL:2 * FULL + 1],
                                 v[FULL * P:FF].rearrange("(p o) -> p o", o=1), allow_slow_non_contiguous=True).then_inc(vec_in, 16)
                load_pieces(sp, list(ffn_pieces(layer)), ffn_base)
                load_pieces(sp, list(attn_pieces(after)), attn_base)
            sp.wait_ge(phase_done, DEPTH * 8 + 4)
            with sp.Fori(0, BATCH) as b:
                sp.wait_ge(fin_ok, b)
                sp.dma_start(xin[:, 0, :], x1_dram[b]).then_inc(fin_in, 16)
                sp.wait_ge(fin_ok, b + 1)
                sp.dma_start(out[b], x1[:, 0, :]).then_inc(fin_out, 16)
            sp.wait_ge(fin_out, BATCH * 16)

        @block.tensor
        def _(pe):
            pe.wait_ge(consts, 1)
            pe.wait_ge(consts_act, 1)
            pe.wait_ge(xw_loaded, XW_LOADS * 16)
            pe.wait_ge(loaded, 80)
            def xperiod(p, b, n):
                par, nxt = p % 2, 1 - p % 2
                for kind, j in in_xperiod(p, "STVIKQPE"):
                    if kind == "S":
                        if j == 0:
                            pe.wait_ge(mask_made, b + 1)
                            pe.wait_ge(xqk_ready, b + 1)
                            pe.wait_ge(xk_ready, b + 1)
                        pe.wait_ge(xs_sub, b * 4 + max(0, j - 1))
                        pe.matmul(bank[2 + j % 2][:, :], ident_bf[:, :], maskf[:, par, None, :].to_broadcast([P, GROUP, SEQ]),
                                  start=True, stop=True)
                        for i in range(GROUP):
                            r = slice(XPAD * j, XPAD * j + XD)
                            ins = pe.matmul(bank[2 + j % 2][:, i * P:(i + 1) * P], xqk[r, 0, i, :], xqk[r, 1, i, :],
                                            start=False, stop=True, skip_group_check=True)
                        ins.then_inc(xs_mm, 1)
                    elif kind == "T":
                        pe.wait_ge(xs_exp, b * 4 + j + 1)
                        pe.wait_ge(xpT_copied, b * 4 + j)
                        for i in range(GROUP):
                            ins = pe.transpose(bank[4][:, i * P:(i + 1) * P], xp[:, j % 2, i * P:(i + 1) * P], ident[:, :])
                        ins.then_inc(xt_mm, 1)
                    elif kind == "V":
                        if j == 0:
                            pe.wait_ge(xv_ready, b + 1)
                        pe.wait_ge(xpT_copied, b * 4 + j + 1)
                        pe.wait_ge(xo_norm, b * 4 + j)
                        for i in range(GROUP):
                            ins = pe.matmul(bank[5][:, i * XVA:(i + 1) * XVA], xpT[:, j % 2, i * P:(i + 1) * P],
                                            xv[:, par, 4 * i + j, :], start=True, stop=True)
                        ins.then_inc(xpv_mm, 1)
                    elif kind == "I":
                        pe.wait_ge(norm1_ok, b + 2)
                        pe.wait_ge(x_in[nxt], n * 48)
                        pe.wait_ge(xT_copied, b + 1)
                        for a, src in ((0, cin[:, nxt, :]), (1, xnorm1)):
                            for c in range(KC):
                                k = 2 * a + c
                                ins = pe.transpose(bank[0][:, k * P:(k + 1) * P], src[:, c * P:(c + 1) * P], ident[:, :])
                        ins.then_inc(xnT_mm, 1)
                    elif kind in "KQ":
                        a, w, done = (0, xwk, xk_mm) if kind == "K" else (1, xwq, xq_mm)
                        if kind == "K":
                            pe.wait_ge(xT_copied, b + 2)
                            pe.wait_ge(xqk_ready, b + 1)
                        else:
                            pe.wait_ge(xk_ready, b + 2)
                        for h in range(4):
                            for c in range(KC):
                                ins = pe.matmul(bank[1][:, h * P:(h + 1) * P], w[:, c, 4 * h:4 * h + 4, :], tT[:, a, c, :],
                                                start=(c == 0), stop=(c == KC - 1))
                        ins.then_inc(done, 1)
                    elif kind == "P":
                        pe.wait_ge(xT_copied, b + 2)
                        if p >= 1:
                            pe.wait_ge(x1_made, b)
                        for c in range(KC):
                            ins = pe.matmul(bank[6][:, 0:DIM], tT[:, 0, c, :], xwv[:, c, :], start=(c == 0), stop=(c == KC - 1))
                        ins.then_inc(xv_mm, 1)
                    elif j == 0:
                        pe.wait_ge(xo_norm, b * 4)
                        pe.wait_ge(x_stored, b - 1)
                        for c in range(KC):
                            ins = pe.transpose(bank[7][:, c * P:(c + 1) * P], xo[:, 8 * c:8 * c + 8, :], ident[:, :])
                        ins.then_inc(xoT_mm, 1)
                    elif j == 1:
                        pe.wait_ge(xoT_copied, b)
                        pe.wait_ge(xv_ready, b + 1 if p < BATCH else b)
                        for c in range(KC):
                            ins = pe.matmul(bank[6][:, 0:DIM], xoT[:, c, :], xwo[:, c, :], start=(c == 0), stop=(c == KC - 1))
                        ins.then_inc(xwo_mm, 1)
                    else:
                        pe.wait_ge(norm2_ok, b)
                        for c in range(KC):
                            ins = pe.transpose(bank[7][:, c * P:(c + 1) * P], xnorm2[:, c * P:(c + 1) * P], ident[:, :])
                        ins.then_inc(x_mm, 1)

            xperiods(pe, xperiod)
            barrier(pe, 0)

            def chunk(bank_out, par, col):
                for k in range(KC):
                    ins = three(pe, bank_out, lambda s: xs[:, par, s, k, :], lambda s: wqkv[:, s, k, col:col + CH],
                                k == 0, k == KC - 1)
                return ins

            def period(u, g, layer, pair):
                odd = u % 2
                for kind, e in in_period(u):
                    if kind == "S":
                        pe.wait_ge(b_copied, g * 2 + 2)
                        pe.wait_ge(s_sub, g * 2)
                        b = bank[2 + e]
                        pe.matmul(b[:, :], ident_bf[:, :], band_bf[:, None, :].to_broadcast([P, GROUP, SEQ]),
                                  start=True, stop=True)
                        r = slice(DH * e, DH * e + DH)
                        for i in range(GROUP):
                            cols = slice(i * P, (i + 1) * P)
                            ins = pe.matmul(b[:, cols], qkT[r, 0, cols], qkT[r, 1, cols], start=False, stop=True,
                                            skip_group_check=True)
                        ins.then_inc(s_mm, 1)
                    elif kind in "QK":
                        n = "QK".index(kind)
                        if u == -2:
                            if n == 0:
                                pe.wait_ge(xs_ready, layer * BATCH + 1)
                            nxt = g
                        else:
                            nxt = g + 2 if u >= 0 else g + 1
                            if n == 0:
                                pe.wait_ge(xs_ready, layer * BATCH + BATCH_OF(u + 2, pair) + 1)
                                pe.wait_ge(rotated, nxt * 2)
                            else:
                                pe.wait_ge(v_copied, nxt - 1)
                        chunk(bank[(3 * u + n) % 2][:, :], ((u + 2) // 2) % 2, n * INNER + odd * CH).then_inc(qk_mm, 1)
                    elif kind == "C":
                        nxt = g + 1 if u >= 0 else g
                        pe.wait_ge(rotated, nxt * 2 + (3 if u + 2 < UNITS else 2))
                        chunk(bank[3 * u % 2][:, :], ((u + 1) // 2) % 2, 2 * INNER + (1 - odd) * CH).then_inc(val_mm, 1)
                    elif kind == "B":
                        nxt = g + 1 if u >= 0 else g
                        pe.wait_ge(qk_ready, nxt * 2 + e + 1)
                        pe.wait_ge(b_copied, nxt * 2 + e)
                        for j in range(4):
                            ins = pe.transpose(bank[4][:, j * P:(j + 1) * P], qkr[:, e, j * P:(j + 1) * P], ident[:, :])
                        ins.then_inc(b_mm, 1)
                    elif kind == "O":
                        pe.wait_ge(o_norm, g * 2)
                        pe.wait_ge(t_copied, g * 2)
                        for i in range(4):
                            h = HPC * (1 - odd) + 2 * i
                            ins = pe.transpose(bank[5][:, i * P:(i + 1) * P], outs[:, h:h + 2, :], ident[:, :])
                        ins.then_inc(o_mm, 1)
                    elif kind == "T":
                        pe.wait_ge(s_exp, g * 2 + e + 1)
                        if e == 0:
                            pe.wait_ge(o_lo, g)
                        else:
                            pe.wait_ge(t_copied, g * 2 + 1)
                        for i in range(GROUP):
                            ins = pe.transpose(bank[5][:, i * P:(i + 1) * P], probs[:, e, i * P:(i + 1) * P], ident[:, :])
                        ins.then_inc(t_mm, 1)
                    elif kind == "V":
                        pe.wait_ge(t_copied, g * 2 + e + 1)
                        pe.wait_ge(v_copied, g + 1)
                        pe.wait_ge(o_norm, g * 2 + e)
                        for i in range(GROUP):
                            ins = pe.matmul(bank[6][:, i * VA:(i + 1) * VA], probsT[:, e, i * P:(i + 1) * P],
                                            vals[:, HPC * odd + 2 * i + e, :], start=True, stop=True)
                        ins.then_inc(v_mm, 1)
                    elif kind == "W":
                        gp = layer * (BATCH // 2) + (pair - 1 if u < UNITS else pair)
                        if e == 0:
                            pe.wait_ge(o_lo, gp * 4 + 4)
                            pe.wait_ge(x_added, gp)
                        for c in range(OC):
                            ins = three(pe, bank[7][:, e * 2 * SEQ:(e + 1) * 2 * SEQ], lambda s: wout[:, s, c, e * P:(e + 1) * P],
                                        lambda s: oT[:, s, c, :], c == 0, c == OC - 1)
                        ins.then_inc(w_mm, 1)

            run_periods = periods(pe, period)

            def m_step(k, gt, t):
                pe.wait_ge(xn_ok, gt)
                pe.matmul(bank[6][:, :], inv_dim[:, :], X0[:, bass.ds(t * 4, 4), :], start=True, stop=False)
                pe.matmul(bank[6][:, :], inv_dim[:, :], X1[:, bass.ds(t * 4, 4), 0:SEQ], start=False, stop=True).then_inc(mean_mm, 1)

            def r_step(k, gt, t):
                pe.wait_ge(xsq, gt + 1)
                pe.wait_ge(var_ok, gt)
                for j in range(4):
                    for c in range(KC):
                        ins = pe.matmul(bank[7][:, j:j + 1], xq[:, c, j * P:(j + 1) * P], inv_dim[:, 0:1],
                                        start=(c == 0), stop=(c == KC - 1))
                ins.then_inc(var_mm, 1)

            def n_step(k, gt, t):
                if k:
                    return
                pe.wait_ge(rstd_ok, gt + 1)
                pe.wait_ge(centred, gt + 1)
                for j in range(4):
                    ins = pe.matmul(bank[6][:, j * P:(j + 1) * P], rstd4[:, j:j + 1].to_broadcast([P, P]), ident[:, :],
                                    start=True, stop=True)
                ins.then_inc(bc_mm, 1)

            def u_step(m, gt):
                if m == 0:
                    pe.wait_ge(xn_lo, gt + 1)
                pe.wait_ge(h_ok, gt * 6 + max(0, m - 1))
                for a in range(2 if m < FULL else 1):
                    rows = P if m < FULL else GATE0 + REST
                    for c in range(KC):
                        ins = three(pe, bank[2 * (m % 2) + a][0:rows, :], lambda s: w1[:, s, c, a * FULL + m if m < FULL else 2 * FULL, 0:rows],
                                    lambda s: xn_parts[:, s, c, :], c == 0, c == KC - 1)
                ins.then_inc(u_mm, 1)

            def d_step(m, gt):
                pe.wait_ge(h_lo, gt * 6 + m + 1)
                if m == 0:
                    pe.wait_ge(f_added, gt)
                rows = P if m < FULL else REST
                for o in range(KC):
                    ins = three(pe, bank[4 + o][:, :], lambda s: w2[0:rows, s, m, o * P:(o + 1) * P],
                                lambda s: h_parts[0:rows, m % 2, s, :], m == 0, m == FULL)
                ins.then_inc(d_mm, 1)

            def feed(gt, nxt, t):
                for kind, n in FFN_STEPS:
                    if kind in "UD":
                        {"U": u_step, "D": d_step}[kind](n, gt)
                    elif nxt is not None:
                        {"M": m_step, "R": r_step, "N": n_step}[kind](n, nxt, t + 1)

            with pe.Fori(0, DEPTH) as layer:
                pe.wait_ge(raw_lo, layer * PIECES + ATTN_N)
                run_periods(layer)
                barrier(pe, layer * 2 + 1)
                pe.wait_ge(raw_lo, layer * PIECES + PIECES)
                for kind, n in FFN_STEPS:
                    if kind in "MRN":
                        {"M": m_step, "R": r_step, "N": n_step}[kind](n, layer * 4, 0)
                with pe.Fori(0, 3) as t:
                    feed(layer * 4 + t, layer * 4 + t + 1, t)
                feed(layer * 4 + 3, None, 3)
                barrier(pe, layer * 2 + 2)
            with pe.Fori(0, BATCH) as b:
                pe.wait_ge(fin_copied, b + 1)
                for c in range(KC):
                    ins = pe.transpose(bank[0][:, c * P:(c + 1) * P], xoT[:, c, :], ident[:, :])
                ins.then_inc(fin_mm, 1)

        @block.scalar
        def _(act):
            act.wait_ge(loaded, 80)
            nc.scalar.copy(ident_bf[:, :], ident[:, :])
            nc.scalar.activation(gates[:, 2:4], gates[:, 0:2], ACT.Tanh)
            nc.scalar.copy(band_bf[:, :], band_f[:, :]).then_inc(consts_act, 1)
            act.wait_ge(xw_loaded, XW_LOADS * 16)
            act.wait_ge(consts, 1)
            def xperiod(p, b, n):
                for kind, j in in_xperiod(p, "STIKQE"):
                    if kind == "S":
                        act.wait_ge(xs_sub, b * 4 + j + 1)
                        nc.scalar.activation(xp[:, j % 2, :], xp[:, j % 2, :], ACT.Exp, scale=XD ** -0.5).then_inc(xs_exp, 1)
                    elif kind == "T":
                        act.wait_ge(xt_mm, b * 4 + j + 1)
                        act.wait_ge(xpv_mm, b * 4 + max(0, j - 1))
                        nc.scalar.copy(xpT[:, j % 2, :], bank[4][:, :]).then_inc(xpT_copied, 1)
                    elif kind == "I":
                        act.wait_ge(xnT_mm, b + 2)
                        act.wait_ge(xq_mm, b + 1)
                        nc.scalar.copy(tT[:, :, :, :], bank[0][:, :]).then_inc(xT_copied, 1)
                    elif kind in "KQ":
                        a, done, ready = (1, xk_mm, xk_ready) if kind == "K" else (0, xq_mm, xqk_ready)
                        act.wait_ge(done, b + 2)
                        if p >= 0:
                            act.wait_ge(xs_mm, b * 4 + 4)
                        for i in range(4):
                            ins = nc.scalar.activation(xqk[:, a, i, :], bank[1][:, i * P:(i + 1) * P], ACT.Identity,
                                                       bias=bqk[:, a, i:i + 1])
                        ins.then_inc(ready, 1)
                    elif j == 0:
                        act.wait_ge(xoT_mm, b)
                        act.wait_ge(xwo_mm, b - 1)
                        nc.scalar.copy(xoT[:, :, :], bank[7][:, 0:DIM]).then_inc(xoT_copied, 1)

            xperiods(act, xperiod)
            barrier(act, 0)

            def period(u, g, layer, pair):
                for kind, e in in_period(u, ACT_PERIOD):
                    if kind == "S":
                        act.wait_ge(s_sub, g * 2 + e + 1)
                        nc.scalar.activation(probs[:, e, :], probs[:, e, :], ACT.Exp, scale=8.0).then_inc(s_exp, 1)
                    elif kind in "QK":
                        n = "QK".index(kind)
                        nxt = g if u == -2 else g + 2 if u >= 0 else g + 1
                        act.wait_ge(qk_mm, nxt * 2 + n + 1)
                        if u > -2:
                            act.wait_ge(norms, nxt * 2 - 1 + n)
                        nc.scalar.square(sq[:, n, :], bank[(3 * u + n) % 2][:, :]).then_inc(squared, 1)
                    elif kind == "C":
                        nxt = g + 1 if u >= 0 else g
                        act.wait_ge(val_mm, nxt + 1)
                        if u > -1:
                            act.wait_ge(v_mm, nxt * 2 - 2)
                        h = HPC * ((u + 1) % 2)
                        nc.scalar.copy(vals[:, h:h + HPC, 0:DH],
                                       bank[3 * u % 2][:, :].rearrange("p (h d) -> p h d", h=HPC)).then_inc(v_copied, 1)
                    elif kind == "B":
                        nxt = g + 1 if u >= 0 else g
                        act.wait_ge(b_mm, nxt * 2 + e + 1)
                        act.wait_ge(s_mm, nxt * 2)
                        nc.scalar.copy(qkT[:, e, :], bank[4][:, :]).then_inc(b_copied, 1)
                    elif kind == "O":
                        act.wait_ge(o_mm, g)
                        if u % 4 == 1:
                            act.wait_ge(w_mm, (layer * (BATCH // 2) + pair) * 2)
                        k, half_ = (u - 1) % 2, (u - 1) // 2 % 2
                        nc.scalar.copy(oT[:, 0, 4 * k:4 * k + 4, half_ * SEQ:(half_ + 1) * SEQ],
                                       bank[5][:, :].rearrange("p (c t) -> p c t", c=4)).then_inc(o_hi, 1)
                    elif kind == "T":
                        act.wait_ge(t_mm, g * 2 + e + 1)
                        act.wait_ge(v_mm, g * 2)
                        nc.scalar.copy(probsT[:, e, :], bank[5][:, :]).then_inc(t_copied, 1)

            run_periods = periods(act, period)

            def ln_steps(kind, k, gt):
                if kind == "M":
                    act.wait_ge(centred, gt + 1)
                    act.wait_ge(var_mm, gt)
                    nc.scalar.square(xq[:, :, :], xc[:, :, :]).then_inc(xsq, 1)
                elif kind == "N" and k == 1:
                    act.wait_ge(xn_ok, gt + 1)
                    act.wait_ge(xn_lo, gt)
                    for c in range(KC):
                        ins = nc.scalar.activation(xg[:, c, :], xq[:, c, :], ACT.Identity, bias=ln_gb[:, 1, c:c + 1],
                                                   scale=ln_gb[:, 0, c:c + 1])
                    ins.then_inc(xg_ok, 1)

            def u_step(m, gt):
                act.wait_ge(u_mm, gt * 6 + m + 1)
                act.wait_ge(h_ok, gt * 6 + max(0, m - 1))
                if m < FULL:
                    ins = nc.scalar.activation(gelu[:, m % 2, :], bank[2 * (m % 2) + 1][:, :], ACT.Gelu,
                                               bias=b1_t[:, FULL + m:FULL + m + 1])
                else:
                    r = slice(GATE0, GATE0 + REST)
                    ins = nc.scalar.activation(gelu[0:REST, m % 2, :], bank[2 * (m % 2)][r, :], ACT.Gelu,
                                               bias=b1_t[r, 2 * FULL:2 * FULL + 1])
                ins.then_inc(gelu_ok, 1)

            def h_high(m, gt):
                rows = P if m < FULL else REST
                act.wait_ge(h_ok, gt * 6 + m + 1)
                act.wait_ge(d_mm, gt * 6 + max(0, m - 1))
                nc.scalar.copy(h_parts[0:rows, m % 2, 0, :], hf[0:rows, m % 2, :]).then_inc(h_hi, 1)

            def feed(gt, nxt):
                for kind, n in FFN_STEPS:
                    if kind == "U":
                        u_step(n, gt)
                        h_high(n, gt)
                    elif kind != "D" and nxt is not None:
                        ln_steps(kind, n, nxt)

            high_parts(act, list(attn_pieces(0)), 0, 0)
            with act.Fori(0, DEPTH) as layer:
                high_parts(act, list(ffn_pieces(0)), layer, 1)
                run_periods(layer)
                barrier(act, layer * 2 + 1)
                act.wait_ge(vec_in, (layer + 1) * VECTORS * 16)
                for kind, n in FFN_STEPS:
                    if kind in "MRN":
                        ln_steps(kind, n, layer * 4)
                high_parts(act, list(attn_pieces(0)), layer + 1, 0)
                with act.Fori(0, 3) as t:
                    feed(layer * 4 + t, layer * 4 + t + 1)
                feed(layer * 4 + 3, None)
                barrier(act, layer * 2 + 2)

        @block.vector
        def _(dve):
            nc.vector.memset(work[:, :], 0.0).then_inc(cleared, 1)
            dve.wait_ge(cleared, 1)
            nc.vector.memset(inv_dim[:, :], 1.0 / DIM)
            nc.vector.memset(X1[:, :, 0:1], 0.0)
            nc.vector.memset(b1_t[:, :], 0.0)
            nc.vector.memset(w1[:, :, :, 2 * FULL, REST:GATE0].bitcast(F32), 0.0)
            nc.vector.memset(xv[:, :, :, XD:XVA], 1.0).then_inc(consts, 1)
            dve.wait_ge(consts_act, 1)
            dve.wait_ge(xw_loaded, XW_LOADS * 16)
            dve.wait_ge(consts, 1)
            def centre(src, mean, cent, scratch, link, base, ready):
                nc.vector.tensor_reduce(mean[:, 0:1], src, AX_X, ALU.add).then_inc(link, 1)
                dve.wait_ge(link, base + 1)
                nc.vector.tensor_scalar(mean[:, 0:1], mean[:, 0:1], 1.0 / DIM, None, ALU.mult).then_inc(link, 1)
                dve.wait_ge(link, base + 2)
                nc.vector.tensor_scalar(cent, src, mean[:, 0:1], None, ALU.subtract).then_inc(link, 1)
                dve.wait_ge(link, base + 3)
                nc.vector.tensor_tensor_reduce(out=scratch, in0=cent, in1=cent, scale=1.0 / DIM, scalar=1e-5,
                                               op0=ALU.mult, op1=ALU.add, accum_out=mean[:, 1:2]).then_inc(ready, 1)

            def xperiod(p, b, n):
                par, nxt = p % 2, 1 - p % 2
                for kind, j in in_xperiod(p, "SVLPNE"):
                    if kind == "S":
                        dve.wait_ge(xs_mm, b * 4 + j + 1)
                        s3 = bank[2 + j % 2][:, :].rearrange("p (h t) -> p h t", h=GROUP)
                        nc.vector.tensor_reduce(xmax[:, j], s3, AX_X, ALU.max).then_inc(xmax_ok, 1)
                        dve.wait_ge(xmax_ok, b * 4 + j + 1)
                        dve.wait_ge(xt_mm, b * 4 + max(0, j - 1))
                        nc.vector.tensor_tensor(xp[:, j % 2, :].rearrange("p (h t) -> p h t", h=GROUP), s3,
                                                xmax[:, j, :, None].to_broadcast([P, GROUP, SEQ]), ALU.subtract).then_inc(xs_sub, 1)
                    elif kind == "V":
                        dve.wait_ge(xpv_mm, b * 4 + j + 1)
                        if j == 0 and p >= 1:
                            dve.wait_ge(xoT_mm, b)
                        o3 = bank[5][:, 0:GROUP * XVA].rearrange("p (h d) -> p h d", h=GROUP)
                        nc.vector.reciprocal(xsum[:, j], o3[:, :, XD]).then_inc(xsum_ok, 1)
                        dve.wait_ge(xsum_ok, b * 4 + j + 1)
                        nc.vector.tensor_tensor(xo.rearrange("p (i j) d -> p i j d", j=4)[:, :, j, :], o3[:, :, 0:XD],
                                                xsum[:, j, :, None].to_broadcast([P, GROUP, XD]), ALU.mult).then_inc(xo_norm, 1)
                    elif kind == "L" and j == 0:
                        dve.wait_ge(x_in[nxt], n * 48)
                        if p >= 0:
                            dve.wait_ge(xnT_mm, b + 1)
                        centre(xin[:, nxt, :], mean1, cent1, xnorm1, link1, b * 3 + 3, var1)
                        if p >= 1:
                            dve.wait_ge(xs_mm, b * 4)
                        nc.vector.tensor_scalar(maskf[:, nxt, :], mask8[:, nxt, :], NEG_INF, None, ALU.mult).then_inc(mask_made, 1)
                    elif kind == "L":
                        dve.wait_ge(rstd1, b + 2)
                        nc.vector.tensor_scalar(xnorm1, cent1, xr1, None, ALU.mult).then_inc(norm1_ok, 1)
                    elif kind == "P":
                        dve.wait_ge(xv_mm, b + 2)
                        if p >= 1:
                            dve.wait_ge(xpv_mm, b * 4)
                        nc.vector.tensor_tensor(xv[:, nxt, :, 0:XD], bank[6][:, 0:DIM].rearrange("p (h d) -> p h d", h=XH),
                                                bvo[:, 0, :].rearrange("p (h d) -> p h d", h=XH), ALU.add).then_inc(xv_ready, 1)
                    elif kind == "N" and j == 0:
                        dve.wait_ge(xwo_mm, b)
                        dve.wait_ge(res_in[nxt], n * 16 - 16)
                        dve.wait_ge(x1_out[nxt], n * 16 - 32)
                        nc.vector.tensor_tensor(x1[:, nxt, :], bank[6][:, 0:DIM], bvo[:, 1, :], ALU.add).then_inc(x1_sum, 1)
                        dve.wait_ge(x1_sum, b)
                        nc.vector.scalar_tensor_tensor(out=x1[:, nxt, :], in0=x1[:, nxt, :], scalar=gates[:, 2:3],
                                                       in1=xres[:, nxt, :], op0=ALU.mult, op1=ALU.add).then_inc(x1_made, 1)
                        dve.wait_ge(x1_made, b)
                        dve.wait_ge(x_mm, b - 1)
                        centre(x1[:, nxt, :], mean2, cent2, xnorm2, link2, b * 3 - 3, var2)
                    elif kind == "N":
                        dve.wait_ge(rstd2, b)
                        nc.vector.tensor_scalar(xnorm2, cent2, xr2, None, ALU.mult).then_inc(norm2_ok, 1)
                    elif j == 2:
                        dve.wait_ge(x_mm, b)
                        at = bass.ds(b - 1, 1)
                        nc.vector.tensor_copy(X0[:, at, :], bank[7][:, 0:P])
                        nc.vector.tensor_copy(X1[:, at, 1:SEQ + 1], bank[7][:, P:2 * P]).then_inc(x_stored, 1)

            xperiods(dve, xperiod)
            barrier(dve, 0)
            nc.vector.memset(vals[:, :, DH:VA], 1.0).then_inc(v_ones, 1)

            def x_step(par, b, layer, reuse):
                if reuse is not None:
                    dve.wait_ge(val_mm, reuse)
                nc.vector.tensor_copy(xs[:, par, 0, 0, :], X0[:, bass.ds(b, 1), :])
                nc.vector.tensor_copy(xs[:, par, 0, 1, :], X1[:, bass.ds(b, 1), 0:SEQ]).then_inc(xs_hi, 1)
                dve.wait_ge(xs_hi, layer * BATCH + b + 1)
                nc.vector.tensor_tensor(xs[:, par, 1, 0, :], X0[:, bass.ds(b, 1), :], xs[:, par, 0, 0, :].bitcast(F32), ALU.subtract)
                nc.vector.tensor_tensor(xs[:, par, 1, 1, :], X1[:, bass.ds(b, 1), 0:SEQ], xs[:, par, 0, 1, :].bitcast(F32),
                                        ALU.subtract).then_inc(xs_ready, 1)

            def rotate(n, src, nxt, first):
                dve.wait_ge(squared, nxt * 2 + n + 1)
                if not first:
                    dve.wait_ge(rope_sum, nxt * 2 - 1 + n)
                src = src.rearrange("p (h d) -> p h d", h=HPC)
                d1 = m1[:, n, :].rearrange("p (h d) -> p h d", h=HPC)
                d2 = m2[:, n, :].rearrange("p (h d) -> p h d", h=HPC)
                cos, sin = rope_q[:, n, 0, :], rope_q[:, n, 1, :]
                for a, b in ((0, HALF), (HALF, 0)):
                    nc.vector.tensor_tensor(d2[:, :, a:a + HALF], src[:, :, b:b + HALF],
                                            sin[:, None, a:a + HALF].to_broadcast([P, HPC, HALF]), ALU.mult)
                nc.vector.tensor_tensor(d1, src, cos[:, None, :].to_broadcast([P, HPC, DH]), ALU.mult).then_inc(rotated, 1)
                if not first:
                    dve.wait_ge(rnorms, nxt * 2 - 1 + n)
                nc.vector.tensor_reduce(norm2[:, n, :], sq[:, n, :].rearrange("p (h d) -> p h d", h=HPC), AX_X,
                                        ALU.add).then_inc(norm_sum, 1)
                dve.wait_ge(norm_sum, nxt * 2 + n + 1)
                nc.vector.tensor_scalar(norm2[:, n, :], norm2[:, n, :], 1e-24, None, ALU.max).then_inc(norms, 1)

            def period(u, g, layer, pair):
                odd = u % 2
                for kind, e in in_period(u):
                    if kind == "S":
                        dve.wait_ge(s_mm, g * 2 + e + 1)
                        s3 = bank[2 + e][:, :].rearrange("p (h t) -> p h t", h=GROUP)
                        nc.vector.tensor_reduce(smax[:, e, :], s3, AX_X, ALU.max).then_inc(s_max, 1)
                        dve.wait_ge(s_max, g * 2 + e + 1)
                        dve.wait_ge(t_mm, g * 2)
                        nc.vector.tensor_tensor(probs[:, e, :].rearrange("p (h t) -> p h t", h=GROUP), s3,
                                                smax[:, e, :, None].to_broadcast([P, GROUP, SEQ]), ALU.subtract).then_inc(s_sub, 1)
                    elif kind in "QK":
                        n = "QK".index(kind)
                        nxt = g if u == -2 else g + 2 if u >= 0 else g + 1
                        rotate(n, bank[(3 * u + n) % 2][:, :], nxt, u == -2)
                    elif kind == "O":
                        dve.wait_ge(o_hi, g)
                        k, half_ = (u - 1) % 2, (u - 1) // 2 % 2
                        cols = slice(half_ * SEQ, (half_ + 1) * SEQ)
                        nc.vector.tensor_tensor(oT[:, 1, 4 * k:4 * k + 4, cols], bank[5][:, :].rearrange("p (c t) -> p c t", c=4),
                                                oT[:, 0, 4 * k:4 * k + 4, cols].bitcast(F32), ALU.subtract).then_inc(o_lo, 1)
                    elif kind == "V":
                        dve.wait_ge(v_mm, g * 2 + e + 1)
                        o3 = bank[6][:, 0:GROUP * VA].rearrange("p (h d) -> p h d", h=GROUP)
                        nc.vector.reciprocal(rsum[:, e, :], o3[:, :, DH]).then_inc(r_sum, 1)
                        dve.wait_ge(r_sum, g * 2 + e + 1)
                        dst = outs[:, HPC * odd:HPC * odd + HPC, :].rearrange("p (i e) d -> p i e d", e=2)[:, :, e, :]
                        nc.vector.tensor_tensor(dst, o3[:, :, 0:DH], rsum[:, e, :, None].to_broadcast([P, GROUP, DH]),
                                                ALU.mult).then_inc(o_norm, 1)
                    elif kind == "W" and e == 1:
                        p = pair - 1 if u < UNITS else pair
                        dve.wait_ge(w_mm, (layer * (BATCH // 2) + p) * 2 + 2)
                        a0, a1 = X0[:, bass.ds(p * 2, 2), :], X1[:, bass.ds(p * 2, 2), 1:SEQ + 1]
                        y = bank[7][:, :].rearrange("p (m b t) -> p m b t", m=KC, b=2)
                        nc.vector.tensor_tensor(a0, a0, y[:, 0], ALU.add)
                        nc.vector.tensor_tensor(a1, a1, y[:, 1], ALU.add).then_inc(x_added, 1)
                    elif kind == "X":
                        nb = BATCH_OF(u + 3, pair)
                        x_step(((u + 3) // 2) % 2, nb, layer, g + 1 if u >= 0 else g)

            run_periods = periods(dve, period)

            def ln_steps(kind, k, gt, t):
                if kind == "M":
                    dve.wait_ge(mean_mm, gt + 1)
                    nc.vector.tensor_tensor(xc[:, 0, :].rearrange("p (b t) -> p b t", b=4), X0[:, bass.ds(t * 4, 4), :],
                                            bank[6][:, :].rearrange("p (b t) -> p b t", b=4), ALU.subtract)
                    nc.vector.tensor_tensor(xc[:, 1, :].rearrange("p (b t) -> p b t", b=4), X1[:, bass.ds(t * 4, 4), 0:SEQ],
                                            bank[6][:, :].rearrange("p (b t) -> p b t", b=4), ALU.subtract).then_inc(centred, 1)
                elif kind == "R":
                    dve.wait_ge(var_mm, gt + 1)
                    dve.wait_ge(rstd_ok, gt)
                    nc.vector.tensor_scalar(var4, bank[7][:, 0:4], 1e-5, None, ALU.add).then_inc(var_ok, 1)
                elif kind == "N" and k == 0:
                    dve.wait_ge(bc_mm, gt + 1)
                    dve.wait_ge(centred, gt + 1)
                    dve.wait_ge(var_mm, gt + 1)
                    nc.vector.tensor_tensor(xq, xc, bank[6][:, None, :].to_broadcast([P, KC, TOK]), ALU.mult).then_inc(xn_ok, 1)
                elif kind == "N":
                    dve.wait_ge(xg_ok, gt + 1)
                    dve.wait_ge(u_mm, gt * 6)
                    nc.vector.tensor_copy(xn_parts[:, 0], xg).then_inc(xn_hi, 1)
                    dve.wait_ge(xn_hi, gt + 1)
                    nc.vector.tensor_tensor(xn_parts[:, 1], xg, xn_parts[:, 0].bitcast(F32), ALU.subtract).then_inc(xn_lo, 1)

            def u_step(m, gt):
                rows = P if m < FULL else REST
                col = m if m < FULL else 2 * FULL
                dve.wait_ge(gelu_ok, gt * 6 + m + 1)
                dve.wait_ge(h_lo, gt * 6 + max(0, m - 1))
                nc.vector.scalar_tensor_tensor(out=hf[0:rows, m % 2, :], in0=bank[2 * (m % 2)][0:rows, :],
                                               scalar=b1_t[0:rows, col:col + 1], in1=gelu[0:rows, m % 2, :],
                                               op0=ALU.add, op1=ALU.mult).then_inc(h_ok, 1)
                dve.wait_ge(h_hi, gt * 6 + m + 1)
                nc.vector.tensor_tensor(h_parts[0:rows, m % 2, 1, :], hf[0:rows, m % 2, :],
                                        h_parts[0:rows, m % 2, 0, :].bitcast(F32), ALU.subtract).then_inc(h_lo, 1)

            def add_ffn(gt, t):
                dve.wait_ge(d_mm, gt * 6 + 6)
                a0, a1 = X0[:, bass.ds(t * 4, 4), :], X1[:, bass.ds(t * 4, 4), 1:SEQ + 1]
                for o, a in enumerate((a0, a1)):
                    ins = nc.vector.scalar_tensor_tensor(out=a, in0=bank[4 + o][:, :].rearrange("p (b t) -> p b t", b=4),
                                                         scalar=b2_t[:, o:o + 1], in1=a, op0=ALU.add, op1=ALU.add)
                ins.then_inc(f_added, 1)

            def feed(gt, nxt, t):
                for kind, n in FFN_STEPS:
                    if kind == "U":
                        u_step(n, gt)
                    elif kind == "D":
                        if n == FULL:
                            add_ffn(gt, t)
                    elif nxt is not None:
                        ln_steps(kind, n, nxt, t + 1)

            low_parts(dve, list(attn_pieces(0)), 0, 0)
            with dve.Fori(0, DEPTH) as layer:
                dve.wait_ge(vec_in, (layer + 1) * VECTORS * 16)
                for a in range(2):
                    nc.vector.tensor_tensor(rope_q[:, a, 0, :], rope_t[:, 2 * a, :], qk_scale[:, a, :], ALU.mult)
                    for lo, hi in ((0, HALF), (HALF, 0)):
                        ins = nc.vector.tensor_tensor(rope_q[:, a, 1, lo:lo + HALF], rope_t[:, 2 * a + 1, lo:lo + HALF],
                                                      qk_scale[:, a, hi:hi + HALF], ALU.mult)
                ins.then_inc(tables, 1)
                dve.wait_ge(tables, layer + 1)
                low_parts(dve, list(ffn_pieces(0)), layer, 1)
                x_step(0, 0, layer, None)
                run_periods(layer)
                barrier(dve, layer * 2 + 1)
                for kind, n in FFN_STEPS:
                    if kind in "MRN":
                        ln_steps(kind, n, layer * 4, 0)
                low_parts(dve, list(attn_pieces(0)), layer + 1, 0)
                with dve.Fori(0, 3) as t:
                    feed(layer * 4 + t, layer * 4 + t + 1, t)
                feed(layer * 4 + 3, None, 3)
                barrier(dve, layer * 2 + 2)
                nc.vector.memset(vals[:, :, DH:VA], 1.0).then_inc(v_ones, 1)
            with dve.Fori(0, BATCH) as b:
                dve.wait_ge(fin_mm, b)
                nc.vector.tensor_copy(xoT[:, 0, :], X0[:, bass.ds(b, 1), :])
                nc.vector.tensor_copy(xoT[:, 1, :], X1[:, bass.ds(b, 1), 1:SEQ + 1]).then_inc(fin_copied, 1)
                dve.wait_ge(fin_mm, b + 1)
                dve.wait_ge(fin_in, b * 16 + 16)
                dve.wait_ge(fin_out, b * 16)
                nc.vector.scalar_tensor_tensor(out=x1[:, 0, :], in0=bank[0][:, 0:DIM], scalar=gates[:, 3:4], in1=xin[:, 0, :], op0=ALU.mult,
                                               op1=ALU.add).then_inc(fin_ok, 1)

        @block.gpsimd
        def _(pool):
            nc.gpsimd.memset(half[:, :], -0.5).then_inc(half_ok, 1)
            pool.wait_ge(half_ok, 1)
            def xperiod(p, b, n):
                for kind, j in in_xperiod(p, "LN"):
                    if j:
                        continue
                    if kind == "L":
                        pool.wait_ge(var1, b + 2)
                        nc.gpsimd.tensor_tensor(xr1, mean1[:, 1:2], half[:, 0:1], ALU.pow).then_inc(rstd1, 1)
                    else:
                        pool.wait_ge(var2, b)
                        nc.gpsimd.tensor_tensor(xr2, mean2[:, 1:2], half[:, 0:1], ALU.pow).then_inc(rstd2, 1)

            xperiods(pool, xperiod)
            barrier(pool, 0)

            def finish(n, g, first):
                pool.wait_ge(rotated, g * 2 + n + 1)
                if not first:
                    pool.wait_ge(b_mm, g * 2 - 1 + n)
                nc.gpsimd.tensor_tensor(qkr[:, n, :], m1[:, n, :], m2[:, n, :], ALU.add).then_inc(rope_sum, 1)
                pool.wait_ge(norms, g * 2 + n + 1)
                if not first:
                    pool.wait_ge(qk_ready, g * 2 - 1 + n)
                nc.gpsimd.tensor_tensor(rnorm[:, n, :], norm2[:, n, :], half[:, 0:HPC], ALU.pow).then_inc(rnorms, 1)
                pool.wait_ge(rnorms, g * 2 + n + 1)
                pool.wait_ge(rope_sum, g * 2 + n + 1)
                q3 = qkr[:, n, :].rearrange("p (h d) -> p h d", h=HPC)
                nc.gpsimd.tensor_tensor(q3, q3, rnorm[:, n, :, None].to_broadcast([P, HPC, DH]), ALU.mult).then_inc(qk_ready, 1)

            with pool.Fori(0, DEPTH) as layer:
                for n in range(2):
                    finish(n, layer * UNITS, True)
                with pool.Fori(1, UNITS) as u:
                    for n in range(2):
                        finish(n, layer * UNITS + u, False)
                barrier(pool, layer * 2 + 1)
                for t in range(4):
                    gt = layer * 4 + t
                    pool.wait_ge(var_ok, gt + 1)
                    pool.wait_ge(bc_mm, gt)
                    nc.gpsimd.tensor_tensor(rstd4, var4, half[:, 0:4], ALU.pow).then_inc(rstd_ok, 1)
                barrier(pool, layer * 2 + 2)


_INS = ['x', 'ctx_1024', 'mask_BxSxS2_bf0', 'g_xattn', 'g_ffn', 'L0_xattn_Wq', 'L0_xattn_bq', 'L0_xattn_Wk',
        'L0_xattn_bk', 'L0_xattn_Wv', 'L0_xattn_bv', 'L0_xattn_Wo', 'L0_xattn_bo', 'L0_ffn_Wqkv', 'L0_ffn_q_scale',
        'L0_ffn_k_scale', 'L0_ffn_Wo', 'L0_ffn_ln_g', 'L0_ffn_ln_b', 'L0_ffn_W1', 'L0_ffn_b1', 'L0_ffn_W2', 'L0_ffn_b2']


def shape_constants():
    f = np.float32
    half = np.arange(0, DH, 2, dtype=f)
    freqs = np.arange(SEQ, dtype=f)[:, None] * (f(1.0) / f(10000.0) ** (half / f(DH)))[None, :]
    power = (np.arange(SEQ, dtype=f) - f(SEQ // 2)) / f(WINDOW // 2)
    scale = ((half + f(0.4 * DH)) / f(1.4 * DH))[None, :] ** power[:, None]
    cos, sin = np.cos(freqs), np.sin(freqs)
    signed = lambda a: np.concatenate([-a, a], -1)
    twice = lambda a: np.concatenate([a, a], -1)
    rope = np.stack([twice(cos * scale), signed(sin * scale), twice(cos / scale), signed(sin / scale)], 1).astype(f)
    i, j = np.arange(SEQ)[:, None], np.arange(SEQ)[None, :]
    band = np.where((i < j) | (i > j + WINDOW), f(NEG_MASK), f(0)).astype(f)
    return {"rope": rope, "band": band, "eye": np.eye(P, dtype=f)}


def kernel(**inputs):
    import concourse.bacc as _bacc
    from concourse.bass_utils import run_bass_kernel_spmd as _run

    nc = _bacc.Bacc("TRN2", target_bir_lowering=False, num_devices=1)
    arrays, args = {}, []
    given = [(n, inputs[n]) for n in _INS] + list(shape_constants().items())
    for name, a in given:
        a = np.ascontiguousarray(a)
        arrays[f"in_{name}_dram"] = a
        args.append(nc.dram_tensor(f"in_{name}_dram", a.shape, mybir.dt.from_np(a.dtype), kind="ExternalInput").ap())
    args.append(nc.dram_tensor("out_0_dram", (BATCH, SEQ, DIM), F32, kind="ExternalOutput").ap())
    build(nc, *args)
    r = _run(nc, [arrays], core_ids=[0])
    return r.results[0]["out_0_dram"]
```

```python
from contextlib import ExitStack

import numpy as np

import concourse.bass as bass
from concourse import mybir

P = 128
ALU = mybir.AluOpType
ACT = mybir.ActivationFunctionType
F32 = mybir.dt.float32
F32R = mybir.dt.float32r
BF16 = mybir.dt.bfloat16
U8 = mybir.dt.uint8
AX_X = mybir.AxisListType.X

BATCH, SEQ, DIM = 16, 128, 256
KC = DIM // P
XH, XD = 16, 16
XPAD = 32
DEPTH, HEADS, DH = 6, 16, 64
WINDOW = 64
INNER = HEADS * DH
OC = INNER // P
FF = DIM * 4 * 2 // 3
FULL = FF // P
REST = FF - FULL * P
GATE0 = 64
HALF = DH // 2
CH = 512
HPC = CH // DH
GROUP = 4
TOK = 4 * SEQ
VA = DH + 1
XVA = XD + 1
NEG_MASK = -1e30
NEG_INF = -1e18

XW_LOADS = 16
XPERIOD = ["S0", "W3", "I0", "S1", "T0", "K0", "P0", "S2", "V0", "E0", "T1", "S3", "E1", "T2", "Q0", "V1", "V2",
           "T3", "E2"]
DVE_XPERIOD = ["L0", "L1", "S0", "W3", "S1", "P0", "S2", "S3", "N0", "N1"]
ACT_XPERIOD = ["I0", "S0", "S1", "T0", "K0", "E0", "T1", "S2", "T2", "S3", "Q0", "T3", "E2"]
VECTORS = 7

PERIOD = ["N0", "S0", "O", "S1", "M0", "Q", "B0", "T0", "K", "B1", "V0", "T1", "W0", "R0", "C", "V1", "W1"]
DVE_PERIOD = ["N0", "S0", "O", "S1", "Q", "M0", "X", "V0", "K", "R0", "V1", "N2", "W1"]
ACT_PERIOD = ["O", "S0", "Q", "S1", "B0", "T0", "M0", "K", "T1", "B1", "C", "N1"]
UNITS = 2 * BATCH
FFN_STEPS = [("M", 0), ("U", 1), ("S", 0), ("U", 2), ("D", 0), ("R", 0), ("U", 3), ("D", 1), ("N", 0), ("S", 1),
             ("N", 1), ("U", 4), ("D", 2), ("N", 2), ("U", 5), ("D", 3), ("D", 4), ("F", 0), ("D", 5)]


def build(nc, x, ctx_1024, mask, g_xattn, g_ffn, Wq, bq, Wk, bk, Wv, bv, Wo, bo,
          Wqkv, q_scale, k_scale, Wout, ln_g, ln_b, W1, b1, W2, b2, rope, band, eye, out):
    with ExitStack() as stack:
        def sb(name, shape, dt=F32):
            return stack.enter_context(nc.sbuf_tensor(name, shape, dt))

        def sem(name):
            return stack.enter_context(nc.semaphore(name))

        bank = [stack.enter_context(nc.psum_tensor(f"bank{i}", [P, CH], F32)) for i in range(8)]

        X0 = sb("X0", [P, BATCH, SEQ])
        X1 = sb("X1", [P, BATCH, SEQ + 1])
        wqkv = sb("wqkv", [P, 2, KC, 3 * INNER], F32R)
        wout = sb("wout", [P, 2, OC, DIM], F32R)
        w1 = sb("w1", [P, 2, KC, 2 * FULL + 1, P], F32R)
        w2 = sb("w2", [P, 2, FULL + 1, DIM], F32R)
        parts = sb("parts", [P, (2 * KC + 4 * 2) * TOK], F32R)
        xs = sb("xs", [P, 2, 2, KC, SEQ], F32R)
        oT = parts[:, 0:2 * OC * 2 * SEQ].rearrange("p (s c t) -> p s c t", s=2, c=OC)
        xn_parts = parts[:, 4 * 2 * TOK:].rearrange("p (s c t) -> p s c t", s=2, c=KC)
        h_parts = [parts[:, a:a + 2 * TOK].rearrange("p (s t) -> p s t", s=2)
                   for a in range(0, 3 * 2 * TOK, 2 * TOK)]
        ident = sb("ident", [P, P])
        ident_bf = sb("ident_bf", [P, P], BF16)
        band_f = sb("band_f", [P, P])
        band_bf = sb("band_bf", [P, P], BF16)
        rope_t = sb("rope_t", [P, 4, DH])
        qk_scale = sb("qk_scale", [P, 2, DH])
        rope_q = sb("rope_q", [P, 2, 2, DH])
        inv_dim = sb("inv_dim", [P, P])
        ln_gb = sb("ln_gb", [P, 2, KC])
        b1_t = sb("b1_t", [P, 2 * FULL + 1])
        b2_t = sb("b2_t", [P, KC])
        gates = sb("gates", [P, 4])
        half = sb("half", [P, 16])
        work = sb("work", [P, 14424])

        offset = [0]

        def part(n):
            a = offset[0]
            offset[0] += n
            assert offset[0] <= work.shape[1], offset[0]
            return work[:, a:a + n]

        raw = part(2 * 1024).rearrange("p (b n) -> p b n", b=2)
        after_raw = offset[0]
        m1 = part(2 * CH).rearrange("p (b n) -> p b n", b=2)
        m2 = part(2 * CH).rearrange("p (b n) -> p b n", b=2)
        sq = part(2 * CH).rearrange("p (b n) -> p b n", b=2)
        qkr = part(2 * CH).rearrange("p (b n) -> p b n", b=2)
        probs = part(2 * CH).rearrange("p (b n) -> p b n", b=2)
        probsT = part(2 * CH).rearrange("p (b n) -> p b n", b=2)
        qkT = part(2 * CH).rearrange("p (s n) -> p s n", s=2)
        vals = part(HEADS * VA).rearrange("p (h d) -> p h d", h=HEADS)
        outs = part(INNER).rearrange("p (h d) -> p h d", h=HEADS)
        norm2 = part(4 * HPC).rearrange("p (b n) -> p b n", b=4)
        rnorm = part(4 * HPC).rearrange("p (b n) -> p b n", b=4)
        smax = part(4 * GROUP).rearrange("p (b n) -> p b n", b=4)
        rsum = part(4 * GROUP).rearrange("p (b n) -> p b n", b=4)
        xc = part(KC * TOK).rearrange("p (c t) -> p c t", c=KC)
        xq = part(KC * TOK).rearrange("p (c t) -> p c t", c=KC)
        xg = xc
        var4 = part(4)
        rstd4 = part(4)
        offset[0] = after_raw
        gelu, hf = probs, probsT
        offset[0] = after_raw
        xwq = part(KC * XH * XPAD).rearrange("p (c h d) -> p c h d", c=KC, h=XH)
        xwk = part(KC * XH * XPAD).rearrange("p (c h d) -> p c h d", c=KC, h=XH)
        padded = work[:, after_raw:offset[0] + 8]
        bqk = part(2 * 4).rearrange("p (a c) -> p a c", a=2)
        xwv = part(KC * DIM).rearrange("p (c n) -> p c n", c=KC)
        xwo = part(KC * DIM).rearrange("p (c n) -> p c n", c=KC)
        bvo = part(2 * DIM).rearrange("p (a n) -> p a n", a=2)
        def two(n):
            return part(2 * n).rearrange("p (b n) -> p b n", b=2)

        xin, cin, xres, x1 = two(DIM), two(DIM), two(DIM), two(DIM)
        mean1, mean2 = part(2), part(2)
        cent1, cent2 = part(DIM), part(DIM)
        xnorm1, xnorm2 = part(DIM), part(DIM)
        tT = part(2 * KC * SEQ).rearrange("p (a c t) -> p a c t", a=2, c=KC)
        xqk = part(2 * 2 * 4 * SEQ).rearrange("p (k a c t) -> p k a c t", k=2, a=2, c=4)
        xv = part(2 * XH * XVA).rearrange("p (b h d) -> p b h d", b=2, h=XH)
        xp, xpT = two(CH), two(CH)
        xo = part(DIM).rearrange("p (h d) -> p h d", h=XH)
        xoT = part(KC * SEQ).rearrange("p (c t) -> p c t", c=KC)
        xmax, xsum = [part(16).rearrange("p (j i) -> p j i", j=4) for _ in range(2)]
        xr1, xr2 = part(1), part(1)
        offset[0] = after_raw
        x_rows, out_rows, x_cols = [part(2 * 2 * DIM).rearrange("p (k b n) -> p k b n", k=2, b=2) for _ in range(3)]
        maskf = sb("maskf", [P, 2, SEQ], BF16)
        mask8 = sb("mask8", [P, 2, SEQ], U8)

        x1_dram = nc.dram_tensor("x_after_xattn", (BATCH, SEQ, DIM), F32, kind="Internal").ap()

        loaded = sem("constants_loaded")
        consts = sem("constants_ready")
        xw_loaded = sem("xattn_weights_loaded")
        x_in = [sem("even_inputs_loaded"), sem("odd_inputs_loaded")]
        x1_out = [sem("even_x1_stored"), sem("odd_x1_stored")]
        phase_done = sem("phase_done")
        consts_act, half_ok = sem("constants_made"), sem("exponents_ready")
        link1, link2 = sem("x_norm_links"), sem("x1_norm_links")
        var1, rstd1, norm1_ok = sem("x_variance"), sem("x_rstd"), sem("x_normalised")
        var2, rstd2, norm2_ok = sem("x1_variance"), sem("x1_rstd"), sem("x1_normalised")
        xmax_ok, xsum_ok, res_in = sem("xattn_max"), sem("xattn_sum_inverted"), [sem("even_residual_loaded"), sem("odd_residual_loaded")]
        xnT_mm, xT_copied = sem("inputs_transposed"), sem("inputsT_copied")
        xk_mm, xv_mm, xq_mm, xk_ready, xqk_ready, xv_ready = (sem("xattn_k"), sem("xattn_v"), sem("xattn_q"), sem("xattn_k_ready"),
                                                              sem("xattn_q_ready"), sem("xattn_v_ready"))
        mask_made, xs_mm, xs_sub, xs_exp = sem("mask_made"), sem("xattn_scores"), sem("xattn_minus_max"), sem("xattn_probs")
        xt_mm, xpT_copied, xpv_mm, xo_norm = (sem("xattn_probs_transposed"), sem("xattn_probsT"), sem("xattn_pv"),
                                              sem("xattn_outs"))
        xoT_mm, xoT_copied, xwo_mm = sem("xattn_outs_transposed"), sem("xattn_outsT"), sem("xattn_wo")
        x1_sum, x1_made, x_mm, x_stored = sem("xattn_biased"), sem("x1_made"), sem("x_transposed"), sem("x_stored")
        norm_sum, cleared, fin_copied = sem("norm_sums_ready"), sem("work_cleared"), sem("x_copied_back")

        raw_in = [sem("raw_weights_loaded0"), sem("raw_weights_loaded1")]
        raw_hi = sem("weights_high_part")
        raw_lo = sem("weights_low_part")
        qk_in, vec_in = sem("qk_scales_loaded"), sem("ffn_vectors_loaded")
        tables = sem("rope_tables_ready")
        xs_hi, xs_ready = sem("xs_high_part"), sem("xs_ready")
        qk_mm, val_mm = sem("qk_chunk_done"), sem("v_chunk_done")
        squared, rotated, v_copied = sem("qk_squared"), sem("qk_rotated"), sem("v_copied")
        norms, rope_sum, rnorms, qk_ready = sem("norms_summed"), sem("rope_summed"), sem("rnorms_ready"), sem("qk_ready")
        b_mm, b_copied = sem("qk_transposed"), sem("qkT_copied")
        s_mm, s_max, s_sub, s_exp = sem("scores_done"), sem("max_ready"), sem("scores_minus_max"), sem("probs_ready")
        t_mm, t_copied = sem("probs_transposed"), sem("probsT_copied")
        v_mm, r_sum, o_norm = sem("pv_done"), sem("sum_inverted"), sem("outs_normalised")
        o_mm, o_hi, o_lo = sem("outs_transposed"), sem("outT_high_part"), sem("outT_low_part")
        w_mm, x_added = sem("wo_done"), sem("attention_added")

        mean_mm, centred, xsq, var_mm, var_ok, rstd_ok = (sem("mean_done"), sem("centred"), sem("centred_squared"),
                                                          sem("variance_done"), sem("variance_ready"), sem("rstd_ready"))
        bc_mm, xn_ok, xg_ok, xn_hi, xn_lo = (sem("rstd_spread"), sem("xn_ready"), sem("xn_affine"), sem("xn_high_part"),
                                             sem("xn_low_part"))
        u_mm, gelu_ok, h_ok, h_hi, h_lo = (sem("up_done"), sem("gelu_ready"), sem("h_ready"), sem("h_high_part"),
                                           sem("h_low_part"))
        d_mm, f_added = sem("down_done"), sem("ffn_added")
        fin_mm, fin_ok = sem("x_back"), sem("out_ready")
        fin_in, fin_out = [sem("even_x1_loaded"), sem("odd_x1_loaded")], [sem("even_out_stored"), sem("odd_out_stored")]

        def norm_banks(t):
            return (2, 3, 4) if isinstance(t, int) else (6, 7, 6)

        def primed(n):
            return n + 1

        def barrier(eng, phase):
            eng.drain().then_inc(phase_done, 1)
            eng.wait_ge(phase_done, phase * 4 + 4)

        def arrive(eng):
            eng.drain().then_inc(phase_done, 1)

        def attn_pieces(layer):
            r = Wqkv[layer].rearrange("(c p) n -> c p n", p=P)
            o = Wout[layer].rearrange("(c p) n -> p c n", p=P)
            for c in range(KC):
                for n in range(0, 3 * INNER, 1024):
                    yield P, r[c, :, n:n + 1024], [(0, 1024, lambda s, c=c, n=n: wqkv[:, s, c, n:n + 1024])]
            for c in range(0, OC, 4):
                yield P, o[:, c:c + 4, :], [(0, 1024, lambda s, c=c: wout[:, s, c:c + 4, :].rearrange("p c n -> p (c n)"))]

        def ffn_pieces(layer):
            r = W1[layer].rearrange("(c p) n -> c p n", p=P)
            d = W2[layer]
            for c in range(KC):
                for a in range(2):
                    g0 = GATE0 if a else 0
                    yield P, r[c, :, a * FF:(a + 1) * FF], [
                        (0, FULL * P, lambda s, c=c, a=a: w1[:, s, c, a * FULL:(a + 1) * FULL, :].rearrange("p m n -> p (m n)")),
                        (FULL * P, FF, lambda s, c=c, g0=g0: w1[:, s, c, 2 * FULL, g0:g0 + REST])]
            full = d[0:FULL * P, :].rearrange("(c p) n -> p c n", p=P)
            for c, n in ((0, 4), (4, 1)):
                yield P, full[:, c:c + n, :], [(0, n * DIM, lambda s, c=c, n=n: w2[:, s, c:c + n, :].rearrange("p c n -> p (c n)"))]
            yield REST, d[FULL * P:FF, :], [(0, DIM, lambda s: w2[0:REST, s, FULL, :])]

        ATTN_N, FFN_N = KC * 3 + OC // 4, KC * 2 + 3
        PIECES = ATTN_N + FFN_N

        def load_pieces(sp, pieces, base, first=0, end=ATTN_N):
            for i, (rows, src, _) in list(enumerate(pieces))[first:end]:
                if not isinstance(base, int) or base + i > 1:
                    sp.wait_ge(raw_lo, base + i - 1 if i else base)
                n = 1
                for w in src.shape[1:]:
                    n *= w
                dst = raw[0:rows, i % 2, 0:n]
                if len(src.shape) == 3:
                    dst = dst.rearrange("p (c n) -> p c n", c=src.shape[1])
                sp.dma_start(dst, src).then_inc(raw_in[i % 2], 16)

        def raw_count(layer, kind, i):
            per = [(ATTN_N + 1) // 2 + (FFN_N + 1) // 2, ATTN_N // 2 + FFN_N // 2][i % 2]
            before = 0 if kind == 0 else [(ATTN_N + 1) // 2, ATTN_N // 2][i % 2]
            return (layer * per + (before + i // 2 + 1)) * 16

        def high_parts(act, pieces, layer, kind, first=0, end=ATTN_N):
            for i, (rows, _, dests) in list(enumerate(pieces))[first:end]:
                act.wait_ge(raw_in[i % 2], raw_count(layer, kind, i))
                for k, (a, b, dst) in enumerate(dests):
                    ins = nc.scalar.copy(dst(0), raw[0:rows, i % 2, a:b])
                ins.then_inc(raw_hi, 1)

        def low_parts(dve, pieces, layer, kind, first=0, end=ATTN_N):
            base = layer * PIECES + (ATTN_N if kind else 0)
            for i, (rows, _, dests) in list(enumerate(pieces))[first:end]:
                dve.wait_ge(raw_hi, base + i + 1)
                dve.wait_ge(raw_in[i % 2], raw_count(layer, kind, i))
                for k, (a, b, dst) in enumerate(dests):
                    ins = nc.vector.tensor_tensor(dst(1), raw[0:rows, i % 2, a:b], dst(0).bitcast(F32), ALU.subtract)
                ins.then_inc(raw_lo, 1)

        def next_piece(i, t):
            if isinstance(t, int):
                return lambda s: wout[:, s, 4 * i:4 * i + 4, :].rearrange("p c n -> p (c n)")
            return lambda s: wqkv[:, s].rearrange("p c n -> p (c n)")[:, bass.ds(t * 2048 + i * 1024, 1024)]

        def next_high(act, i, t, layer):
            act.wait_ge(raw_in[i], raw_count(layer + 1, 0, i) + t * 16)
            nc.scalar.copy(next_piece(i, t)(0), raw[:, i, :]).then_inc(raw_hi, 1)

        def next_low(dve, i, t, layer):
            dve.wait_ge(raw_hi, (layer + 1) * PIECES + t * 2 + i + 1)
            dve.wait_ge(raw_in[i], raw_count(layer + 1, 0, i) + t * 16)
            dst = next_piece(i, t)
            nc.vector.tensor_tensor(dst(1), raw[:, i, :], dst(0).bitcast(F32), ALU.subtract).then_inc(raw_lo, 1)

        def three(pe, out_ap, lhs, rhs, first, last):
            pe.matmul(out_ap, lhs(0), rhs(0), start=first, stop=False)
            pe.matmul(out_ap, lhs(0), rhs(1), start=False, stop=False)
            return pe.matmul(out_ap, lhs(1), rhs(0), start=False, stop=last)

        def xperiods(engine, period, between=lambda i: None):
            period(-1, -1, 1)
            between(0)
            period(0, 0, 1)
            between(2)
            with engine.Fori(0, BATCH // 2 - 1) as two_:
                period(1, two_ * 2 + 1, two_ + 2)
                period(2, two_ * 2 + 2, two_ + 2)
            period(BATCH - 1, BATCH - 1, BATCH // 2 + 1)
            between(4)
            period(BATCH, BATCH, BATCH // 2 + 1)
            between(6)

        def in_xperiod(p, order):
            here = {**dict.fromkeys("STV", 0 <= p < BATCH), **dict.fromkeys("LIKQP", p + 1 < BATCH),
                    **dict.fromkeys("WEN", p >= 1)}
            return [(step[0], int(step[1])) for step in order if here[step[0]]]

        def periods(engine, period, ffn_left, between=lambda i, layer: None):
            def run(layer):
                g0 = layer * UNITS
                for u in range(-2, 4):
                    if u == 0:
                        ffn_left(layer)
                    period(u, g0 + u if u >= 0 else g0, layer, 0)
                    if u >= 0:
                        between(u, layer)
                with engine.Fori(1, BATCH // 2 - 1) as pair:
                    for u in range(4):
                        period(u + 4, g0 + pair * 4 + u, layer, pair)
                for u in range(UNITS - 4, UNITS + 1):
                    period(u, g0 + u, layer, BATCH // 2 - 1)
                    if u < UNITS - 1:
                        between(u - UNITS + 8, layer)
            return run

        def BATCH_OF(unit, pair):
            if isinstance(pair, int):
                return unit // 2
            return pair * 2 + unit // 2 - 2

        def in_period(u, order=PERIOD):
            here = {"S": 0 <= u < UNITS, "T": 0 <= u < UNITS, "V": 0 <= u < UNITS, "Q": u + 2 < UNITS,
                    "K": u + 2 < UNITS, "B": 0 <= u + 1 < UNITS, "C": 0 <= u + 1 < UNITS, "O": u >= 1,
                    "W": u >= 4 and u % 4 == 0, "X": u % 2 == 1 and u + 3 < UNITS,
                    "M": u == UNITS - 1, "R": u == UNITS - 1, "N": u == UNITS}
            return [(step[0], int(step[1:] or 0)) for step in order if here[step[0]]]

        block = stack.enter_context(nc.Block())

        @block.sync
        def _(sp):
            def load_inputs(b, par):
                sp.dma_start(xin[:, par, :], x[b]).then_inc(x_in[par], 16)
                sp.dma_start(cin[:, par, :], ctx_1024[b]).then_inc(x_in[par], 16)
                sp.dma_start(mask8[:, par, :], mask[b]).then_inc(x_in[par], 16)

            load_inputs(0, 0)
            for dst, src in ((ident, eye), (band_f, band)):
                sp.dma_start(dst[:, :], src).then_inc(loaded, 16)
            sp.dma_start(rope_t[:, :, :], rope).then_inc(loaded, 16)
            sp.dma_start(gates[:, 0:1], g_xattn.rearrange("(o n) -> o n", o=1).to_broadcast([P, 1])).then_inc(loaded, 16)
            sp.dma_start(gates[:, 1:2], g_ffn.rearrange("(o n) -> o n", o=1).to_broadcast([P, 1])).then_inc(loaded, 16)
            sp.wait_ge(consts, 1)
            for dst, src, c in ((xwq, Wq, 0), (xwk, Wk, 0), (xwq, Wq, 1), (xwk, Wk, 1)):
                sp.dma_start(dst[:, c, :, 0:XD], src[c * P:(c + 1) * P, :].rearrange("p (h d) -> p h d", h=XH)).then_inc(xw_loaded, 16)
            sp.dma_start(xwv, Wv.rearrange("(c p) n -> p c n", p=P)).then_inc(xw_loaded, 16)
            sp.dma_start(xwo, Wo.rearrange("(c p) n -> p c n", p=P)).then_inc(xw_loaded, 16)
            for a, b in ((0, bq), (1, bk)):
                for j in range(4):
                    sp.dma_start(bqk[32 * j:32 * j + XD, a, :], b.rearrange("(c j d) -> j d c", j=4, d=XD)[j],
                                 allow_slow_non_contiguous=True).then_inc(xw_loaded, 16)
            for a, b in ((0, bv), (1, bo)):
                sp.dma_start(bvo[:, a, :], b.rearrange("(o n) -> o n", o=1).to_broadcast([P, DIM])).then_inc(xw_loaded, 16)
            for b in range(2):
                if b:
                    load_inputs(b, b)
                sp.dma_start(xres[:, b, :], x[b]).then_inc(res_in[b], 16)
            load_pieces(sp, attn_pieces(0), 0, 0, 4)
            for par in range(2):
                sp.sem_inc(x1_out[par], 16)
            def next_inputs(b, par):
                sp.wait_ge(norm1_ok, primed(b + 1))
                sp.wait_ge(xnT_mm, primed(b + 1))
                sp.wait_ge(mask_made, primed(b + 1))
                load_inputs(b + 2, par)

            def store_x1(b, par):
                sp.dma_start(x1_dram[b], x1[:, par, :]).then_inc(x1_out[par], 16)

            def swap_residual(b, par):
                sp.wait_ge(x1_made, primed(b - 1))
                sp.dma_start(xres[:, par, :], x[b]).then_inc(res_in[par], 16)
                store_x1(b - 2, par)

            for par in range(2):
                next_inputs(par, par)
            with sp.Fori(1, BATCH // 2 - 1) as two_:
                for par in range(2):
                    next_inputs(two_ * 2 + par, par)
                    swap_residual(two_ * 2 + par, par)
            load_pieces(sp, attn_pieces(0), 0, 4, 6)
            for par in range(2):
                swap_residual(BATCH - 2 + par, par)
            for par in range(2):
                if par:
                    load_pieces(sp, attn_pieces(0), 0, 6, 8)
                sp.wait_ge(x1_made, primed(BATCH - 1 + par))
                store_x1(BATCH - 2 + par, par)
            for par in range(2):
                sp.wait_ge(x1_out[par], BATCH * 8 + 16)
            def load_scales(layer):
                sp.dma_start(qk_scale[:, 0, :], q_scale[bass.ds(layer, 1), :].to_broadcast([P, DH])).then_inc(qk_in, 16)
                sp.dma_start(qk_scale[:, 1, :], k_scale[bass.ds(layer, 1), :].to_broadcast([P, DH])).then_inc(qk_in, 16)

            load_scales(0)
            with sp.Fori(0, DEPTH) as layer:
                after = sp.snap((layer + 1) % DEPTH)
                ffn_base = sp.snap(layer * PIECES + ATTN_N)
                attn_base = sp.snap(layer * PIECES + PIECES)
                load_pieces(sp, ffn_pieces(layer), ffn_base, 0, 2)
                sp.wait_ge(phase_done, layer * 8 + 8)
                for a, b in ((0, ln_g), (1, ln_b)):
                    sp.dma_start(ln_gb[:, a, :], b[layer].rearrange("(c p) -> p c", p=P), allow_slow_non_contiguous=True).then_inc(vec_in, 16)
                sp.dma_start(b2_t[:, :], b2[layer].rearrange("(c p) -> p c", p=P), allow_slow_non_contiguous=True).then_inc(vec_in, 16)
                for a in range(2):
                    v = b1[layer][a * FF:(a + 1) * FF]
                    sp.dma_start(b1_t[:, a * FULL:(a + 1) * FULL], v[0:FULL * P].rearrange("(c p) -> p c", p=P),
                                 allow_slow_non_contiguous=True).then_inc(vec_in, 16)
                    sp.dma_start(b1_t[a * GATE0:a * GATE0 + REST, 2 * FULL:2 * FULL + 1],
                                 v[FULL * P:FF].rearrange("(p o) -> p o", o=1), allow_slow_non_contiguous=True).then_inc(vec_in, 16)
                load_pieces(sp, ffn_pieces(layer), ffn_base, 2)
                sp.wait_ge(tables, primed(layer + 1))
                load_scales(after)
                load_pieces(sp, attn_pieces(after), attn_base)
            sp.wait_ge(phase_done, DEPTH * 8 + 8)
            def x1_pair(k):
                return x1_dram[bass.ds(k * 2, 2)].rearrange("b p n -> p b n")

            def out_pair(k):
                return out[bass.ds(k * 2, 2)].rearrange("b p n -> p b n")

            for par in range(2):
                sp.dma_start(x_rows[:, par], x1_pair(par)).then_inc(fin_in[par], 16)
            with sp.Fori(0, BATCH // 4 - 1) as two_:
                for par in range(2):
                    k = two_ * 2 + par
                    sp.wait_ge(fin_ok, primed(k + 1))
                    sp.dma_start(out_pair(k), out_rows[:, par]).then_inc(fin_out[par], 16)
                    sp.dma_start(x_rows[:, par], x1_pair(k + 2)).then_inc(fin_in[par], 16)
            for par in range(2):
                sp.wait_ge(fin_ok, primed(BATCH // 2 - 1 + par))
                sp.dma_start(out_pair(BATCH // 2 - 2 + par), out_rows[:, par]).then_inc(fin_out[par], 16)
            for par in range(2):
                sp.wait_ge(fin_out[par], BATCH // 4 * 16)

        @block.tensor
        def _(pe):
            for s in (b_mm, bc_mm, d_mm, fin_mm, mean_mm, o_mm, qk_mm, s_mm, t_mm, u_mm, v_mm, val_mm, var_mm,
                      w_mm, x_mm, xk_mm, xnT_mm, xoT_mm, xpv_mm, xq_mm, xs_mm, xt_mm, xv_mm, xwo_mm):
                pe.sem_inc(s, 1)
            pe.wait_ge(consts, 1)
            pe.wait_ge(consts_act, 1)
            pe.wait_ge(loaded, 80)
            def xperiod(p, b, n):
                par, nxt = p % 2, 1 - p % 2
                for kind, j in in_xperiod(p, XPERIOD):
                    if kind == "S":
                        if j == 0:
                            pe.wait_ge(mask_made, primed(b + 1))
                            pe.wait_ge(xqk_ready, primed(b + 1))
                            pe.wait_ge(xk_ready, primed(b + 1))
                        pe.wait_ge(xs_sub, primed(b * 4 + max(0, j - 1)))
                        pe.matmul(bank[2 + j % 2][:, :], ident_bf[:, :], maskf[:, par, None, :].to_broadcast([P, GROUP, SEQ]),
                                  start=True, stop=True)
                        for i in range(GROUP):
                            r = slice(XPAD * j, XPAD * j + XD)
                            ins = pe.matmul(bank[2 + j % 2][:, i * P:(i + 1) * P], xqk[r, par, 0, i, :], xqk[r, par, 1, i, :],
                                            start=False, stop=True, skip_group_check=True)
                        ins.then_inc(xs_mm, 1)
                    elif kind == "T":
                        pe.wait_ge(xs_exp, primed(b * 4 + j + 1))
                        pe.wait_ge(xpT_copied, primed(b * 4 + j))
                        for i in range(GROUP):
                            ins = pe.transpose(bank[4][:, i * P:(i + 1) * P], xp[:, j % 2, i * P:(i + 1) * P], ident[:, :])
                        ins.then_inc(xt_mm, 1)
                    elif kind in "VW":
                        bb = b if kind == "V" else b - 1
                        if j == 0:
                            pe.wait_ge(xv_ready, primed(b + 1))
                            pe.wait_ge(xo_norm, primed(b))
                        pe.wait_ge(xpT_copied, primed(bb * 4 + j + 1))
                        for i in range(GROUP):
                            o = (GROUP * j + i) * XVA
                            ins = pe.matmul(bank[5][:, o:o + XVA], xpT[:, j % 2, i * P:(i + 1) * P],
                                            xv[:, par if kind == "V" else nxt, 4 * i + j, :], start=True, stop=True)
                        ins.then_inc(xpv_mm, 1)
                    elif kind == "I":
                        pe.wait_ge(norm1_ok, primed(b + 2))
                        pe.wait_ge(x_in[nxt], n * 48)
                        pe.wait_ge(xT_copied, primed(b + 1))
                        for a, src in ((0, cin[:, nxt, :]), (1, xnorm1)):
                            for c in range(KC):
                                k = 2 * a + c
                                ins = pe.transpose(bank[0][:, k * P:(k + 1) * P], src[:, c * P:(c + 1) * P], ident[:, :])
                        ins.then_inc(xnT_mm, 1)
                    elif kind in "KQ":
                        a, w, done = (0, xwk, xk_mm) if kind == "K" else (1, xwq, xq_mm)
                        if kind == "K":
                            if p < 0:
                                pe.wait_ge(xw_loaded, XW_LOADS * 16)
                            pe.wait_ge(xT_copied, primed(b + 2))
                            pe.wait_ge(xqk_ready, primed(b + 1))
                        else:
                            pe.wait_ge(xk_ready, primed(b + 2))
                        for h in range(4):
                            for c in range(KC):
                                ins = pe.matmul(bank[1][:, h * P:(h + 1) * P], w[:, c, 4 * h:4 * h + 4, :], tT[:, a, c, :],
                                                start=(c == 0), stop=(c == KC - 1))
                        ins.then_inc(done, 1)
                    elif kind == "P":
                        pe.wait_ge(xT_copied, primed(b + 2))
                        if p >= 1:
                            pe.wait_ge(x1_made, primed(b - 1))
                        for c in range(KC):
                            ins = pe.matmul(bank[6][:, 0:DIM], tT[:, 0, c, :], xwv[:, c, :], start=(c == 0), stop=(c == KC - 1))
                        ins.then_inc(xv_mm, 1)
                    elif j == 0:
                        pe.wait_ge(xo_norm, primed(b))
                        pe.wait_ge(x_stored, primed(b - 1))
                        for c in range(KC):
                            ins = pe.transpose(bank[7][:, c * P:(c + 1) * P], xo[:, 8 * c:8 * c + 8, :], ident[:, :])
                        ins.then_inc(xoT_mm, 1)
                    elif j == 1:
                        pe.wait_ge(xoT_copied, primed(b))
                        pe.wait_ge(xv_ready, primed(min(p + 2, BATCH) if isinstance(b, int) else b + 2))
                        for c in range(KC):
                            ins = pe.matmul(bank[6][:, 0:DIM], xoT[:, c, :], xwo[:, c, :], start=(c == 0), stop=(c == KC - 1))
                        ins.then_inc(xwo_mm, 1)
                    else:
                        pe.wait_ge(norm2_ok, primed(b))
                        for c in range(KC):
                            ins = pe.transpose(bank[7][:, c * P:(c + 1) * P], xnorm2[:, c * P:(c + 1) * P], ident[:, :])
                        ins.then_inc(x_mm, 1)

            xperiods(pe, xperiod)
            barrier(pe, 0)

            def chunk(bank_out, par, col):
                for k in range(KC):
                    ins = three(pe, bank_out, lambda s: xs[:, par, s, k, :], lambda s: wqkv[:, s, k, col:col + CH],
                                k == 0, k == KC - 1)
                return ins

            def first_chunks(layer):
                pe.wait_ge(raw_lo, layer * PIECES + KC * 3)
                pe.wait_ge(xs_ready, primed(layer * BATCH + 1))
                for n in range(2):
                    chunk(bank[n][:, :], 0, n * INNER).then_inc(qk_mm, 1)

            def period(u, g, layer, pair):
                odd = u % 2
                for kind, e in in_period(u):
                    if kind == "S":
                        pe.wait_ge(b_copied, primed(g * 2 + 2))
                        pe.wait_ge(s_sub, primed(g * 2))
                        b = bank[2 + e]
                        pe.matmul(b[:, :], ident_bf[:, :], band_bf[:, None, :].to_broadcast([P, GROUP, SEQ]),
                                  start=True, stop=True)
                        r = slice(DH * e, DH * e + DH)
                        for i in range(GROUP):
                            cols = slice(i * P, (i + 1) * P)
                            ins = pe.matmul(b[:, cols], qkT[r, 0, cols], qkT[r, 1, cols], start=False, stop=True,
                                            skip_group_check=True)
                        ins.then_inc(s_mm, 1)
                    elif kind in "QK":
                        n = "QK".index(kind)
                        if u == -2:
                            continue
                        nxt = g + 2 if u >= 0 else g + 1
                        if n == 0:
                            pe.wait_ge(xs_ready, primed(layer * BATCH + BATCH_OF(u + 2, pair) + 1))
                            pe.wait_ge(rotated, primed(nxt * 2))
                        else:
                            pe.wait_ge(v_copied, primed(nxt - 1))
                        chunk(bank[(3 * u + n) % 2][:, :], ((u + 2) // 2) % 2, n * INNER + odd * CH).then_inc(qk_mm, 1)
                    elif kind == "C":
                        nxt = g + 1 if u >= 0 else g
                        pe.wait_ge(rotated, primed(nxt * 2 + (3 if u + 2 < UNITS else 2)))
                        chunk(bank[3 * u % 2][:, :], ((u + 1) // 2) % 2, 2 * INNER + (1 - odd) * CH).then_inc(val_mm, 1)
                    elif kind == "B":
                        nxt = g + 1 if u >= 0 else g
                        pe.wait_ge(qk_ready, primed(nxt * 2 + e + 1))
                        pe.wait_ge(b_copied, primed(nxt * 2 + e))
                        if u == -1:
                            pe.wait_ge(f_added, primed(layer * 4))
                        for j in range(4):
                            ins = pe.transpose(bank[4][:, j * P:(j + 1) * P], qkr[:, e, j * P:(j + 1) * P], ident[:, :])
                        ins.then_inc(b_mm, 1)
                    elif kind == "O":
                        pe.wait_ge(o_norm, primed(g * 2))
                        pe.wait_ge(t_copied, primed(g * 2))
                        for i in range(4):
                            h = HPC * (1 - odd) + 2 * i
                            ins = pe.transpose(bank[5][:, i * P:(i + 1) * P], outs[:, h:h + 2, :], ident[:, :])
                        ins.then_inc(o_mm, 1)
                    elif kind == "T":
                        pe.wait_ge(s_exp, primed(g * 2 + e + 1))
                        if e == 0:
                            pe.wait_ge(o_lo, primed(g))
                        else:
                            pe.wait_ge(t_copied, primed(g * 2 + 1))
                        for i in range(GROUP):
                            ins = pe.transpose(bank[5][:, i * P:(i + 1) * P], probs[:, e, i * P:(i + 1) * P], ident[:, :])
                        ins.then_inc(t_mm, 1)
                    elif kind == "V":
                        pe.wait_ge(t_copied, primed(g * 2 + e + 1))
                        pe.wait_ge(v_copied, primed(g + 1))
                        pe.wait_ge(o_norm, primed(g * 2 + e))
                        for i in range(GROUP):
                            ins = pe.matmul(bank[6][:, i * VA:(i + 1) * VA], probsT[:, e, i * P:(i + 1) * P],
                                            vals[:, HPC * odd + 2 * i + e, :], start=True, stop=True)
                        ins.then_inc(v_mm, 1)
                    elif kind == "W":
                        gp = layer * (BATCH // 2) + (pair - 1 if u < UNITS else pair)
                        if e == 0:
                            pe.wait_ge(o_lo, primed(gp * 4 + 4))
                            pe.wait_ge(x_added, primed(gp))
                        for c in range(OC):
                            ins = three(pe, bank[7][:, e * 2 * SEQ:(e + 1) * 2 * SEQ], lambda s: wout[:, s, c, e * P:(e + 1) * P],
                                        lambda s: oT[:, s, c, :], c == 0, c == OC - 1)
                        ins.then_inc(w_mm, 1)

                    elif kind in "MRN":
                        ffn_norm[kind](e, layer * 4, 0)

            run_periods = periods(pe, period, lambda layer: arrive(pe))

            def m_step(k, gt, t):
                mean = bank[norm_banks(t)[0]]
                pe.wait_ge(xn_ok, primed(gt))
                if isinstance(t, int):
                    pe.wait_ge(s_sub, primed(gt * (UNITS * 2 // 4) + UNITS * 2 - 1))
                pe.matmul(mean[:, :], inv_dim[:, :], X0[:, bass.ds(t * 4, 4), :], start=True, stop=False)
                pe.matmul(mean[:, :], inv_dim[:, :], X1[:, bass.ds(t * 4, 4), 0:SEQ], start=False, stop=True).then_inc(mean_mm, 1)

            def r_step(k, gt, t):
                pe.wait_ge(xsq, primed(gt + 1))
                pe.wait_ge(var_ok, primed(gt))
                for j in range(4):
                    for c in range(KC):
                        ins = pe.matmul(bank[norm_banks(t)[1]][:, j:j + 1], xq[:, c, j * P:(j + 1) * P], inv_dim[:, 0:1],
                                        start=(c == 0), stop=(c == KC - 1))
                ins.then_inc(var_mm, 1)

            def n_step(k, gt, t):
                if k:
                    return
                pe.wait_ge(rstd_ok, primed(gt + 1))
                pe.wait_ge(centred, primed(gt + 1))
                spread = bank[norm_banks(t)[2]]
                for j in range(4):
                    ins = pe.matmul(spread[:, j * P:(j + 1) * P], rstd4[:, j:j + 1].to_broadcast([P, P]), ident[:, :],
                                    start=True, stop=True)
                ins.then_inc(bc_mm, 1)

            def u_step(m, gt, alone=False):
                if m == 0:
                    pe.wait_ge(xn_lo, primed(gt + 1))
                if m or not alone:
                    pe.wait_ge(h_ok, primed(gt * 6 + m - 1))
                for a in range(2 if m < FULL else 1):
                    rows = P if m < FULL else GATE0 + REST
                    for c in range(KC):
                        ins = three(pe, bank[2 * (m % 2) + a][0:rows, :], lambda s: w1[:, s, c, a * FULL + m if m < FULL else 2 * FULL, 0:rows],
                                    lambda s: xn_parts[:, s, c, :], c == 0, c == KC - 1)
                ins.then_inc(u_mm, 1)

            def d_step(m, gt):
                pe.wait_ge(h_lo, primed(gt * 6 + m + 1))
                if m == 0:
                    pe.wait_ge(f_added, primed(gt))
                rows = P if m < FULL else REST
                for o in range(KC):
                    ins = three(pe, bank[4 + o][:, :], lambda s: w2[0:rows, s, m, o * P:(o + 1) * P],
                                lambda s: h_parts[m % 3][0:rows, s, :], m == 0, m == FULL)
                ins.then_inc(d_mm, 1)

            def feed(gt, nxt, t, layer):
                for kind, n in FFN_STEPS:
                    if kind in "UD":
                        {"U": u_step, "D": d_step}[kind](n, gt)
                    elif kind == "F" and nxt is not None:
                        u_step(0, nxt)
                    elif kind == "F":
                        pe.wait_ge(h_ok, primed(gt * 6 + FULL))
                        first_chunks(layer + 1)
                    elif nxt is not None and kind != "S":
                        ffn_norm[kind](n, nxt, t + 1)

            ffn_norm = {"M": m_step, "R": r_step, "N": n_step}
            first_chunks(0)
            with pe.Fori(0, DEPTH) as layer:
                pe.wait_ge(raw_lo, layer * PIECES + ATTN_N)
                run_periods(layer)
                pe.wait_ge(raw_lo, layer * PIECES + PIECES)
                u_step(0, layer * 4, True)
                arrive(pe)
                with pe.Fori(0, 3) as t:
                    feed(layer * 4 + t, layer * 4 + t + 1, t, layer)
                feed(layer * 4 + 3, None, 3, layer)
            arrive(pe)
            with pe.Fori(0, BATCH // 4) as two_:
                for par in range(2):
                    pe.wait_ge(fin_copied, primed(two_ * 2 + par + 1))
                    pe.wait_ge(fin_ok, primed(two_ * 2))
                    for b in range(2):
                        for c in range(KC):
                            ins = pe.transpose(bank[par][:, b * DIM + c * P:b * DIM + (c + 1) * P],
                                               x_cols[:, par, c, b * P:(b + 1) * P], ident[:, :])
                    ins.then_inc(fin_mm, 1)

        @block.scalar
        def _(act):
            for s in (b_copied, fin_copied, gelu_ok, h_hi, o_hi, s_exp, squared, t_copied, v_copied, xT_copied, xg_ok,
                      x_stored, xk_ready, xoT_copied, xpT_copied, xqk_ready, xs_exp, xsq):
                act.sem_inc(s, 1)
            act.wait_ge(loaded, 80)
            nc.scalar.copy(ident_bf[:, :], ident[:, :])
            nc.scalar.activation(gates[:, 2:4], gates[:, 0:2], ACT.Tanh)
            nc.scalar.copy(band_bf[:, :], band_f[:, :]).then_inc(consts_act, 1)
            act.wait_ge(consts, 1)
            def xperiod(p, b, n):
                for kind, j in in_xperiod(p, ACT_XPERIOD):
                    if kind == "S":
                        act.wait_ge(xs_sub, primed(b * 4 + j + 1))
                        nc.scalar.activation(xp[:, j % 2, :], xp[:, j % 2, :], ACT.Exp, scale=XD ** -0.5).then_inc(xs_exp, 1)
                    elif kind == "T":
                        act.wait_ge(xt_mm, primed(b * 4 + j + 1))
                        act.wait_ge(xpv_mm, primed(b * 4 + max(0, j - 1)))
                        nc.scalar.copy(xpT[:, j % 2, :], bank[4][:, :]).then_inc(xpT_copied, 1)
                    elif kind == "I":
                        act.wait_ge(xnT_mm, primed(b + 2))
                        act.wait_ge(xq_mm, primed(b + 1))
                        nc.scalar.copy(tT[:, :, :, :], bank[0][:, :]).then_inc(xT_copied, 1)
                    elif kind in "KQ":
                        a, done, ready = (1, xk_mm, xk_ready) if kind == "K" else (0, xq_mm, xqk_ready)
                        if p < 0:
                            act.wait_ge(xw_loaded, XW_LOADS * 16)
                        act.wait_ge(done, primed(b + 2))
                        if p >= 1:
                            act.wait_ge(xs_mm, primed(b * 4))
                        for i in range(4):
                            ins = nc.scalar.activation(xqk[:, 1 - p % 2, a, i, :], bank[1][:, i * P:(i + 1) * P], ACT.Identity,
                                                       bias=bqk[:, a, i:i + 1])
                        ins.then_inc(ready, 1)
                    elif j == 0:
                        act.wait_ge(xoT_mm, primed(b))
                        act.wait_ge(xwo_mm, primed(b - 1))
                        nc.scalar.copy(xoT[:, :, :], bank[7][:, 0:DIM]).then_inc(xoT_copied, 1)
                    elif j == 2:
                        act.wait_ge(x_mm, primed(b))
                        at = bass.ds(b - 1, 1)
                        nc.scalar.copy(X0[:, at, :], bank[7][:, 0:P])
                        nc.scalar.copy(X1[:, at, 1:SEQ + 1], bank[7][:, P:2 * P]).then_inc(x_stored, 1)

            xperiods(act, xperiod, lambda i: high_parts(act, attn_pieces(0), 0, 0, i, i + 2))
            barrier(act, 0)

            def first_squares(layer):
                for n in range(2):
                    act.wait_ge(qk_mm, primed(layer * UNITS * 2 + n + 1))
                    nc.scalar.square(sq[:, n, :], bank[n][:, :]).then_inc(squared, 1)

            def period(u, g, layer, pair):
                for kind, e in in_period(u, ACT_PERIOD):
                    if kind == "S":
                        act.wait_ge(s_sub, primed(g * 2 + e + 1))
                        nc.scalar.activation(probs[:, e, :], probs[:, e, :], ACT.Exp, scale=8.0).then_inc(s_exp, 1)
                    elif kind in "QK":
                        n = "QK".index(kind)
                        if u == -2:
                            continue
                        nxt = g + 2 if u >= 0 else g + 1
                        act.wait_ge(qk_mm, primed(nxt * 2 + n + 1))
                        act.wait_ge(norms, primed(nxt * 2 - 1 + n))
                        nc.scalar.square(sq[:, n, :], bank[(3 * u + n) % 2][:, :]).then_inc(squared, 1)
                    elif kind == "C":
                        nxt = g + 1 if u >= 0 else g
                        act.wait_ge(val_mm, primed(nxt + 1))
                        if u > -1:
                            act.wait_ge(v_mm, primed(nxt * 2 - 2))
                        h = HPC * ((u + 1) % 2)
                        nc.scalar.copy(vals[:, h:h + HPC, 0:DH],
                                       bank[3 * u % 2][:, :].rearrange("p (h d) -> p h d", h=HPC)).then_inc(v_copied, 1)
                    elif kind == "B":
                        nxt = g + 1 if u >= 0 else g
                        act.wait_ge(b_mm, primed(nxt * 2 + e + 1))
                        act.wait_ge(s_mm, primed(nxt * 2))
                        nc.scalar.copy(qkT[:, e, :], bank[4][:, :]).then_inc(b_copied, 1)
                    elif kind == "O":
                        act.wait_ge(o_mm, primed(g))
                        if u % 4 == 1:
                            act.wait_ge(w_mm, primed((layer * (BATCH // 2) + pair) * 2))
                        k, half_ = (u - 1) % 2, (u - 1) // 2 % 2
                        nc.scalar.copy(oT[:, 0, 4 * k:4 * k + 4, half_ * SEQ:(half_ + 1) * SEQ],
                                       bank[5][:, :].rearrange("p (c t) -> p c t", c=4)).then_inc(o_hi, 1)
                    elif kind == "T":
                        act.wait_ge(t_mm, primed(g * 2 + e + 1))
                        act.wait_ge(v_mm, primed(g * 2))
                        nc.scalar.copy(probsT[:, e, :], bank[5][:, :]).then_inc(t_copied, 1)

                    elif kind in "MN":
                        if kind == "N":
                            act.wait_ge(vec_in, (layer + 1) * VECTORS * 16)
                        ln_steps(kind, e, layer * 4)

            run_periods = periods(act, period, lambda layer: barrier(act, layer * 2 + 1),
                                  lambda i, layer: high_parts(act, ffn_pieces(0), layer, 1, i, i + 1))

            def ln_steps(kind, k, gt):
                if kind == "M":
                    act.wait_ge(centred, primed(gt + 1))
                    act.wait_ge(var_mm, primed(gt))
                    nc.scalar.square(xq[:, :, :], xc[:, :, :]).then_inc(xsq, 1)
                elif kind == "N" and k == 1:
                    act.wait_ge(xn_ok, primed(gt + 1))
                    act.wait_ge(xn_lo, primed(gt))
                    for c in range(KC):
                        ins = nc.scalar.activation(xg[:, c, :], xq[:, c, :], ACT.Identity, bias=ln_gb[:, 1, c:c + 1],
                                                   scale=ln_gb[:, 0, c:c + 1])
                    ins.then_inc(xg_ok, 1)

            def u_step(m, gt):
                act.wait_ge(u_mm, primed(gt * 6 + m + 1))
                act.wait_ge(h_ok, primed(gt * 6 + max(0, m - 1)))
                if m < FULL:
                    ins = nc.scalar.activation(gelu[:, m % 2, :], bank[2 * (m % 2) + 1][:, :], ACT.Gelu,
                                               bias=b1_t[:, FULL + m:FULL + m + 1])
                else:
                    r = slice(GATE0, GATE0 + REST)
                    ins = nc.scalar.activation(gelu[0:REST, m % 2, :], bank[2 * (m % 2)][r, :], ACT.Gelu,
                                               bias=b1_t[r, 2 * FULL:2 * FULL + 1])
                ins.then_inc(gelu_ok, 1)

            def h_high(m, gt):
                rows = P if m < FULL else REST
                act.wait_ge(h_ok, primed(gt * 6 + m + 1))
                act.wait_ge(d_mm, primed(gt * 6 + max(0, m - 2)))
                nc.scalar.copy(h_parts[m % 3][0:rows, 0, :], hf[0:rows, m % 2, :]).then_inc(h_hi, 1)

            def feed(gt, nxt, t, layer):
                for kind, n in FFN_STEPS:
                    if kind == "U":
                        u_step(n, gt)
                        h_high(n, gt)
                    elif kind == "S":
                        next_high(act, n, t, layer)
                    elif kind == "F" and nxt is not None:
                        u_step(0, nxt)
                        h_high(0, nxt)
                    elif kind == "F":
                        first_squares(layer + 1)
                    elif kind in "MRN" and nxt is not None:
                        ln_steps(kind, n, nxt)

            first_squares(0)
            with act.Fori(0, DEPTH) as layer:
                run_periods(layer)
                barrier(act, layer * 2 + 2)
                u_step(0, layer * 4)
                h_high(0, layer * 4)
                with act.Fori(0, 3) as t:
                    feed(layer * 4 + t, layer * 4 + t + 1, t, layer)
                feed(layer * 4 + 3, None, 3, layer)
            barrier(act, DEPTH * 2 + 1)
            with act.Fori(0, BATCH // 4) as two_:
                for par in range(2):
                    act.wait_ge(fin_mm, primed(two_ * 2))
                    pair = bass.ds(two_ * 4 + par * 2, 2)
                    nc.scalar.copy(x_cols[:, par, 0].rearrange("p (b t) -> p b t", b=2), X0[:, pair, :])
                    nc.scalar.copy(x_cols[:, par, 1].rearrange("p (b t) -> p b t", b=2),
                                   X1[:, pair, 1:SEQ + 1]).then_inc(fin_copied, 1)

        @block.vector
        def _(dve):
            for s in (centred, f_added, fin_ok, h_lo, h_ok, link1, link2, mask_made, norm1_ok,
                      norm2_ok, norm_sum, norms, o_lo, o_norm, r_sum, rotated, s_max, s_sub, var1, var2, var_ok,
                      x1_made, x1_sum, x_added, xmax_ok, xn_hi, xn_lo, xn_ok, xo_norm, xs_hi,
                      xs_ready, xs_sub, xsum_ok, xv_ready, tables):
                dve.sem_inc(s, 1)
            nc.vector.memset(padded, 0.0).then_inc(cleared, 1)
            dve.wait_ge(cleared, 1)
            nc.vector.memset(inv_dim[:, :], 1.0 / DIM)
            nc.vector.memset(X1[:, :, 0:1], 0.0)
            nc.vector.memset(b1_t[:, :], 0.0)
            nc.vector.memset(w1[:, :, :, 2 * FULL, REST:GATE0].bitcast(F32), 0.0)
            nc.vector.memset(xv[:, :, :, XD:XVA], 1.0).then_inc(consts, 1)
            dve.wait_ge(consts_act, 1)
            dve.wait_ge(consts, 1)
            def centre(src, mean, cent, scratch, link, base, ready):
                nc.vector.tensor_reduce(mean[:, 0:1], src, AX_X, ALU.add).then_inc(link, 1)
                dve.wait_ge(link, primed(base + 1))
                nc.vector.tensor_scalar(mean[:, 0:1], mean[:, 0:1], 1.0 / DIM, None, ALU.mult).then_inc(link, 1)
                dve.wait_ge(link, primed(base + 2))
                nc.vector.tensor_scalar(cent, src, mean[:, 0:1], None, ALU.subtract).then_inc(link, 1)
                dve.wait_ge(link, primed(base + 3))
                nc.vector.tensor_tensor_reduce(out=scratch, in0=cent, in1=cent, scale=1.0 / DIM, scalar=1e-5,
                                               op0=ALU.mult, op1=ALU.add, accum_out=mean[:, 1:2]).then_inc(ready, 1)

            def xperiod(p, b, n):
                par, nxt = p % 2, 1 - p % 2
                for kind, j in in_xperiod(p, DVE_XPERIOD):
                    if kind == "S":
                        dve.wait_ge(xs_mm, primed(b * 4 + j + 1))
                        s3 = bank[2 + j % 2][:, :].rearrange("p (h t) -> p h t", h=GROUP)
                        nc.vector.tensor_reduce(xmax[:, j], s3, AX_X, ALU.max).then_inc(xmax_ok, 1)
                        dve.wait_ge(xmax_ok, primed(b * 4 + j + 1))
                        dve.wait_ge(xt_mm, primed(b * 4 + max(0, j - 1)))
                        nc.vector.tensor_tensor(xp[:, j % 2, :].rearrange("p (h t) -> p h t", h=GROUP), s3,
                                                xmax[:, j, :, None].to_broadcast([P, GROUP, SEQ]), ALU.subtract).then_inc(xs_sub, 1)
                    elif kind == "W":
                        dve.wait_ge(xpv_mm, primed(b * 4))
                        dve.wait_ge(xoT_mm, primed(b - 1))
                        o4 = bank[5][:, 0:XH * XVA].rearrange("p (j i d) -> p j i d", j=4, i=GROUP)
                        nc.vector.reciprocal(xsum, o4[:, :, :, XD]).then_inc(xsum_ok, 1)
                        dve.wait_ge(xsum_ok, primed(b))
                        nc.vector.tensor_tensor(xo.rearrange("p (i j) d -> p j i d", j=4), o4[:, :, :, 0:XD],
                                                xsum[:, :, :, None].to_broadcast([P, 4, GROUP, XD]), ALU.mult).then_inc(xo_norm, 1)
                    elif kind == "L" and j == 0:
                        dve.wait_ge(x_in[nxt], n * 48)
                        if p >= 0:
                            dve.wait_ge(xnT_mm, primed(b + 1))
                        centre(xin[:, nxt, :], mean1, cent1, xnorm1, link1, b * 3 + 3, var1)
                        if p >= 1:
                            dve.wait_ge(xs_mm, primed(b * 4))
                        nc.vector.tensor_scalar(maskf[:, nxt, :], mask8[:, nxt, :], NEG_INF, None, ALU.mult).then_inc(mask_made, 1)
                    elif kind == "L":
                        dve.wait_ge(rstd1, primed(b + 2))
                        nc.vector.tensor_scalar(xnorm1, cent1, xr1, None, ALU.mult).then_inc(norm1_ok, 1)
                    elif kind == "P":
                        if p < 0:
                            dve.wait_ge(xw_loaded, XW_LOADS * 16)
                        dve.wait_ge(xv_mm, primed(b + 2))
                        if p >= 1:
                            dve.wait_ge(xpv_mm, primed(b * 4))
                        nc.vector.tensor_tensor(xv[:, nxt, :, 0:XD], bank[6][:, 0:DIM].rearrange("p (h d) -> p h d", h=XH),
                                                bvo[:, 0, :].rearrange("p (h d) -> p h d", h=XH), ALU.add).then_inc(xv_ready, 1)
                    elif kind == "N" and j == 0:
                        dve.wait_ge(xwo_mm, primed(b))
                        dve.wait_ge(res_in[nxt], n * 16 - 16)
                        dve.wait_ge(x1_out[nxt], n * 16 - 16)
                        nc.vector.tensor_tensor(x1[:, nxt, :], bank[6][:, 0:DIM], bvo[:, 1, :], ALU.add).then_inc(x1_sum, 1)
                        dve.wait_ge(x1_sum, primed(b))
                        nc.vector.scalar_tensor_tensor(out=x1[:, nxt, :], in0=x1[:, nxt, :], scalar=gates[:, 2:3],
                                                       in1=xres[:, nxt, :], op0=ALU.mult, op1=ALU.add).then_inc(x1_made, 1)
                        dve.wait_ge(x1_made, primed(b))
                        dve.wait_ge(x_mm, primed(b - 1))
                        centre(x1[:, nxt, :], mean2, cent2, xnorm2, link2, b * 3 - 3, var2)
                    elif kind == "N":
                        dve.wait_ge(rstd2, primed(b))
                        nc.vector.tensor_scalar(xnorm2, cent2, xr2, None, ALU.mult).then_inc(norm2_ok, 1)

            xperiods(dve, xperiod, lambda i: low_parts(dve, attn_pieces(0), 0, 0, i, i + 2))
            barrier(dve, 0)
            nc.vector.memset(vals[:, :, DH:VA], 1.0)

            def x_step(par, b, layer, reuse):
                if reuse is not None:
                    dve.wait_ge(val_mm, primed(reuse))
                nc.vector.tensor_copy(xs[:, par, 0, 0, :], X0[:, bass.ds(b, 1), :])
                nc.vector.tensor_copy(xs[:, par, 0, 1, :], X1[:, bass.ds(b, 1), 0:SEQ]).then_inc(xs_hi, 1)
                dve.wait_ge(xs_hi, primed(layer * BATCH + b + 1))
                nc.vector.tensor_tensor(xs[:, par, 1, 0, :], X0[:, bass.ds(b, 1), :], xs[:, par, 0, 0, :].bitcast(F32), ALU.subtract)
                nc.vector.tensor_tensor(xs[:, par, 1, 1, :], X1[:, bass.ds(b, 1), 0:SEQ], xs[:, par, 0, 1, :].bitcast(F32),
                                        ALU.subtract).then_inc(xs_ready, 1)

            def rotate(n, src, nxt, first):
                dve.wait_ge(squared, primed(nxt * 2 + n + 1))
                if not first:
                    dve.wait_ge(rope_sum, primed(nxt * 2 - 1 + n))
                src = src.rearrange("p (h d) -> p h d", h=HPC)
                d1 = m1[:, n, :].rearrange("p (h d) -> p h d", h=HPC)
                d2 = m2[:, n, :].rearrange("p (h d) -> p h d", h=HPC)
                cos, sin = rope_q[:, n, 0, :], rope_q[:, n, 1, :]
                for a, b in ((0, HALF), (HALF, 0)):
                    nc.vector.tensor_tensor(d2[:, :, a:a + HALF], src[:, :, b:b + HALF],
                                            sin[:, None, a:a + HALF].to_broadcast([P, HPC, HALF]), ALU.mult)
                nc.vector.tensor_tensor(d1, src, cos[:, None, :].to_broadcast([P, HPC, DH]), ALU.mult).then_inc(rotated, 1)
                if not first:
                    dve.wait_ge(rnorms, primed(nxt * 2 - 1 + n))
                nc.vector.tensor_reduce(norm2[:, n, :], sq[:, n, :].rearrange("p (h d) -> p h d", h=HPC), AX_X,
                                        ALU.add).then_inc(norm_sum, 1)
                dve.wait_ge(norm_sum, primed(nxt * 2 + n + 1))
                nc.vector.tensor_scalar(norm2[:, n, :], norm2[:, n, :], 1e-24, None, ALU.max).then_inc(norms, 1)

            def make_tables(layer):
                dve.wait_ge(qk_in, (layer + 1) * 32)
                for a in range(2):
                    nc.vector.tensor_tensor(rope_q[:, a, 0, :], rope_t[:, 2 * a, :], qk_scale[:, a, :], ALU.mult)
                    for lo, hi in ((0, HALF), (HALF, 0)):
                        ins = nc.vector.tensor_tensor(rope_q[:, a, 1, lo:lo + HALF], rope_t[:, 2 * a + 1, lo:lo + HALF],
                                                      qk_scale[:, a, hi:hi + HALF], ALU.mult)
                ins.then_inc(tables, 1)
                dve.wait_ge(tables, primed(layer + 1))
            def first_rotations(layer):
                for n in range(2):
                    rotate(n, bank[n][:, :], layer * UNITS, True)

            def period(u, g, layer, pair):
                odd = u % 2
                for kind, e in in_period(u, DVE_PERIOD):
                    if kind == "S":
                        dve.wait_ge(s_mm, primed(g * 2 + e + 1))
                        s3 = bank[2 + e][:, :].rearrange("p (h t) -> p h t", h=GROUP)
                        nc.vector.tensor_reduce(smax[:, e, :], s3, AX_X, ALU.max).then_inc(s_max, 1)
                        dve.wait_ge(s_max, primed(g * 2 + e + 1))
                        dve.wait_ge(t_mm, primed(g * 2))
                        nc.vector.tensor_tensor(probs[:, e, :].rearrange("p (h t) -> p h t", h=GROUP), s3,
                                                smax[:, e, :, None].to_broadcast([P, GROUP, SEQ]), ALU.subtract).then_inc(s_sub, 1)
                    elif kind in "QK":
                        n = "QK".index(kind)
                        if u > -2:
                            rotate(n, bank[(3 * u + n) % 2][:, :], g + 2 if u >= 0 else g + 1, False)
                    elif kind == "O":
                        dve.wait_ge(o_hi, primed(g))
                        k, half_ = (u - 1) % 2, (u - 1) // 2 % 2
                        cols = slice(half_ * SEQ, (half_ + 1) * SEQ)
                        nc.vector.tensor_tensor(oT[:, 1, 4 * k:4 * k + 4, cols], bank[5][:, :].rearrange("p (c t) -> p c t", c=4),
                                                oT[:, 0, 4 * k:4 * k + 4, cols].bitcast(F32), ALU.subtract).then_inc(o_lo, 1)
                    elif kind == "V":
                        dve.wait_ge(v_mm, primed(g * 2 + e + 1))
                        o3 = bank[6][:, 0:GROUP * VA].rearrange("p (h d) -> p h d", h=GROUP)
                        nc.vector.reciprocal(rsum[:, e, :], o3[:, :, DH]).then_inc(r_sum, 1)
                        dve.wait_ge(r_sum, primed(g * 2 + e + 1))
                        dst = outs[:, HPC * odd:HPC * odd + HPC, :].rearrange("p (i e) d -> p i e d", e=2)[:, :, e, :]
                        nc.vector.tensor_tensor(dst, o3[:, :, 0:DH], rsum[:, e, :, None].to_broadcast([P, GROUP, DH]),
                                                ALU.mult).then_inc(o_norm, 1)
                    elif kind == "W" and e == 1:
                        p = pair - 1 if u < UNITS else pair
                        dve.wait_ge(w_mm, primed((layer * (BATCH // 2) + p) * 2 + 2))
                        a0, a1 = X0[:, bass.ds(p * 2, 2), :], X1[:, bass.ds(p * 2, 2), 1:SEQ + 1]
                        y = bank[7][:, :].rearrange("p (m b t) -> p m b t", m=KC, b=2)
                        nc.vector.tensor_tensor(a0, a0, y[:, 0], ALU.add)
                        nc.vector.tensor_tensor(a1, a1, y[:, 1], ALU.add).then_inc(x_added, 1)
                    elif kind == "X":
                        nb = BATCH_OF(u + 3, pair)
                        x_step(((u + 3) // 2) % 2, nb, layer, g + 1 if u >= 0 else g)

                    elif kind in "MRN":
                        ln_steps(kind, e, layer * 4, 0)

            run_periods = periods(dve, period, lambda layer: barrier(dve, layer * 2 + 1),
                                  lambda i, layer: low_parts(dve, ffn_pieces(0), layer, 1, i, i + 1))

            def ln_steps(kind, k, gt, t):
                means, variances, spread = [bank[n] for n in norm_banks(t)]
                if kind == "M":
                    dve.wait_ge(mean_mm, primed(gt + 1))
                    nc.vector.tensor_tensor(xc[:, 0, :].rearrange("p (b t) -> p b t", b=4), X0[:, bass.ds(t * 4, 4), :],
                                            means[:, :].rearrange("p (b t) -> p b t", b=4), ALU.subtract)
                    nc.vector.tensor_tensor(xc[:, 1, :].rearrange("p (b t) -> p b t", b=4), X1[:, bass.ds(t * 4, 4), 0:SEQ],
                                            means[:, :].rearrange("p (b t) -> p b t", b=4), ALU.subtract).then_inc(centred, 1)
                elif kind == "R":
                    dve.wait_ge(var_mm, primed(gt + 1))
                    dve.wait_ge(rstd_ok, primed(gt))
                    nc.vector.tensor_scalar(var4, variances[:, 0:4], 1e-5, None, ALU.add).then_inc(var_ok, 1)
                elif kind == "N" and k == 0:
                    dve.wait_ge(bc_mm, primed(gt + 1))
                    dve.wait_ge(centred, primed(gt + 1))
                    dve.wait_ge(var_mm, primed(gt + 1))
                    nc.vector.tensor_tensor(xq, xc, spread[:, None, :].to_broadcast([P, KC, TOK]), ALU.mult).then_inc(xn_ok, 1)
                elif kind == "N" and k == 2:
                    dve.wait_ge(xg_ok, primed(gt + 1))
                    dve.wait_ge(u_mm, primed(gt * 6))
                    nc.vector.tensor_copy(xn_parts[:, 0], xg).then_inc(xn_hi, 1)
                    dve.wait_ge(xn_hi, primed(gt + 1))
                    nc.vector.tensor_tensor(xn_parts[:, 1], xg, xn_parts[:, 0].bitcast(F32), ALU.subtract).then_inc(xn_lo, 1)

            def u_step(m, gt):
                rows = P if m < FULL else REST
                col = m if m < FULL else 2 * FULL
                dve.wait_ge(gelu_ok, primed(gt * 6 + m + 1))
                dve.wait_ge(h_lo, primed(gt * 6 + max(0, m - 1)))
                nc.vector.scalar_tensor_tensor(out=hf[0:rows, m % 2, :], in0=bank[2 * (m % 2)][0:rows, :],
                                               scalar=b1_t[0:rows, col:col + 1], in1=gelu[0:rows, m % 2, :],
                                               op0=ALU.add, op1=ALU.mult).then_inc(h_ok, 1)
                dve.wait_ge(h_hi, primed(gt * 6 + m + 1))
                nc.vector.tensor_tensor(h_parts[m % 3][0:rows, 1, :], hf[0:rows, m % 2, :],
                                        h_parts[m % 3][0:rows, 0, :].bitcast(F32), ALU.subtract).then_inc(h_lo, 1)

            def add_ffn(gt, t):
                dve.wait_ge(d_mm, primed(gt * 6 + 6))
                a0, a1 = X0[:, bass.ds(t * 4, 4), :], X1[:, bass.ds(t * 4, 4), 1:SEQ + 1]
                for o, a in enumerate((a0, a1)):
                    ins = nc.vector.scalar_tensor_tensor(out=a, in0=bank[4 + o][:, :].rearrange("p (b t) -> p b t", b=4),
                                                         scalar=b2_t[:, o:o + 1], in1=a, op0=ALU.add, op1=ALU.add)
                ins.then_inc(f_added, 1)

            def feed(gt, nxt, t, layer):
                for kind, n in FFN_STEPS:
                    if kind == "U":
                        u_step(n, gt)
                    elif kind == "D":
                        if n == FULL:
                            add_ffn(gt, t)
                    elif kind == "S":
                        next_low(dve, n, t, layer)
                    elif kind == "F" and nxt is not None:
                        u_step(0, nxt)
                    elif kind == "F":
                        first_rotations(layer + 1)
                    elif kind in "MRN" and nxt is not None:
                        ln_steps(kind, n, nxt, t + 1)
                    elif kind == "M":
                        x_step(0, 0, layer + 1, None)
                        make_tables(layer + 1)

            x_step(0, 0, 0, None)
            make_tables(0)
            first_rotations(0)
            with dve.Fori(0, DEPTH) as layer:
                run_periods(layer)
                barrier(dve, layer * 2 + 2)
                dve.wait_ge(vec_in, (layer + 1) * VECTORS * 16)
                u_step(0, layer * 4)
                with dve.Fori(0, 3) as t:
                    feed(layer * 4 + t, layer * 4 + t + 1, t, layer)
                feed(layer * 4 + 3, None, 3, layer)

            barrier(dve, DEPTH * 2 + 1)

            def finish(k, par, two_):
                dve.wait_ge(fin_mm, primed(k + 1))
                dve.wait_ge(fin_in[par], two_ * 16 + 16)
                if not isinstance(two_, int):
                    dve.wait_ge(fin_out[par], two_ * 16)
                nc.vector.scalar_tensor_tensor(out=out_rows[:, par], in0=bank[par][:, :].rearrange("p (b n) -> p b n", b=2),
                                               scalar=gates[:, 3:4], in1=x_rows[:, par], op0=ALU.mult,
                                               op1=ALU.add).then_inc(fin_ok, 1)

            for par in range(2):
                finish(par, par, 0)
            with dve.Fori(1, BATCH // 4) as two_:
                for par in range(2):
                    finish(two_ * 2 + par, par, two_)

        @block.gpsimd
        def _(pool):
            for s in (qk_ready, rnorms, rope_sum, rstd1, rstd2, rstd_ok):
                pool.sem_inc(s, 1)
            nc.gpsimd.memset(half[:, :], -0.5).then_inc(half_ok, 1)
            pool.wait_ge(half_ok, 1)
            def xperiod(p, b, n):
                for kind, j in in_xperiod(p, ["L0", "N0"]):
                    if kind == "L":
                        pool.wait_ge(var1, primed(b + 2))
                        nc.gpsimd.tensor_tensor(xr1, mean1[:, 1:2], half[:, 0:1], ALU.pow).then_inc(rstd1, 1)
                    else:
                        pool.wait_ge(var2, primed(b))
                        nc.gpsimd.tensor_tensor(xr2, mean2[:, 1:2], half[:, 0:1], ALU.pow).then_inc(rstd2, 1)

            xperiods(pool, xperiod)
            barrier(pool, 0)

            def finish(n, g, first):
                pool.wait_ge(rotated, primed(g * 2 + n + 1))
                if not first:
                    pool.wait_ge(b_mm, primed(g * 2 - 1 + n))
                nc.gpsimd.tensor_tensor(qkr[:, n, :], m1[:, n, :], m2[:, n, :], ALU.add).then_inc(rope_sum, 1)
                pool.wait_ge(norms, primed(g * 2 + n + 1))
                if not first:
                    pool.wait_ge(qk_ready, primed(g * 2 - 1 + n))
                nc.gpsimd.tensor_tensor(rnorm[:, n, :], norm2[:, n, :], half[:, 0:HPC], ALU.pow).then_inc(rnorms, 1)
                pool.wait_ge(rnorms, primed(g * 2 + n + 1))
                pool.wait_ge(rope_sum, primed(g * 2 + n + 1))
                q3 = qkr[:, n, :].rearrange("p (h d) -> p h d", h=HPC)
                nc.gpsimd.tensor_tensor(q3, q3, rnorm[:, n, :, None].to_broadcast([P, HPC, DH]), ALU.mult).then_inc(qk_ready, 1)

            with pool.Fori(0, DEPTH) as layer:
                for n in range(2):
                    finish(n, layer * UNITS, True)
                arrive(pool)
                with pool.Fori(1, UNITS) as u:
                    for n in range(2):
                        finish(n, layer * UNITS + u, False)
                for t in range(4):
                    gt = layer * 4 + t
                    if t == 1:
                        arrive(pool)
                    pool.wait_ge(var_ok, primed(gt + 1))
                    pool.wait_ge(bc_mm, primed(gt))
                    nc.gpsimd.tensor_tensor(rstd4, var4, half[:, 0:4], ALU.pow).then_inc(rstd_ok, 1)

            arrive(pool)

_INS = ['x', 'ctx_1024', 'mask_BxSxS2_bf0', 'g_xattn', 'g_ffn', 'L0_xattn_Wq', 'L0_xattn_bq', 'L0_xattn_Wk',
        'L0_xattn_bk', 'L0_xattn_Wv', 'L0_xattn_bv', 'L0_xattn_Wo', 'L0_xattn_bo', 'L0_ffn_Wqkv', 'L0_ffn_q_scale',
        'L0_ffn_k_scale', 'L0_ffn_Wo', 'L0_ffn_ln_g', 'L0_ffn_ln_b', 'L0_ffn_W1', 'L0_ffn_b1', 'L0_ffn_W2', 'L0_ffn_b2']


def shape_constants():
    f = np.float32
    half = np.arange(0, DH, 2, dtype=f)
    freqs = np.arange(SEQ, dtype=f)[:, None] * (f(1.0) / f(10000.0) ** (half / f(DH)))[None, :]
    power = (np.arange(SEQ, dtype=f) - f(SEQ // 2)) / f(WINDOW // 2)
    scale = ((half + f(0.4 * DH)) / f(1.4 * DH))[None, :] ** power[:, None]
    cos, sin = np.cos(freqs), np.sin(freqs)
    signed = lambda a: np.concatenate([-a, a], -1)
    twice = lambda a: np.concatenate([a, a], -1)
    rope = np.stack([twice(cos * scale), signed(sin * scale), twice(cos / scale), signed(sin / scale)], 1).astype(f)
    i, j = np.arange(SEQ)[:, None], np.arange(SEQ)[None, :]
    band = np.where((i < j) | (i > j + WINDOW), f(NEG_MASK), f(0)).astype(f)
    return {"rope": rope, "band": band, "eye": np.eye(P, dtype=f)}


def kernel(**inputs):
    import concourse.bacc as _bacc
    from concourse.bass_utils import run_bass_kernel_spmd as _run

    nc = _bacc.Bacc("TRN2", target_bir_lowering=False, num_devices=1)
    arrays, args = {}, []
    given = [(n, inputs[n]) for n in _INS] + list(shape_constants().items())
    for name, a in given:
        a = np.ascontiguousarray(a)
        arrays[f"in_{name}_dram"] = a
        args.append(nc.dram_tensor(f"in_{name}_dram", a.shape, mybir.dt.from_np(a.dtype), kind="ExternalInput").ap())
    args.append(nc.dram_tensor("out_0_dram", (BATCH, SEQ, DIM), F32, kind="ExternalOutput").ap())
    build(nc, *args)
    r = _run(nc, [arrays], core_ids=[0])
    return r.results[0]["out_0_dram"]
```
